# Optimizing a Trainium2 kernel written in Bass

```python
import numpy as np
import jax
import jax.numpy as jnp

def _softmax(x, axis=-1):
    return jax.nn.softmax(x, axis=axis)

def _gelu(x):
    return jax.nn.gelu(x, approximate=True)

def _silu(x):
    return jax.nn.silu(x)

def _sigmoid(x):
    return jax.nn.sigmoid(x)

def _layernorm(x, axis=-1, eps=1e-05):
    m = jnp.mean(x, axis=axis, keepdims=True)
    v = jnp.var(x, axis=axis, keepdims=True)
    return (x - m) / jnp.sqrt(v + eps)

def _scatter_add(tgt, idx, src, axis=0):
    return tgt.at[idx].add(src)

def _segment_sum(src, seg, n):
    return jax.ops.segment_sum(src, seg, n)
kernel_name = 'mk_decoder_preln_d1_seqx_r4_3c2e36'

def setup_inputs(seed: int=0):
    np.random.seed(seed)
    _w = jnp.asarray

    def _rec_inputs():
        import jax
        import jax.numpy as jnp
        _rk = jax.random.key(seed)
        x = -0.0005207 + 1.001 * jax.random.normal(jax.random.fold_in(_rk, 1), (8, 256, 512), jnp.float32)
        _lenS = 256 - jax.random.randint(jax.random.fold_in(_rk, 7), (8,), 0, max(1, 256 // 4) + 1, jnp.int32)
        _lenS2 = 256 - jax.random.randint(jax.random.fold_in(_rk, 8), (8,), 0, max(1, 256 // 4) + 1, jnp.int32)
        _ctx_2048P = jax.random.normal(jax.random.fold_in(_rk, 12), (8, 16, 512), jnp.float32)
        _ctx_2048c = jax.random.dirichlet(jax.random.fold_in(_rk, 512), 0.3 * jnp.ones((16,), jnp.float32), (8, 256))
        _ctx_2048t = jnp.einsum('bsk,bkd->bsd', _ctx_2048c, _ctx_2048P)
        _ctx_2048t = _ctx_2048t * jax.lax.rsqrt(jnp.mean(jnp.square(_ctx_2048t)) + 1e-12) * 0.953939
        ctx_2048 = -5.72187e-05 + 0.999849 * (_ctx_2048t + 0.3 * jax.random.normal(jax.random.fold_in(_rk, 612), (8, 256, 512), jnp.float32))
        _validS = jnp.arange(256)[None, :] < _lenS[:, None]
        _validS2 = jnp.arange(256)[None, :] < _lenS2[:, None]
        _causal = jnp.tril(jnp.ones((256, 256), dtype=bool))
        mask_BxSx4224_bf0 = jnp.logical_not(jnp.ones((8, 256, 1056), dtype=bool))
        return (x, ctx_2048, mask_BxSx4224_bf0)
    x, ctx_2048, mask_BxSx4224_bf0 = _rec_inputs()

    def _L0_attn_setup():
        import jax, jax.numpy as jnp
        import numpy as np
        HIDDEN = 512
        HEADS = 16
        HEAD_DIM = HIDDEN // HEADS
        NEG = -10000000000.0
        key = jax.random.key(seed)
        k1, k2, k3 = jax.random.split(key, 3)
        x = jax.random.normal(k1, (2, 512, HIDDEN), dtype=jnp.float32)
        w_qkv = jax.random.normal(k2, (HIDDEN, 3 * HIDDEN), dtype=jnp.float32) / np.sqrt(HIDDEN)
        w_out = jax.random.normal(k3, (HIDDEN, HIDDEN), dtype=jnp.float32) / np.sqrt(HIDDEN)
        return {'x': x, 'w_qkv': w_qkv, 'w_out': w_out}
    _L0_attn_all = _L0_attn_setup()
    _L0_attn_in = {k: v for k, v in _L0_attn_all.items() if k in ('w_qkv', 'w_out')}
    del _L0_attn_all

    def _L0_xattn_setup():
        import jax, jax.numpy as jnp
        import numpy as np
        import math
        DIM = 512
        B, Q_LEN, KV_LEN = (8, 128, 1024)
        key = jax.random.key(seed)
        ks = jax.random.split(key, 8)
        x = jax.random.normal(ks[0], (B, Q_LEN, DIM), dtype=jnp.float32)
        mask = jnp.zeros((B, Q_LEN, KV_LEN + Q_LEN), dtype=bool)
        k_cache = jax.random.normal(ks[1], (B, KV_LEN, DIM), dtype=jnp.float32)
        v_cache = jax.random.normal(ks[2], (B, KV_LEN, DIM), dtype=jnp.float32)
        scale = 1.0 / math.sqrt(DIM)
        wq = jax.random.normal(ks[3], (DIM, DIM), dtype=jnp.float32) * scale
        wk = jax.random.normal(ks[4], (DIM, DIM), dtype=jnp.float32) * scale
        wv = jax.random.normal(ks[5], (DIM, DIM), dtype=jnp.float32) * scale
        wo = jax.random.normal(ks[6], (DIM, DIM), dtype=jnp.float32) * scale
        return {'x': x, 'mask': mask, 'k_cache': k_cache, 'v_cache': v_cache, 'wq': wq, 'wk': wk, 'wv': wv, 'wo': wo}
    _L0_xattn_all = _L0_xattn_setup()
    _L0_xattn_in = {k: v for k, v in _L0_xattn_all.items() if k in ('wq', 'wk', 'wv', 'wo')}
    del _L0_xattn_all

    def _L0_ffn_setup():
        import jax, jax.numpy as jnp
        import numpy as np
        B, S, H, E = (4, 512, 512, 8)
        key = jax.random.key(seed)
        k_x, k_wg, k_w, k_b = jax.random.split(key, 4)
        x = jax.random.normal(k_x, (B, S, H), dtype=jnp.float32)
        wg = jax.random.normal(k_wg, (H, E), dtype=jnp.float32) * (1.0 / np.sqrt(H))
        W = jax.random.normal(k_w, (E, H, H), dtype=jnp.float32) * (1.0 / np.sqrt(H))
        b = jax.random.normal(k_b, (E, H), dtype=jnp.float32) * 0.01
        return {'x': x, 'wg': wg, 'W': W, 'b': b}
    _L0_ffn_all = _L0_ffn_setup()
    _L0_ffn_in = {k: v for k, v in _L0_ffn_all.items() if k in ('wg', 'W', 'b')}
    del _L0_ffn_all
    return {'x': x, 'ctx_2048': ctx_2048, 'mask_BxSx4224_bf0': mask_BxSx4224_bf0, 'L0_attn_w_qkv': _L0_attn_in['w_qkv'], 'L0_attn_w_out': _L0_attn_in['w_out'], 'L0_xattn_wq': _L0_xattn_in['wq'], 'L0_xattn_wk': _L0_xattn_in['wk'], 'L0_xattn_wv': _L0_xattn_in['wv'], 'L0_xattn_wo': _L0_xattn_in['wo'], 'L0_ffn_wg': _L0_ffn_in['wg'], 'L0_ffn_W': _L0_ffn_in['W'], 'L0_ffn_b': _L0_ffn_in['b']}

def reference(x, ctx_2048, mask_BxSx4224_bf0, L0_attn_w_qkv, L0_attn_w_out, L0_xattn_wq, L0_xattn_wk, L0_xattn_wv, L0_xattn_wo, L0_ffn_wg, L0_ffn_W, L0_ffn_b):
    import jax
    import jax.numpy as jnp

    def _L0_attn_ref(x, w_qkv, w_out):
        import jax, jax.numpy as jnp
        import numpy as np
        HIDDEN = 512
        HEADS = 16
        HEAD_DIM = HIDDEN // HEADS
        NEG = -10000000000.0
        b, s, _ = x.shape
        qkv = x @ w_qkv
        qkv = qkv.reshape(b, s, 3, HEADS, HEAD_DIM)
        q, k, v = (qkv[:, :, 0], qkv[:, :, 1], qkv[:, :, 2])
        scale = jnp.sqrt(jnp.float32(HEAD_DIM)).astype(x.dtype)
        q = q / scale
        scores = jnp.einsum('bqhd,bkhd->bhqk', q, k)
        causal_mask = jnp.arange(s)[:, None] >= jnp.arange(s)[None, :]
        scores = jnp.where(causal_mask[None, None], scores, NEG)
        attn = jax.nn.softmax(scores, axis=-1)
        out = jnp.einsum('bhqk,bkhd->bqhd', attn, v).reshape(b, s, HIDDEN)
        return out @ w_out

    def _L0_xattn_ref(x, mask, k_cache, v_cache, wq, wk, wv, wo):
        import jax, jax.numpy as jnp
        import numpy as np
        import math
        DIM = 512
        B, Q_LEN, KV_LEN = (8, 128, 1024)
        q = jnp.einsum('bsd,ed->bse', x, wq)
        k_new = jnp.einsum('bsd,ed->bse', x, wk)
        v_new = jnp.einsum('bsd,ed->bse', x, wv)
        k = jnp.concatenate([k_cache, k_new], axis=1)
        v = jnp.concatenate([v_cache, v_new], axis=1)
        scale = 1.0 / math.sqrt(q.shape[-1])
        scores = jnp.einsum('bqd,bkd->bqk', q, k) * scale
        attn = jax.nn.softmax(scores, axis=-1)
        out = jnp.einsum('bqk,bkd->bqd', attn, v)
        return jnp.einsum('bqd,ed->bqe', out, wo)

    def _L0_ffn_ref(x, wg, W, b):
        import jax, jax.numpy as jnp
        import numpy as np
        B, S, H, E = (4, 512, 512, 8)
        Bv, Sv, Hv = x.shape
        Ev = W.shape[0]
        xt = x.reshape(-1, Hv)
        logits = xt @ wg
        probs = jax.nn.softmax(logits, axis=-1)
        idx = jnp.argmax(probs, axis=-1)
        gate = jnp.take_along_axis(probs, idx[:, None], axis=1)
        onehot = jax.nn.one_hot(idx, Ev, dtype=x.dtype)
        expert_out = jnp.einsum('nh,eoh->neo', xt, W) + b[None, :, :]
        combine = onehot * gate
        out = jnp.einsum('ne,neo->no', combine, expert_out)
        return out.reshape(Bv, Sv, Hv)
    x = x + _L0_attn_ref(_layernorm(x, axis=-1), L0_attn_w_qkv, L0_attn_w_out)
    x = x + _L0_xattn_ref(_layernorm(x, axis=-1), mask_BxSx4224_bf0, ctx_2048, ctx_2048, L0_xattn_wq, L0_xattn_wk, L0_xattn_wv, L0_xattn_wo)
    x = x + _L0_ffn_ref(_layernorm(x, axis=-1), L0_ffn_wg, L0_ffn_W, L0_ffn_b)
    return x

_drawn_inputs = setup_inputs


def setup_inputs(seed=0):
    import zlib

    import numpy as np

    out = dict(_drawn_inputs(seed))
    spreads = {}
    factors = {'L0_ffn_b': 8.0}
    for name, (base, spread) in spreads.items():
        noise = np.random.default_rng([zlib.crc32(name.encode()), seed]).standard_normal(out[name].shape)
        drawn = base * np.exp(spread * noise) if base else spread * noise
        out[name] = jnp.asarray(drawn.astype(out[name].dtype))
    for name, factor in factors.items():
        out[name] = (out[name] * factor).astype(out[name].dtype)
    return out
```

```python
from contextlib import ExitStack

import concourse.bass as bass
from concourse import mybir

F32 = mybir.dt.float32
F32R = mybir.dt.float32r
BF16 = mybir.dt.bfloat16
I32 = mybir.dt.int32
U32 = mybir.dt.uint32
ALU = mybir.AluOpType
ACT = mybir.ActivationFunctionType
AX = mybir.AxisListType

P = 128
B, S, D = 8, 256, 512
DC = D // P
TB = S // P
NT = B * TB
H, HD = 16, 32
HG = P // HD
G = H // HG
E = 8
EPS = 1e-5
NEG = -1e10
BIG = 3e38


def free_ap(ap, offset, dims):
    return bass.AP(tensor=ap.tensor, offset=ap.offset + offset, ap=[list(ap.ap[0])] + dims)


def wait(engine, semaphore, value):
    if not isinstance(value, int) or value > 0:
        engine.wait_ge(semaphore, value)


def batch_rows(tensor, b):
    rows = tensor[b * S:(b + 1) * S, :] if isinstance(b, int) else tensor[bass.ds(b * S, S), :]
    return rows.rearrange("(t p) n -> p t n", p=P)


def three_pass(pe_matmul, out, lhs, rhs, first=True, last=True):
    (lh, ll), (rh, rl) = lhs, rhs
    steps = [(a, b) for a, b in zip(lh, rh)] + [(a, b) for a, b in zip(lh, rl)] + [(a, b) for a, b in zip(ll, rh)]
    for i, (a, b) in enumerate(steps):
        ins = pe_matmul(out, a, b, start=first and i == 0, stop=last and i == len(steps) - 1)
    return ins



def self_attention(nc, ident, x, w_qkv, w_out, x1):
    scale = float(HD) ** -0.5
    GH = G // 2
    HALF_IN = 16 * 3 * HG
    NPROB, NPT = 4, 4
    STRIP = 352
    V_AT = {0: 0, 3: 128, 1: 192, 2: 288}
    with ExitStack() as cx:
        sb = lambda n, s, d=F32: cx.enter_context(nc.sbuf_tensor(n, s, d))
        ps = lambda n, s: cx.enter_context(nc.psum_tensor(n, s, F32))
        sem = lambda n: cx.enter_context(nc.semaphore(n))
        w_hi, w_lo = sb("wqkv_hi", [P, DC, 3 * D], F32R), sb("wqkv_lo", [P, DC, 3 * D], F32R)
        wo_hi, wo_lo = sb("wout_hi", [P, DC, D], F32R), sb("wout_lo", [P, DC, D], F32R)
        xin, xr = sb("a_xin", [P, TB, D]), sb("a_xr", [P, TB, D])
        stats, mv = sb("a_stats", [P, TB, 6]), sb("a_mv", [P, TB, 2])
        veps, rstd, expo = sb("a_veps", [P, TB]), sb("a_rstd", [P, TB]), sb("a_expo", [P, TB])
        xn = sb("a_xn", [P, TB, D])
        xt_hi, xt_lo = sb("a_xt_hi", [P, DC, S], F32R), sb("a_xt_lo", [P, DC, S], F32R)
        qk = sb("qk", [P, 2, 4, GH, S], F32R)
        v_hi, v_lo = sb("v_hi", [P, TB, G * STRIP], F32R), sb("v_lo", [P, TB, G * STRIP], F32R)
        mask = sb("mask", [P, 2 * P])
        nmax = sb("nmax", [P, H, TB])
        prob = sb("prob", [P, NPROB, 3 * P])
        rsum, rinv8 = sb("rsum", [P, G, TB, HG]), sb("rinv8", [P, G, TB, HG])
        rinv = sb("rinv", [P, TB, HG, HD])
        r_sb = o_sb = rinv[:].rearrange("p q j d -> p (q j d)")
        pt_hi, pt_lo = sb("pt_hi", [P, NPT, 4 * P], F32R), sb("pt_lo", [P, NPT, 4 * P], F32R)
        ot_hi, ot_lo = sb("ot_hi", [P, G, S], F32R), sb("ot_lo", [P, G, S], F32R)
        with ExitStack() as early:
            raw = early.enter_context(nc.sbuf_tensor("a_raw", [P, DC * 3 * D], F32))
        stack = sb("stack", [3 * HD, 2, HG, 2, GH, S], F32R)
        job_ps = [ps(f"a_job{i}", [P, D]) for i in range(2)]
        s_ps = [ps(f"a_s{i}", [P, TB, S]) for i in range(2)]
        t_ps = [ps(f"a_t{i}", [P, 4 * P]) for i in range(2)]
        o_ps = [ps(f"a_o{i}", [P, 2, S]) for i in range(2)]

        wqkv_in, wout_in, x_in, xr_in, x1_out = (sem(f"a_{n}") for n in ("wqkv_in", "wout_in", "x_in", "xr_in", "x1_out"))
        consts, tick, tick_sp = sem("a_consts"), sem("a_tick"), sem("a_tick_sp")
        w_split_hi, w_split = sem("w_split_hi"), sem("w_split")
        ln_dve, ln_rstd, xn_ready = sem("a_ln_dve"), sem("a_ln_rstd"), sem("a_xn_ready")
        job_done, job_hi, job_ev = sem("a_job_done"), sem("a_job_hi"), sem("a_job_ev")
        stacked = [sem("stacked_0"), sem("stacked_1")]
        s_done, mx_done, ex_done = sem("s_done"), sem("mx_done"), sem("ex_done")
        rinv8_done, rinv_done, t_done = sem("rinv8_done"), sem("rinv_done"), sem("t_done")
        pt_hi_done, pt_done = sem("pt_hi_done"), sem("pt_done")
        av_done, r_done, rs_done = sem("av_done"), sem("r_done"), sem("rs_done")
        on_done, ot_hi_done, ot_done = sem("on_done"), sem("ot_hi_done"), sem("ot_done")

        SLOTS = {0: ["q3"], 1: ["k3"], 4: ["w0"], 5: ["w1", "X0"], 6: ["X1"], 7: ["y0", "q0"], 8: ["y1", "k0"],
                 9: ["q1"], 10: ["k1"], 12: ["u0"], 13: ["u1"], 14: ["q2"], 15: ["k2"]}
        OWN, LATE = ("q3", "k3", "w0", "w1"), ("y0", "y1")
        ORDER = [j for s in sorted(SLOTS) for j in SLOTS[s]]
        PROLOGUE = [j for j in ORDER if j not in OWN + LATE]
        JOBS, HI_JOBS = len(ORDER), len(ORDER) - len(LATE)
        assert JOBS % 2 == 0 and len(PROLOGUE) % 2 == 0
        T_LAG, LO_LAG, RINV_LAG, AV_LAG, R_LAG, ON_LAG, OT_LAG = 2, 3, 3, 4, 5, 6, 7
        LO_JOB_LAG = 1
        EPILOGUE_SLOTS = 10

        def has(j, n):
            if not isinstance(n, int):
                return True
            return n >= 1 if j in LATE else n < B if j in OWN else n < B - 1

        def number(j, n):
            return [i for i in ORDER if has(i, n)].index(j)

        def job_at(j, n):
            if not isinstance(n, int):
                return len(PROLOGUE) - len(LATE) + n * JOBS + number(j, n)
            if n < 0:
                return PROLOGUE.index(j)
            return len(PROLOGUE) + sum(has(i, m) for m in range(n) for i in ORDER) + number(j, n)

        def hi_at(j, n):
            if isinstance(n, int) and n < 0:
                return PROLOGUE.index(j)
            order = [i for i in ORDER if has(i, n) and i not in LATE]
            return len(PROLOGUE) + n * HI_JOBS + order.index(j)

        def bank(j, n):
            return job_ps[(PROLOGUE.index(j) if isinstance(n, int) and n < 0 else number(j, n)) % 2]

        def jobs_of(slot, n):
            return [j for j in SLOTS.get(slot, []) if has(j, n)]

        def head_at(slot, lag, n):
            t = slot - lag
            if isinstance(n, int) and (n < 1 if t < 0 else n >= B):
                return None
            return t % H if t < H else None

        def group_at(slot, lag, n):
            a = head_at(slot, lag, n)
            return a // HG if a is not None and a % HG == HG - 1 else None

        def groups_before(slot, lag, n):
            return n * G + (slot - lag) // HG

        def pe_job(j, n, tensor=nc.tensor):
            b, i = bank(j, n), int(j[1])
            toks = slice(i * P, (i + 1) * P)
            chunks = range(DC)
            if j[0] == "X":
                for c in chunks:
                    m = tensor.transpose(b[:, c * P:(c + 1) * P], xn[:, i, c * P:(c + 1) * P], ident[:])
            elif j[0] in "uw":
                o = 2 * D + (0 if j[0] == "u" else D // 2)
                cols = slice(o, o + D // 2)
                m = three_pass(tensor.matmul, b[:, 0:D // 2],
                               ([xt_hi[:, c, toks] for c in chunks], [xt_lo[:, c, toks] for c in chunks]),
                               ([w_hi[:, c, cols] for c in chunks], [w_lo[:, c, cols] for c in chunks]))
            elif j[0] == "y":
                m = three_pass(tensor.matmul, b[:, :],
                               ([ot_hi[:, c, toks] for c in chunks], [ot_lo[:, c, toks] for c in chunks]),
                               ([wo_hi[:, c, :] for c in chunks], [wo_lo[:, c, :] for c in chunks]))
            else:
                o = (0 if j[0] == "q" else D) + i * P
                m = three_pass(tensor.matmul, b[:, 0:S],
                               ([w_hi[:, c, o:o + P] for c in chunks], [w_lo[:, c, o:o + P] for c in chunks]),
                               ([xt_hi[:, c, :] for c in chunks], [xt_lo[:, c, :] for c in chunks]))
            m.then_inc(job_done, 1)

        def parts_of(j, n):
            b, i = bank(j, n), int(j[1])
            if j[0] == "X":
                cols = slice(i * P, (i + 1) * P)
                return [(xt_hi[:, :, cols], xt_lo[:, :, cols], b[:, :].rearrange("p (c n) -> p c n", c=DC))]
            if j[0] in "uw":
                first = 0 if j[0] == "u" else GH * STRIP
                out = []
                for a, z in ((0, 3), (1, 2)):
                    dst = [[STRIP, GH], [V_AT[z] - V_AT[a], 2], [1, HD]]
                    out.append((free_ap(v_hi[:, i, :], first + V_AT[a], dst), free_ap(v_lo[:, i, :], first + V_AT[a], dst),
                                free_ap(b[:, :], a * HD, [[P, GH], [(z - a) * HD, 2], [1, HD]])))
                return out
            w = 0 if j[0] == "q" else 2
            at = lambda part: qk[:, i // GH, w + part, i % GH, :]
            return [(at(0), at(1), b[:, 0:S])]

        block = cx.enter_context(nc.Block())

        @block.sync
        def _(sp):
            wv = w_qkv.rearrange("(c p) n -> c p n", p=P)
            for c in range(DC):
                sp.dma_start(raw[:, c * 3 * D:(c + 1) * 3 * D], wv[c]).then_inc(wqkv_in, 16)
            sp.wait_ge(w_split, DC)
            sp.dma_start(raw[:, 0:DC * D].rearrange("p (c n) -> p c n", c=DC),
                         w_out.rearrange("(c p) n -> p c n", p=P)).then_inc(wout_in, 16)
            sp.wait_ge(w_split, DC + 1)

            def stack_half(half):
                for r, parts in enumerate((slice(0, 3, 2), slice(1, 3), slice(0, 4, 3))):
                    for j in range(HG):
                        dst = stack[HD * r:HD * (r + 1), half, j, :, :, :].bitcast(F32)
                        src = qk[HD * j:HD * (j + 1), half, parts, :, :].bitcast(F32)
                        sp.dma_start(dst.rearrange("p w g s -> p w (g s)"),
                                     src.rearrange("p w g s -> p w (g s)")).then_inc(stacked[half], 16)

            def batch(n):
                wait(sp, job_ev, job_at("k3", n) + 1)
                sp.sem_inc(tick_sp, 1)
                wait(sp, s_done, n * H)
                stack_half(1)
                if has("k1", n):
                    wait(sp, job_ev, job_at("k1", n) + 1)
                    sp.sem_inc(tick_sp, 1)
                    wait(sp, s_done, n * H + H // 2)
                    stack_half(0)

            wait(sp, job_ev, job_at("k1", -1) + 1)
            stack_half(0)
            batch(0)
            with sp.Fori(1, B - 1) as n:
                batch(n)
            batch(B - 1)

        @block.gpsimd
        def _(pool):
            pool.dma_start(xin[:], batch_rows(x, 0)).then_inc(x_in, 16)
            pool.dma_start(xr[:], batch_rows(x, 0)).then_inc(xr_in, 16)
            nc.gpsimd.memset(ident[:], 0.0).then_inc(consts, 1)
            nc.gpsimd.memset(mask[:], 0.0).then_inc(consts, 1)
            nc.gpsimd.memset(expo[:], -0.5).then_inc(consts, 1)
            pool.wait_ge(consts, 3)
            nc.gpsimd.affine_select(out=ident[:], in_=ident[:], compare_op=ALU.not_equal, fill=1.0, base=0,
                                    pattern=[[-1, P]], channel_multiplier=1).then_inc(consts, 1)
            nc.gpsimd.affine_select(out=mask[:, P:], in_=mask[:, P:], compare_op=ALU.is_ge, fill=NEG, base=0,
                                    pattern=[[-1, P]], channel_multiplier=1).then_inc(consts, 1)

            def rstd_and_next(k, after):
                pool.wait_ge(ln_dve, k * 5 + 5)
                nc.gpsimd.tensor_tensor(rstd[:], veps[:], expo[:], ALU.pow).then_inc(ln_rstd, 1)
                if after:
                    pool.wait_ge(xn_ready, k * TB + TB)
                    pool.dma_start(xin[:], batch_rows(x, k + 1)).then_inc(x_in, 16)

            def store(k, after):
                pool.wait_ge(job_ev, job_at("y1", k + 1) + 1)
                pool.dma_start(batch_rows(x1, k), xr[:]).then_inc(x1_out, 16)
                if after:
                    pool.wait_ge(x1_out, k * 16 + 16)
                    pool.dma_start(xr[:], batch_rows(x, k + 1)).then_inc(xr_in, 16)

            rstd_and_next(0, True)
            for t in (pt_hi, pt_lo):
                nc.gpsimd.memset(t[:, :, 0:P].bitcast(F32), 0.0).then_inc(consts, 1)
            for t in (v_hi, v_lo):
                nc.gpsimd.memset(t[:].bitcast(F32), 0.0).then_inc(consts, 1)
            rstd_and_next(1, True)
            with pool.Fori(1, B - 2) as n:
                rstd_and_next(n + 1, True)
                store(n - 1, True)
            rstd_and_next(B - 1, False)
            store(B - 3, True)
            store(B - 2, True)
            store(B - 1, False)
            pool.wait_ge(x1_out, 16 * B)

        CONSTS = 9

        @block.scalar
        def _(act):
            def evac(j, n):
                act.wait_ge(job_done, job_at(j, n) + 1)
                if j == "q0":
                    wait(act, stacked[0], (n + 1) * HALF_IN)
                if j == "q2":
                    wait(act, stacked[1], (n + 1) * HALF_IN)
                if j == "u0":
                    wait(act, av_done, n * H + H // 2 if not isinstance(n, int) or n >= 0 else 0)
                if j == "w0":
                    wait(act, av_done, n * H)
                pieces = parts_of(j, n)
                for i, (hi, _, src) in enumerate(pieces):
                    e = nc.scalar.copy(hi, src)
                e.then_inc(job_hi, 1)

            for c in range(DC):
                act.wait_ge(wqkv_in, 16 * DC)
                nc.scalar.copy(w_hi[:, c, :], raw[:, c * 3 * D:(c + 1) * 3 * D]).then_inc(w_split_hi, 1)
            for j in PROLOGUE:
                if j == "q0":
                    act.wait_ge(wout_in, 16)
                    nc.scalar.copy(wo_hi[:].rearrange("p c n -> p (c n)"), raw[:, 0:DC * D]).then_inc(w_split_hi, 1)
                if j == "u0":
                    act.wait_ge(consts, CONSTS)
                evac(j, -1)

            def slot(n, h):
                e = head_at(h, 0, n)
                if e is not None:
                    g, j = divmod(e, HG)
                    act.wait_ge(mx_done, n * H + h + 1)
                    for q, cols in ((0, slice(0, P)), (1, slice(P, 3 * P))):
                        a = nc.scalar.activation(prob[:, e % NPROB, cols], prob[:, e % NPROB, cols], ACT.Exp, scale=-1.0,
                                                 bias=nmax[:, e, q:q + 1], accum_out=rsum[:, g, q, j:j + 1])
                    a.then_inc(ex_done, 1)
                for j in jobs_of(h, n):
                    if j not in LATE:
                        evac(j, n)
                t = head_at(h, T_LAG, n)
                if t is not None:
                    act.wait_ge(t_done, n * H + h - T_LAG + 1)
                    wait(act, av_done, n * H + h - T_LAG + 1 - NPT)
                    nc.scalar.copy(pt_hi[:, t % NPT, P:], t_ps[t % 2][:, P:]).then_inc(pt_hi_done, 1)
                g = group_at(h, R_LAG, n)
                if g is not None:
                    act.wait_ge(r_done, groups_before(h, R_LAG, n) + 1)
                    nc.scalar.copy(r_sb, o_ps[g % 2][:, 1, :]).then_inc(rs_done, 1)
                g = group_at(h, ON_LAG, n)
                if g is not None:
                    if g == 0 and not (isinstance(n, int) and n < 1):
                        act.wait_ge(job_done, job_at("y1", n) + 1)
                    act.wait_ge(on_done, groups_before(h, ON_LAG, n) + 1)
                    nc.scalar.copy(ot_hi[:, g, :], o_sb).then_inc(ot_hi_done, 1)

            for h in range(H):
                slot(0, h)
            with act.Fori(1, B - 1) as n:
                for h in range(H):
                    slot(n, h)
            for h in range(H):
                slot(B - 1, h)
            for h in range(EPILOGUE_SLOTS):
                slot(B, h)

        @block.tensor
        def _(pe):
            def job(j, n):
                if j == "X0":
                    pe.wait_ge(xn_ready, (n + 2) * TB)
                if j == "q0":
                    pe.wait_ge(job_ev, job_at("X1", n) + 1)
                if j == "y0":
                    pe.wait_ge(ot_done, n * G)
                wait(pe, job_ev, job_at(j, n) - 1)
                pe_job(j, n)

            pe.wait_ge(consts, 4)
            for j in PROLOGUE:
                if j == "q0":
                    pe.wait_ge(w_split, DC)
                job(j, -1)

            def slot(n, h):
                s = head_at(h, 0, n)
                if s is not None:
                    g, j = divmod(s, HG)
                    if s % (H // 2) == 0:
                        pe.wait_ge(stacked[g // GH], (n + 1) * HALF_IN)
                    wait(pe, mx_done, n * H + h - 1)
                    for q in range(TB):
                        m = nc.tensor.matmul(s_ps[s % 2][:, q, :], stack[:, g // GH, j, 0, g % GH, q * P:(q + 1) * P],
                                             stack[:, g // GH, j, 1, g % GH, :], start=True, stop=True)
                    m.then_inc(s_done, 1)
                for j in jobs_of(h, n):
                    job(j, n)
                t = head_at(h, T_LAG, n)
                if t is not None:
                    pe.wait_ge(ex_done, n * H + h - T_LAG + 1)
                    wait(pe, pt_done, n * H + h - T_LAG - 1)
                    for o, cols in ((P, slice(2 * P, 3 * P)), (2 * P, slice(0, P)), (3 * P, slice(P, 2 * P))):
                        m = nc.tensor.transpose(t_ps[t % 2][:, o:o + P], prob[:, t % NPROB, cols], ident[:])
                    m.then_inc(t_done, 1)
                a = head_at(h, AV_LAG, n)
                if a is not None:
                    g, j = divmod(a, HG)
                    of = n if h >= AV_LAG else n - 1
                    if a == 0:
                        pe.wait_ge(job_ev, job_at("u1", of - 1) + 1)
                    if a == H // 2:
                        pe.wait_ge(job_ev, job_at("w1", of) + 1)
                    if j == 0:
                        wait(pe, on_done, groups_before(h, AV_LAG, n) - 1)
                    pe.wait_ge(pt_done, n * H + h - AV_LAG + 1)
                    at = g * STRIP + V_AT[j] - HD * j
                    keys = range(TB)
                    ranges = [slice(2 * P, 4 * P), slice(0, 2 * P)]
                    m = three_pass(nc.tensor.matmul, o_ps[g % 2][:, 0, :],
                                   ([v_hi[:, k, at:at + P] for k in keys], [v_lo[:, k, at:at + P] for k in keys]),
                                   ([pt_hi[:, a % NPT, r] for r in ranges], [pt_lo[:, a % NPT, r] for r in ranges]),
                                   j == 0, j == HG - 1)
                    m.then_inc(av_done, 1)
                    if j == HG - 1:
                        pe.wait_ge(rinv_done, groups_before(h, AV_LAG, n) + 1)
                        for q in range(TB):
                            m = nc.tensor.matmul(o_ps[g % 2][:, 1, q * P:(q + 1) * P],
                                                 rinv[:, q, :, :].rearrange("p j d -> p (j d)"), ident[:],
                                                 start=True, stop=True)
                        m.then_inc(r_done, 1)

            for h in range(H):
                slot(0, h)
            with pe.Fori(1, B - 1) as n:
                for h in range(H):
                    slot(n, h)
            for h in range(H):
                slot(B - 1, h)
            for h in range(EPILOGUE_SLOTS):
                slot(B, h)

        @block.vector
        def _(dve):
            def norm_stats(k):
                dve.wait_ge(x_in, 16 * (k + 1))
                dve.sem_inc(tick, 1)
                for t in range(TB):
                    nc.vector.bn_stats(stats[:, t, :], xin[:, t, :]).then_inc(ln_dve, 1)
                for t in range(TB):
                    dve.wait_ge(ln_dve, k * 5 + 1 + t)
                    dve.sem_inc(tick, 1)
                    nc.vector.bn_aggr(mv[:, t, :], stats[:, t, :]).then_inc(ln_dve, 1)
                dve.wait_ge(ln_dve, k * 5 + 4)
                nc.vector.tensor_scalar(veps[:], mv[:, :, 1], EPS, None, ALU.add).then_inc(ln_dve, 1)

            def norm_apply(k):
                dve.wait_ge(ln_rstd, k + 1)
                for t in range(TB):
                    nc.vector.tensor_scalar(xn[:, t, :], xin[:, t, :], mv[:, t, 0:1], rstd[:, t:t + 1],
                                            ALU.subtract, ALU.mult).then_inc(xn_ready, 1)

            def evac(j, n):
                dve.wait_ge(job_hi, hi_at(j, n) + 1)
                pieces = parts_of(j, n)
                for hi, lo, src in pieces:
                    m = nc.vector.tensor_tensor(lo, src, hi.bitcast(F32), ALU.subtract)
                m.then_inc(job_ev, 1)

            norm_stats(0)
            norm_apply(0)
            for c in range(DC):
                dve.wait_ge(w_split_hi, c + 1)
                nc.vector.tensor_tensor(w_lo[:, c, :], raw[:, c * 3 * D:(c + 1) * 3 * D], w_hi[:, c, :].bitcast(F32),
                                        ALU.subtract).then_inc(w_split, 1)
            for j in PROLOGUE:
                if j == "q0":
                    dve.wait_ge(w_split_hi, DC + 1)
                    nc.vector.tensor_tensor(wo_lo[:].rearrange("p c n -> p (c n)"), raw[:, 0:DC * D],
                                            wo_hi[:].bitcast(F32).rearrange("p c n -> p (c n)"),
                                            ALU.subtract).then_inc(w_split, 1)
                if j == "u0":
                    dve.wait_ge(consts, CONSTS)
                evac(j, -1)

            def slot(n, h):
                s = head_at(h, 0, n)
                if s is not None:
                    dve.wait_ge(s_done, n * H + h + 1)
                    wait(dve, t_done, n * H + h - NPROB + 1)
                    dve.sem_inc(tick, 1)
                    for q, cols in ((0, slice(0, P)), (1, slice(P, 3 * P))):
                        m = nc.vector.tensor_tensor_reduce(
                            out=prob[:, s % NPROB, cols], in0=s_ps[s % 2][:, q, 0:P * (q + 1)],
                            in1=mask[:, P * (1 - q):], scale=-scale, scalar=BIG, op0=ALU.add, op1=ALU.min,
                            accum_out=nmax[:, s, q:q + 1])
                    m.then_inc(mx_done, 1)
                before = h - LO_JOB_LAG
                for j in jobs_of(before, n) if before >= 0 else jobs_of(H + before, n - 1 if isinstance(n, int) else n):
                    of = n if before >= 0 else n - 1
                    if isinstance(of, int) and of < 0:
                        continue
                    if j in LATE:
                        dve.wait_ge(job_done, job_at(j, of) + 1)
                        dve.wait_ge(xr_in, 16 * of)
                        xt = xr[:, int(j[1]), :]
                        nc.vector.tensor_tensor(xt, bank(j, of)[:, :], xt, ALU.add).then_inc(job_ev, 1)
                    else:
                        evac(j, of)
                t = head_at(h, LO_LAG, n)
                if t is not None:
                    dve.wait_ge(pt_hi_done, n * H + h - LO_LAG + 1)
                    nc.vector.tensor_tensor(pt_lo[:, t % NPT, P:], t_ps[t % 2][:, P:],
                                            pt_hi[:, t % NPT, P:].bitcast(F32), ALU.subtract).then_inc(pt_done, 1)
                g = group_at(h, ON_LAG, n)
                if g is not None:
                    dve.wait_ge(rs_done, groups_before(h, ON_LAG, n) + 1)
                    nc.vector.tensor_tensor(o_sb, o_ps[g % 2][:, 0, :], r_sb, ALU.mult).then_inc(on_done, 1)
                g = group_at(h, OT_LAG, n)
                if g is not None:
                    dve.wait_ge(ot_hi_done, groups_before(h, OT_LAG, n) + 1)
                    nc.vector.tensor_tensor(ot_lo[:, g, :], o_sb, ot_hi[:, g, :].bitcast(F32),
                                            ALU.subtract).then_inc(ot_done, 1)
                g = group_at(h, RINV_LAG, n)
                if g is not None:
                    before = groups_before(h, RINV_LAG, n)
                    dve.wait_ge(ex_done, before * HG + HG)
                    nc.vector.reciprocal(rinv8[:, g, :, :], rsum[:, g, :, :]).then_inc(rinv8_done, 1)
                    dve.wait_ge(rinv8_done, before + 1)
                    wait(dve, ot_done, before)
                    nc.vector.tensor_copy(rinv[:], free_ap(rinv8[:, g, :, :], 0, [[HG, TB], [1, HG], [0, HD]]))\
                        .then_inc(rinv_done, 1)
                if head_at(h, 0, n) is not None and (not isinstance(n, int) or n < B - 1):
                    if h == 0:
                        norm_stats(n + 1)
                    if h == 2:
                        norm_apply(n + 1)

            for h in range(H):
                slot(0, h)
            with dve.Fori(1, B - 1) as n:
                for h in range(H):
                    slot(n, h)
            for h in range(H):
                slot(B - 1, h)
            for h in range(EPILOGUE_SLOTS):
                slot(B, h)


def cross_attention(nc, ident, logits, x1, ctx, wq, wk, wv, wo, wg, x2n):
    scale = float(D) ** -0.5
    RING = 7
    KEYS = 2 * S
    KC = KEYS // P
    with ExitStack() as cx:
        sb = lambda n, s, d=F32: cx.enter_context(nc.sbuf_tensor("b_" + n, s, d))
        sem = lambda n: cx.enter_context(nc.semaphore("b_" + n))
        raw = [sb(f"raw_{n}", [P, DC, D]) for n in "qkvo"]
        wt_hi = {n: sb(f"w{n}t_hi", [P, DC, D], F32R) for n in "qkvo"}
        wt_lo = {n: sb(f"w{n}t_lo", [P, DC, D], F32R) for n in "qkvo"}
        wg_sb = sb("wg", [P, DC, E])
        xin, xr, cin = sb("xin", [P, TB, D]), sb("xr", [P, TB, D]), sb("cin", [P, TB, D])
        xn, x2_sb, xn3_sb = sb("xn", [P, TB, D]), sb("x2_sb", [P, TB, D]), sb("xn3_sb", [P, TB, D])
        stats, mv, veps, rstd = sb("stats", [P, 2, TB, 6]), sb("mv", [P, 2, TB, 2]), sb("veps", [P, 2, TB]), sb("rstd", [P, 2, TB])
        expo = sb("expo", [P, TB])
        xt_hi, xt_lo = sb("xt_hi", [P, DC, S], F32R), sb("xt_lo", [P, DC, S], F32R)
        qt_hi, qt_lo = sb("qt_hi", [P, DC, S], F32R), sb("qt_lo", [P, DC, S], F32R)
        kt_hi, kt_lo = sb("kt_hi", [P, DC, KEYS], F32R), sb("kt_lo", [P, DC, KEYS], F32R)
        v_hi, v_lo = sb("v_hi", [P, KC, D], F32R), sb("v_lo", [P, KC, D], F32R)
        smax, nmax, rsum, rinv = sb("smax", [P, TB]), sb("nmax", [P, TB]), sb("rsum", [P, TB]), sb("rinv", [P, TB])
        prob = sb("prob", [P, TB, KEYS])
        pt_hi, pt_lo = sb("pt_hi", [P, KC, S], F32R), sb("pt_lo", [P, KC, S], F32R)
        ot_hi, ot_lo = sb("ot_hi", [P, DC, S], F32R), sb("ot_lo", [P, DC, S], F32R)
        xt3 = sb("xt3", [P, DC, S])
        ring = [cx.enter_context(nc.psum_tensor(f"b_bank{i}", [P, D], F32)) for i in range(RING)]

        w_in = [sem(f"w{n}_in") for n in "qkvo"]
        wg_in, x_in, xr_in, c_in, x2_out, xn3_out = (sem(n) for n in ("wg_in", "x_in", "xr_in", "c_in", "x2_out", "xn3_out"))
        consts, tick = sem("consts"), sem("tick")
        ln_dve, ln_rstd, xn_ready = sem("ln_dve"), sem("ln_rstd"), sem("xn_ready")
        ln3_dve, ln3_rstd, xn3_ready = sem("ln3_dve"), sem("ln3_rstd"), sem("xn3_ready")
        job_done, job_hi, job_ev = sem("job_done"), sem("job_hi"), sem("job_ev")
        c_hi, c_split = sem("c_hi"), sem("c_split")
        max_done, mx_done, ex_done, rinv_done = sem("max_done"), sem("mx_done"), sem("ex_done"), sem("rinv_done")

        ORDER = ("s0 s1 X0 X1 C0 C1 q0 q1 p0 p1 q2 q3 o0 o1 o2 o3 k0 y0 y1 k1 k2 k3 v0 Y0 Y1 v1 l0 l1").split()
        FRONT = "XCqkv"
        LAST = [j for j in ORDER if j[0] not in FRONT]
        PROLOGUE = ("wq0 wq1 wq2 wq3 X0 X1 C0 C1 q0 q1 wk0 wk1 q2 q3 wk2 wk3 k0 k1 wv0 wv1 k2 k3 wv2 wv3 v0 wo0 wo1 v1 wo2 wo3").split()
        ev_jobs = lambda js: [j for j in js if j[0] != "s"]
        hi_jobs = lambda js: [j for j in js if j[0] not in "syYl"]

        def order(n):
            return ORDER if not isinstance(n, int) or n < B - 1 else LAST

        def count(j, n, kind):
            if isinstance(n, int) and n < 0:
                return kind(PROLOGUE).index(j)
            return len(kind(PROLOGUE)) + n * len(kind(ORDER)) + kind(order(n)).index(j)

        done_at = lambda j, n: count(j, n, list) + 1
        ev_at = lambda j, n: count(j, n, ev_jobs) + 1
        hi_at = lambda j, n: count(j, n, hi_jobs) + 1

        def bank(j, n):
            if isinstance(n, int) and n < 0:
                return ring[PROLOGUE.index(j) % RING]
            return ring[(len(PROLOGUE) + order(n).index(j)) % RING]
        assert len(ORDER) % RING == 0

        def parts_of(j, n):
            b, i = bank(j, n), int(j[-1])
            toks = slice(i * P, (i + 1) * P)
            chunked = b[:, :].rearrange("p (c n) -> p c n", c=DC)
            return {"w": lambda: (wt_hi[j[1]][:, i, :], wt_lo[j[1]][:, i, :], b[:, :]),
                    "X": lambda: (xt_hi[:, :, toks], xt_lo[:, :, toks], chunked),
                    "C": lambda: (kt_hi[:, :, toks], kt_lo[:, :, toks], chunked),
                    "q": lambda: (qt_hi[:, i, :], qt_lo[:, i, :], b[:, 0:S]),
                    "k": lambda: (kt_hi[:, i, S:], kt_lo[:, i, S:], b[:, 0:S]),
                    "v": lambda: (v_hi[:, TB + i, :], v_lo[:, TB + i, :], b[:, :]),
                    "p": lambda: (pt_hi[:, 2 * i:2 * i + 2, :], pt_lo[:, 2 * i:2 * i + 2, :],
                                  b[:, :].rearrange("p (c n) -> p c n", c=2)),
                    "o": lambda: (ot_hi[:, i, :], ot_lo[:, i, :], b[:, 0:S])}[j[0]]()

        block = cx.enter_context(nc.Block())

        @block.sync
        def _(sp):
            chunks = lambda t: t.rearrange("(c p) n -> p c n", p=P)
            sp.dma_start(xin[:], batch_rows(x1, 0)).then_inc(x_in, 16)
            sp.dma_start(raw[0][:], chunks(wq)).then_inc(w_in[0], 16)
            sp.dma_start(cin[:], batch_rows(ctx, 0)).then_inc(c_in, 16)
            for r, w, s in zip(raw[1:], (wk, wv, wo), w_in[1:]):
                sp.dma_start(r[:], chunks(w)).then_inc(s, 16)
            sp.dma_start(xr[:], batch_rows(x1, 0)).then_inc(xr_in, 16)
            sp.dma_start(wg_sb[:], chunks(wg)).then_inc(wg_in, 16)
            sp.wait_ge(xn_ready, TB)
            sp.dma_start(xin[:], batch_rows(x1, 1)).then_inc(x_in, 16)
            sp.wait_ge(c_split, 1)
            sp.wait_ge(job_done, done_at("C1", -1))
            sp.dma_start(cin[:], batch_rows(ctx, 1)).then_inc(c_in, 16)

            def batch(n, more, load):
                if load:
                    sp.wait_ge(xn_ready, (n + 2) * TB)
                    sp.dma_start(xin[:], batch_rows(x1, n + 2)).then_inc(x_in, 16)
                    sp.wait_ge(c_split, n + 2)
                    sp.wait_ge(job_done, done_at("C1", n))
                    sp.dma_start(cin[:], batch_rows(ctx, n + 2)).then_inc(c_in, 16)
                sp.wait_ge(job_ev, ev_at("y1", n))
                sp.dma_start(batch_rows(x2n[:, 0:D], n), x2_sb[:]).then_inc(x2_out, 16)
                if more:
                    sp.dma_start(xr[:], batch_rows(x1, n + 1)).then_inc(xr_in, 16)
                sp.wait_ge(xn3_ready, (n + 1) * TB)
                sp.dma_start(batch_rows(x2n[:, D:], n), xn3_sb[:]).then_inc(xn3_out, 16)

            batch(0, True, True)
            with sp.Fori(1, B - 2) as n:
                batch(n, True, True)
            batch(B - 2, True, False)
            batch(B - 1, False, False)
            sp.wait_ge(x2_out, 16 * B)
            sp.wait_ge(xn3_out, 16 * B)

        @block.gpsimd
        def _(pool):
            nc.gpsimd.memset(expo[:], -0.5).then_inc(consts, 1)
            pool.wait_ge(consts, 1)

            def rstd_ln2(k):
                pool.wait_ge(ln_dve, k * 5 + 5)
                nc.gpsimd.tensor_tensor(rstd[:, 0, :], veps[:, 0, :], expo[:], ALU.pow).then_inc(ln_rstd, 1)

            def rstd_ln3(k):
                pool.wait_ge(ln3_dve, k * 5 + 5)
                nc.gpsimd.tensor_tensor(rstd[:, 1, :], veps[:, 1, :], expo[:], ALU.pow).then_inc(ln3_rstd, 1)

            rstd_ln2(0)
            rstd_ln2(1)
            with pool.Fori(0, B - 2) as n:
                rstd_ln3(n)
                rstd_ln2(n + 2)
            rstd_ln3(B - 2)
            rstd_ln3(B - 1)

        @block.scalar
        def _(act):
            def hi_part(j, n):
                act.wait_ge(job_done, done_at(j, n))
                hi, _, src = parts_of(j, n)
                nc.scalar.copy(hi, src).then_inc(job_hi, 1)

            def ctx_hi(k):
                act.wait_ge(c_in, 16 * (k + 1))
                nc.scalar.copy(v_hi[:, 0:TB, :], cin[:]).then_inc(c_hi, 1)

            for j in PROLOGUE:
                hi_part(j, -1)
                if j == "C1":
                    ctx_hi(0)

            def batch(n):
                for q in range(TB):
                    act.wait_ge(mx_done, n * TB + q + 1)
                    nc.scalar.activation(prob[:, q, :], bank(f"s{q}", n)[:, :], ACT.Exp, scale=scale,
                                         bias=nmax[:, q:q + 1], accum_out=rsum[:, q:q + 1]).then_inc(ex_done, 1)
                for j in hi_jobs(order(n)):
                    hi_part(j, n)
                    if j == "o3" and order(n) is ORDER:
                        ctx_hi(n + 1)

            batch(0)
            with act.Fori(1, B - 1) as n:
                batch(n)
            batch(B - 1)

        @block.tensor
        def _(pe):
            def wait_bank(j, n):
                if isinstance(n, int) and n < 0:
                    before, of = PROLOGUE.index(j) - RING, -1
                    if before < 0:
                        return
                    last = PROLOGUE[before]
                else:
                    before = order(n).index(j) - RING
                    if before >= 0:
                        last, of = order(n)[before], n
                    elif isinstance(n, int) and n == 0:
                        last, of = PROLOGUE[before], -1
                    else:
                        last, of = ORDER[before], n - 1
                if last[0] == "s":
                    pe.wait_ge(ex_done, of * TB + int(last[1]) + 1)
                else:
                    pe.wait_ge(job_ev, ev_at(last, of))

            def job(j, n):
                wait_bank(j, n)
                b, i = bank(j, n), int(j[-1])
                toks = slice(i * P, (i + 1) * P)
                rows = slice(i * P, (i + 1) * P)
                chunks = range(DC)
                if j[0] == "w":
                    if i == 0:
                        pe.wait_ge(w_in["qkvo".index(j[1])], 16)
                    for c in chunks:
                        m = nc.tensor.transpose(b[:, c * P:(c + 1) * P], raw["qkvo".index(j[1])][:, c, rows], ident[:])
                elif j[0] in "XCY":
                    if j == "X0":
                        pe.wait_ge(xn_ready, (n + 2) * TB)
                    if j == "C0":
                        pe.wait_ge(c_in, 16 * (n + 2))
                    if j[0] == "Y":
                        pe.wait_ge(xn3_ready, n * TB + i + 1)
                    src = {"X": xn, "C": cin, "Y": xn3_sb}[j[0]]
                    for c in chunks:
                        m = nc.tensor.transpose(b[:, c * P:(c + 1) * P], src[:, i, c * P:(c + 1) * P], ident[:])
                elif j[0] in "qk":
                    if j == "q0":
                        pe.wait_ge(job_ev, ev_at("X1", n))
                    if isinstance(n, int) and n < 0 and i == 0:
                        pe.wait_ge(job_ev, ev_at(f"w{j[0]}3", n))
                    m = three_pass(nc.tensor.matmul, b[:, 0:S],
                                   ([wt_hi[j[0]][:, c, rows] for c in chunks], [wt_lo[j[0]][:, c, rows] for c in chunks]),
                                   ([xt_hi[:, c, :] for c in chunks], [xt_lo[:, c, :] for c in chunks]))
                elif j[0] == "v":
                    if isinstance(n, int) and n < 0 and i == 0:
                        pe.wait_ge(job_ev, ev_at("wv3", n))
                    m = three_pass(nc.tensor.matmul, b[:, :],
                                   ([xt_hi[:, c, toks] for c in chunks], [xt_lo[:, c, toks] for c in chunks]),
                                   ([wt_hi["v"][:, c, :] for c in chunks], [wt_lo["v"][:, c, :] for c in chunks]))
                elif j[0] == "s":
                    if i == 0:
                        pe.wait_ge(job_ev, ev_at("k3", n - 1))
                    m = three_pass(nc.tensor.matmul, b[:, :],
                                   ([qt_hi[:, c, toks] for c in chunks], [qt_lo[:, c, toks] for c in chunks]),
                                   ([kt_hi[:, c, :] for c in chunks], [kt_lo[:, c, :] for c in chunks]))
                elif j[0] == "p":
                    pe.wait_ge(ex_done, (n + 1) * TB)
                    for k in range(2):
                        for q in range(TB):
                            m = nc.tensor.transpose(b[:, (k * TB + q) * P:(k * TB + q + 1) * P],
                                                    prob[:, q, (2 * i + k) * P:(2 * i + k + 1) * P], ident[:])
                elif j[0] == "o":
                    if i == 0:
                        pe.wait_ge(job_ev, ev_at("p1", n))
                        pe.wait_ge(c_split, n + 1)
                    keys = range(KC)
                    m = three_pass(nc.tensor.matmul, b[:, 0:S],
                                   ([v_hi[:, k, rows] for k in keys], [v_lo[:, k, rows] for k in keys]),
                                   ([pt_hi[:, k, :] for k in keys], [pt_lo[:, k, :] for k in keys]))
                elif j[0] == "y":
                    if i == 0:
                        pe.wait_ge(job_ev, ev_at("o3", n))
                    m = three_pass(nc.tensor.matmul, b[:, :],
                                   ([ot_hi[:, c, toks] for c in chunks], [ot_lo[:, c, toks] for c in chunks]),
                                   ([wt_hi["o"][:, c, :] for c in chunks], [wt_lo["o"][:, c, :] for c in chunks]))
                else:
                    if i == 0:
                        pe.wait_ge(job_ev, ev_at("Y1", n))
                    for c in chunks:
                        m = nc.tensor.matmul(b[:, 0:E], xt3[:, c, toks], wg_sb[:, c, :], start=c == 0, stop=c == DC - 1)
                m.then_inc(job_done, 1)

            for j in PROLOGUE:
                job(j, -1)
            pe.wait_ge(wg_in, 16)

            def batch(n):
                for j in order(n):
                    job(j, n)

            batch(0)
            with pe.Fori(1, B - 1) as n:
                batch(n)
            batch(B - 1)

        @block.vector
        def _(dve):
            def norm_stats(which, k, src, done):
                for t in range(TB):
                    nc.vector.bn_stats(stats[:, which, t, :], src[:, t, :]).then_inc(done, 1)
                for t in range(TB):
                    dve.wait_ge(done, k * 5 + 1 + t)
                    dve.sem_inc(tick, 1)
                    nc.vector.bn_aggr(mv[:, which, t, :], stats[:, which, t, :]).then_inc(done, 1)
                dve.wait_ge(done, k * 5 + 4)
                nc.vector.tensor_scalar(veps[:, which, :], mv[:, which, :, 1], EPS, None, ALU.add).then_inc(done, 1)

            def norm_apply(which, dst, src, ready):
                for t in range(TB):
                    nc.vector.tensor_scalar(dst[:, t, :], src[:, t, :], mv[:, which, t, 0:1], rstd[:, which, t:t + 1],
                                            ALU.subtract, ALU.mult).then_inc(ready, 1)

            def ln2_stats(k):
                dve.wait_ge(x_in, 16 * (k + 1))
                dve.sem_inc(tick, 1)
                norm_stats(0, k, xin, ln_dve)

            def ln2_apply(k):
                dve.wait_ge(ln_rstd, k + 1)
                norm_apply(0, xn, xin, xn_ready)

            def lo_part(j, n):
                dve.wait_ge(job_hi, hi_at(j, n))
                hi, lo, src = parts_of(j, n)
                nc.vector.tensor_tensor(lo, src, hi.bitcast(F32), ALU.subtract).then_inc(job_ev, 1)

            def ctx_lo(k):
                dve.wait_ge(c_hi, k + 1)
                nc.vector.tensor_tensor(v_lo[:, 0:TB, :], cin[:], v_hi[:, 0:TB, :].bitcast(F32),
                                        ALU.subtract).then_inc(c_split, 1)

            ln2_stats(0)
            ln2_apply(0)
            for j in PROLOGUE:
                lo_part(j, -1)
                if j == "C1":
                    ctx_lo(0)
            ln2_stats(1)
            ln2_apply(1)

            def batch(n):
                for q in range(TB):
                    dve.wait_ge(job_done, done_at(f"s{q}", n))
                    dve.sem_inc(tick, 1)
                    nc.vector.tensor_reduce(smax[:, q:q + 1], bank(f"s{q}", n)[:, :], AX.X, ALU.max).then_inc(max_done, 1)
                    dve.wait_ge(max_done, n * TB + q + 1)
                    nc.vector.tensor_scalar(nmax[:, q:q + 1], smax[:, q:q + 1], -scale, None, ALU.mult)\
                        .then_inc(mx_done, 1)
                for j in ev_jobs(order(n)):
                    if j[0] == "y":
                        i = int(j[1])
                        if i == 0:
                            dve.wait_ge(xr_in, 16 * (n + 1))
                            wait(dve, x2_out, 16 * n)
                            dve.wait_ge(rinv_done, n + 1)
                        dve.wait_ge(job_done, done_at(j, n))
                        nc.vector.scalar_tensor_tensor(x2_sb[:, i, :], bank(j, n)[:, :], rinv[:, i:i + 1], xr[:, i, :],
                                                       ALU.mult, ALU.add).then_inc(job_ev, 1)
                    elif j[0] == "Y":
                        dve.wait_ge(job_done, done_at(j, n))
                        nc.vector.tensor_copy(xt3[:, :, int(j[1]) * P:(int(j[1]) + 1) * P],
                                              bank(j, n)[:, :].rearrange("p (c n) -> p c n", c=DC)).then_inc(job_ev, 1)
                    elif j[0] == "l":
                        dve.wait_ge(job_done, done_at(j, n))
                        nc.vector.tensor_copy(logits[:, bass.ds(n * TB + int(j[1]), 1), :],
                                              bank(j, n)[:, 0:E].unsqueeze(1)).then_inc(job_ev, 1)
                    else:
                        lo_part(j, n)
                    if j == "o3" and order(n) is ORDER:
                        ctx_lo(n + 1)
                    if j == "p1":
                        nc.vector.reciprocal(rinv[:], rsum[:]).then_inc(rinv_done, 1)
                    if j == "y1":
                        dve.wait_ge(job_ev, ev_at("y1", n))
                        dve.sem_inc(tick, 1)
                        norm_stats(1, n, x2_sb, ln3_dve)
                    if j == ("k1" if order(n) is ORDER else "y1"):
                        wait(dve, xn3_out, 16 * n)
                        dve.wait_ge(ln3_rstd, n + 1)
                        norm_apply(1, xn3_sb, x2_sb, xn3_ready)
                    if j in ("k3", "v1") and (not isinstance(n, int) or n < B - 2):
                        (ln2_stats if j == "k3" else ln2_apply)(n + 2)

            batch(0)
            with dve.Fori(1, B - 2) as n:
                batch(n)
            batch(B - 2)
            batch(B - 1)


def mixture_of_experts(nc, ident, logits, x2n, w, bias, table, out):
    N = B * S
    BLOCKS = NT + E - 1
    AHEAD = 2
    BEHIND = 3
    RX = 4
    FIRST = BEHIND + RX
    RAWS = 3
    RING = 7
    W_JOBS = E * DC
    assert (BLOCKS - FIRST) % RX == 0
    TABLE_PARTS = [(0, 4), (4, 12), (12, BLOCKS)]
    with ExitStack() as cx:
        sb = lambda n, s, d=F32: cx.enter_context(nc.sbuf_tensor("c_" + n, s, d))
        sem = lambda n: cx.enter_context(nc.semaphore("c_" + n))
        wt_hi, wt_lo = sb("wt_hi", [P, DC, E * D], F32R), sb("wt_lo", [P, DC, E * D], F32R)
        raw = [sb(f"raw{i}", [P, DC, D]) for i in range(RAWS)]
        bias_sb = sb("bias", [P, E * D])
        rows = sb("rows", [P, RX, 2 * D])
        xt_hi, xt_lo = sb("xt_hi", [P, 2, D], F32R), sb("xt_lo", [P, 2, D], F32R)
        y_sb = sb("y_sb", [P, 2, D])
        lmax, diff, eq = sb("lmax", [P, NT]), sb("diff", [P, NT, E]), sb("eq", [P, NT, E])
        ex, gsum = sb("ex", [P, NT, E]), sb("gsum", [P, NT])
        rank_i, rank = sb("rank_i", [P, E], I32), sb("rank", [P, E])
        best, onehot = sb("best", [P, NT]), sb("onehot", [P, NT, E], BF16)
        before, ones = sb("before", [P, P], BF16), sb("ones", [P, P], BF16)
        full_i, full = sb("full_i", [P, NT], I32), sb("full", [P, NT])
        upto = sb("upto", [P, E, E])
        block_i, block_no = sb("block_i", [P, BLOCKS], I32), sb("block_no", [P, BLOCKS])
        number = sb("number", [P, E])
        over, blocks = sb("over", [P, E, NT]), sb("blocks", [P, E])
        cum, end, start = sb("cum", [P, E, E]), sb("end", [P, E]), sb("start", [P, E])
        past, owner, owner_i = sb("past", [P, BLOCKS, E]), sb("owner", [P, BLOCKS]), sb("owner_i", [P, BLOCKS], I32)
        place, slot, slot_i = sb("place", [P, NT, E]), sb("slot", [P, NT]), sb("slot_i", [P, NT], U32)
        entry = sb("entry", [P, NT, 2], I32)
        unused = sb("unused", [P, BLOCKS, 2], I32)
        tab = sb("tab", [P, BLOCKS + AHEAD, 2], I32)
        gather_no, scatter_no = sb("gather_no", [P, RX, 1], U32), sb("scatter_no", [P, RX, 1], U32)
        route_ps = cx.enter_context(nc.psum_tensor("c_route", [P, 2, NT * E], F32))
        ring = [cx.enter_context(nc.psum_tensor(f"c_bank{i}", [P, D], F32)) for i in range(RING)]
        t_ps, y_ps = ring[0:2], ring[2:4]

        bias_in, init_in, entries_in = sem("bias_in"), sem("init_in"), sem("entries_in")
        w_in = [sem(f"w_in{i}") for i in range(RAWS)]
        rows_in, out_done = [sem(f"rows_in{i}") for i in range(RX)], [sem(f"out_done{i}") for i in range(RX)]
        tab_in = [sem(f"tab_in{i}") for i in range(len(TABLE_PARTS))]
        consts, route, diff_done, ex_done = sem("consts"), sem("route"), sem("diff_done"), sem("ex_done")
        onehot_done, ranks_done, entry_done, slot_done = sem("onehot_done"), sem("ranks_done"), sem("entry_done"), sem("slot_done")
        owner_done, tick_act, tick_pool = sem("owner_done"), sem("tick_act"), sem("tick_pool")
        w_done, w_hi_done, w_split = sem("w_done"), sem("w_hi_done"), sem("w_split")
        gather_no_done, scatter_no_done = sem("gather_no_done"), sem("scatter_no_done")
        t_done, xt_hi_done, xt_done = sem("t_done"), sem("xt_hi_done"), sem("xt_done")
        y_done, bias_done, fin_done = sem("y_done"), sem("bias_done"), sem("fin_done")
        block = cx.enter_context(nc.Block())
        CONSTS_INIT, CONSTS = 8, 13

        def blocks_loop(engine, step):
            for k in range(FIRST):
                step(0, k)
            with engine.Fori(0, (BLOCKS - FIRST) // RX) as i:
                for k in range(FIRST, FIRST + RX):
                    step(i, k)

        def number_of(i, k):
            return i * RX + k

        def turn(i, k):
            return i + k // RX

        def column(t, i, k, c):
            return t[:, k, c:c + 1] if isinstance(i, int) else t[:, bass.ds(i * RX + k, 1), c]

        @block.sync
        def _(sp):
            for e in range(E):
                if e >= RAWS:
                    sp.wait_ge(w_split, (e - RAWS + 1) * DC)
                sp.dma_start(raw[e % RAWS][:], w[e].rearrange("(c p) h -> p c h", p=P)).then_inc(w_in[e % RAWS], 16)
                if e == 0:
                    sp.wait_ge(consts, CONSTS_INIT)
                    sp.dma_start(table.rearrange("(j p) c -> p j c", p=P), unused[:]).then_inc(init_in, 16)
                if e == 1:
                    sp.dma_start(bias_sb[:], bass.AP(tensor=bias.tensor, offset=bias.offset, ap=[[0, P], [1, E * D]]))\
                        .then_inc(bias_in, 16)
            sp.wait_ge(entries_in, 16 * NT)
            rows_of = table.rearrange("(j p) c -> p j c", p=P)
            for (a, b), s in zip(TABLE_PARTS, tab_in):
                sp.dma_start(tab[:, a:b, :], rows_of[:, a:b, :]).then_inc(s, 16)

        @block.gpsimd
        def _(pool):
            nc.gpsimd.memset(unused[:], 0).then_inc(consts, 1)
            pool.wait_ge(consts, 1)
            nc.gpsimd.iota(unused[:, :, 0], pattern=[[P, BLOCKS]], base=N, channel_multiplier=1).then_inc(consts, 1)
            nc.gpsimd.iota(rank_i[:], pattern=[[-1, E]], base=E, channel_multiplier=0).then_inc(consts, 1)
            nc.gpsimd.memset(before[:], 1.0).then_inc(consts, 1)
            nc.gpsimd.memset(ones[:], 1.0).then_inc(consts, 1)
            nc.gpsimd.memset(upto[:], 1.0).then_inc(consts, 1)
            nc.gpsimd.memset(tab[:, BLOCKS:, :], 0).then_inc(consts, 1)
            pool.wait_ge(consts, 7)
            nc.gpsimd.tensor_copy(rank[:], rank_i[:]).then_inc(consts, 1)
            nc.gpsimd.affine_select(out=before[:], in_=before[:], compare_op=ALU.is_gt, fill=0.0, base=0,
                                    pattern=[[1, P]], channel_multiplier=-1).then_inc(consts, 1)
            nc.gpsimd.affine_select(out=upto[:], in_=upto[:], compare_op=ALU.is_ge, fill=0.0, base=0,
                                    pattern=[[1, E], [-1, E]], channel_multiplier=0).then_inc(consts, 1)
            nc.gpsimd.iota(full_i[:], pattern=[[P, NT]], base=0, channel_multiplier=0).then_inc(consts, 1)
            nc.gpsimd.iota(block_i[:], pattern=[[1, BLOCKS]], base=0, channel_multiplier=0).then_inc(consts, 1)
            nc.gpsimd.iota(entry[:, :, 0], pattern=[[P, NT]], base=0, channel_multiplier=1).then_inc(consts, 1)
            nc.gpsimd.memset(rows[:], 0.0).then_inc(entry_done, 1)
            pool.wait_ge(entry_done, 2)
            pool.wait_ge(consts, CONSTS)
            pool.wait_ge(slot_done, 1)
            pool.wait_ge(init_in, 16)
            for t in range(NT):
                pool.indirect_dma_start(table, bass.IndirectOffsetOnAxis(ap=slot_i[:, t:t + 1], axis=0),
                                        entry[:, t, :], None).then_inc(entries_in, 16)

            def gather(i, k):
                m = number_of(i, k)
                pool.wait_ge(gather_no_done, m + 1)
                if k >= RX:
                    pool.wait_ge(fin_done, m - RX + 1)
                pool.sem_inc(tick_pool, 1)
                pool.indirect_dma_start(rows[:, k % RX, :], None, x2n,
                                        bass.IndirectOffsetOnAxis(ap=gather_no[:, k % RX, :], axis=0),
                                        bounds_check=N - 1, oob_is_err=False).then_inc(rows_in[k % RX], 16)

            def scatter(i, k):
                m = number_of(i, k)
                pool.wait_ge(fin_done, m + 1)
                pool.wait_ge(scatter_no_done, m + 1)
                pool.sem_inc(tick_pool, 1)
                pool.indirect_dma_start(out, bass.IndirectOffsetOnAxis(ap=scatter_no[:, k % RX, :], axis=0),
                                        y_sb[:, k % 2, :], None, bounds_check=N - 1, oob_is_err=False)\
                    .then_inc(out_done[k % RX], 16)

            def step(i, k):
                gather(i, k)
                if k >= BEHIND:
                    scatter(i, k - BEHIND)

            blocks_loop(pool, step)
            for m in range(BLOCKS - BEHIND, BLOCKS):
                scatter(0, m)
            for k in range(BLOCKS - RX, BLOCKS):
                pool.wait_ge(out_done[k % RX], 16 * (turn(0, k) + 1))

        @block.scalar
        def _(act):
            act.wait_ge(diff_done, 1)
            nc.scalar.activation(ex[:], diff[:], ACT.Exp).then_inc(ex_done, 1)
            for e in range(E):
                for c in range(DC):
                    i = e * DC + c
                    act.wait_ge(w_done, i + 1)
                    nc.scalar.copy(wt_hi[:, c, e * D:(e + 1) * D], ring[i % RING][:, :]).then_inc(w_hi_done, 1)

            def gather_numbers(i, k):
                m = number_of(i, k)
                nc.scalar.copy(gather_no[:, k % RX, :], column(tab, i, k, 0)).then_inc(gather_no_done, 1)

            def scatter_numbers(i, k):
                m = number_of(i, k)
                if k >= RX:
                    act.wait_ge(out_done[k % RX], 16 * turn(i, k))
                    act.sem_inc(tick_act, 1)
                nc.scalar.copy(scatter_no[:, k % RX, :], column(tab, i, k, 0)).then_inc(scatter_no_done, 1)

            for s in tab_in:
                act.wait_ge(s, 16)
            act.wait_ge(consts, CONSTS)
            for m in range(AHEAD):
                gather_numbers(0, m)

            def step(i, k):
                m = number_of(i, k)
                act.wait_ge(t_done, m + 1)
                nc.scalar.copy(xt_hi[:, k % 2, :], t_ps[k % 2][:, :]).then_inc(xt_hi_done, 1)
                gather_numbers(i, k + AHEAD)
                if k >= 1:
                    scatter_numbers(i, k - 1)

            blocks_loop(act, step)
            scatter_numbers(0, BLOCKS - 1)

        @block.tensor
        def _(pe):
            def w_job(i):
                e, c = divmod(i, DC)
                if c == 0:
                    pe.wait_ge(w_in[e % RAWS], 16 * (e // RAWS + 1))
                if i >= RING:
                    pe.wait_ge(w_split, i - RING + 1)
                for o in range(DC):
                    m = nc.tensor.transpose(ring[i % RING][:, o * P:(o + 1) * P],
                                            raw[e % RAWS][:, o, c * P:(c + 1) * P], ident[:])
                m.then_inc(w_done, 1)

            for i in range(DC):
                w_job(i)
            pe.wait_ge(consts, CONSTS)
            pe.wait_ge(onehot_done, 1)
            flat = onehot[:].rearrange("p t e -> p (t e)")
            nc.tensor.matmul(route_ps[:, 0, :], before[:], flat, start=True, stop=False)
            for t in range(NT - 1):
                nc.tensor.matmul(route_ps[:, 0, (t + 1) * E:], ones[:],
                                 free_ap(onehot[:], t * E, [[0, NT - 1 - t], [1, E]]), start=False, stop=t == NT - 2)
            nc.tensor.matmul(route_ps[:, 1, :], ones[:], flat, start=True, stop=True).then_inc(ranks_done, 1)
            for i in range(DC, W_JOBS):
                w_job(i)
            pe.wait_ge(owner_done, 1)
            pe.wait_ge(w_split, W_JOBS)

            def transposes(i, k):
                m = number_of(i, k)
                pe.wait_ge(rows_in[k % RX], (turn(i, k) + 1) * 16)
                if k >= 2:
                    pe.wait_ge(xt_done, m - 1)
                for c in range(DC):
                    t = nc.tensor.transpose(t_ps[k % 2][:, c * P:(c + 1) * P],
                                            rows[:, k % RX, D + c * P:D + (c + 1) * P], ident[:])
                t.then_inc(t_done, 1)

            def product(i, k):
                m = number_of(i, k)
                e = pe.value_load(owner_i[0:1, bass.ds(m, 1)] if not isinstance(m, int) else owner_i[0:1, m:m + 1],
                                  min_val=0, max_val=E - 1)
                pe.wait_ge(xt_done, m + 1)
                if k >= 2:
                    pe.wait_ge(bias_done, m - 1)
                y = three_pass(nc.tensor.matmul, y_ps[k % 2][:, :],
                               ([xt_hi[:, k % 2, c * P:(c + 1) * P] for c in range(DC)],
                                [xt_lo[:, k % 2, c * P:(c + 1) * P] for c in range(DC)]),
                               ([wt_hi[:, c, bass.ds(e * D, D)] for c in range(DC)],
                                [wt_lo[:, c, bass.ds(e * D, D)] for c in range(DC)]))
                y.then_inc(y_done, 1)

            def step(i, k):
                transposes(i, k)
                if k >= 1:
                    product(i, k - 1)

            blocks_loop(pe, step)
            product(0, BLOCKS - 1)

        @block.vector
        def _(dve):
            over_e = lambda t: free_ap(t, 0, [[1, NT], [0, E]])
            over_t = lambda t: free_ap(t, 0, [[0, NT], [1, E]])
            steps = [0]

            def then(instruction):
                steps[0] += 1
                instruction.then_inc(route, 1)
                dve.wait_ge(route, steps[0])

            dve.wait_ge(consts, CONSTS)
            then(nc.vector.tensor_reduce(lmax[:], logits[:], AX.X, ALU.max))
            nc.vector.tensor_tensor(diff[:], logits[:], over_e(lmax[:]), ALU.subtract).then_inc(diff_done, 1)
            then(nc.vector.tensor_tensor(eq[:], logits[:], over_e(lmax[:]), ALU.is_equal))
            then(nc.vector.tensor_tensor(eq[:], eq[:], over_t(rank[:]), ALU.mult))
            then(nc.vector.tensor_reduce(best[:], eq[:], AX.X, ALU.max))
            nc.vector.tensor_tensor(onehot[:], eq[:], over_e(best[:]), ALU.is_equal).then_inc(onehot_done, 1)
            dve.wait_ge(ex_done, 1)
            then(nc.vector.tensor_reduce(gsum[:], ex[:], AX.X, ALU.add))
            nc.vector.reciprocal(entry[:, :, 1].bitcast(F32), gsum[:]).then_inc(entry_done, 1)
            nc.vector.tensor_copy(full[:], full_i[:]).then_inc(route, 1)
            then(nc.vector.tensor_copy(block_no[:], block_i[:]))
            steps[0] += 1
            dve.wait_ge(ranks_done, 1)
            then(nc.vector.tensor_reduce(number[:], free_ap(route_ps[:, 1, :], 0, [[1, E], [E, NT]]), AX.X, ALU.add))
            then(nc.vector.tensor_tensor(over[:], free_ap(number[:], 0, [[1, E], [0, NT]]),
                                         free_ap(full[:], 0, [[0, E], [1, NT]]), ALU.is_gt))
            then(nc.vector.tensor_reduce(blocks[:], over[:], AX.X, ALU.add))
            then(nc.vector.tensor_tensor(cum[:], upto[:], free_ap(blocks[:], 0, [[0, E], [1, E]]), ALU.mult))
            then(nc.vector.tensor_reduce(end[:], cum[:], AX.X, ALU.add))
            then(nc.vector.tensor_tensor(start[:], end[:], blocks[:], ALU.subtract))
            then(nc.vector.tensor_scalar(start[:], start[:], float(P), None, ALU.mult))
            then(nc.vector.tensor_tensor(place[:], route_ps[:, 0, :].rearrange("p (t e) -> p t e", e=E),
                                         over_t(start[:]), ALU.add))
            then(nc.vector.tensor_tensor(place[:], place[:], onehot[:], ALU.mult))
            then(nc.vector.tensor_reduce(slot[:], place[:], AX.X, ALU.add))
            nc.vector.tensor_copy(slot_i[:], slot[:]).then_inc(slot_done, 1)
            then(nc.vector.tensor_tensor(past[:], free_ap(end[:], 0, [[0, BLOCKS], [1, E]]),
                                         free_ap(block_no[:], 0, [[1, BLOCKS], [0, E]]), ALU.is_le))
            then(nc.vector.tensor_reduce(owner[:], past[:], AX.X, ALU.add))
            nc.vector.tensor_scalar(owner_i[:], owner[:], float(E - 1), None, ALU.min).then_inc(owner_done, 1)

            for i in range(W_JOBS):
                e, c = divmod(i, DC)
                dve.wait_ge(w_hi_done, i + 1)
                nc.vector.tensor_tensor(wt_lo[:, c, e * D:(e + 1) * D], ring[i % RING][:, :],
                                        wt_hi[:, c, e * D:(e + 1) * D].bitcast(F32), ALU.subtract).then_inc(w_split, 1)
            dve.wait_ge(bias_in, 16)
            dve.wait_ge(owner_done, 1)

            def finish(i, k):
                m = number_of(i, k)
                e = dve.value_load(owner_i[0:1, bass.ds(m, 1)] if not isinstance(m, int) else owner_i[0:1, m:m + 1],
                                   min_val=0, max_val=E - 1)
                if k >= 2:
                    dve.wait_ge(out_done[(k - 2) % RX], (turn(i, k - 2) + 1) * 16)
                dve.wait_ge(y_done, m + 1)
                nc.vector.tensor_tensor(y_sb[:, k % 2, :], y_ps[k % 2][:, :], bias_sb[:, bass.ds(e * D, D)], ALU.add)\
                    .then_inc(bias_done, 1)
                dve.wait_ge(bias_done, m + 1)
                gate = column(tab, i, k, 1).bitcast(F32)
                nc.vector.scalar_tensor_tensor(y_sb[:, k % 2, :], y_sb[:, k % 2, :], gate, rows[:, k % RX, 0:D],
                                               ALU.mult, ALU.add).then_inc(fin_done, 1)

            def step(i, k):
                m = number_of(i, k)
                dve.wait_ge(xt_hi_done, m + 1)
                nc.vector.tensor_tensor(xt_lo[:, k % 2, :], t_ps[k % 2][:, :], xt_hi[:, k % 2, :].bitcast(F32),
                                        ALU.subtract).then_inc(xt_done, 1)
                if k >= 1:
                    finish(i, k - 1)

            blocks_loop(dve, step)
            finish(0, BLOCKS - 1)


def program(nc, x, ctx, w_qkv, w_out, wq, wk, wv, wo, wg, w, bias, out):
    with ExitStack() as cx:
        ident = cx.enter_context(nc.sbuf_tensor("ident", [P, P], F32))
        logits = cx.enter_context(nc.sbuf_tensor("logits", [P, NT, E], F32))
        x1 = nc.dram_tensor("x1", [B * S, D], F32).ap()
        x2n = nc.dram_tensor("x2n", [B * S, 2 * D], F32).ap()
        table = nc.dram_tensor("slots", [P * (NT + E - 1), 2], I32).ap()
        self_attention(nc, ident, x, w_qkv, w_out, x1)
        cross_attention(nc, ident, logits, x1, ctx, wq, wk, wv, wo, wg, x2n)
        mixture_of_experts(nc, ident, logits, x2n, w, bias, table, out)


def kernel(x, ctx_2048, mask_BxSx4224_bf0, L0_attn_w_qkv, L0_attn_w_out, L0_xattn_wq, L0_xattn_wk, L0_xattn_wv,
           L0_xattn_wo, L0_ffn_wg, L0_ffn_W, L0_ffn_b):
    import concourse.bacc as bacc
    import numpy as np
    from concourse.bass_utils import run_bass_kernel_spmd

    rows = lambda t: np.ascontiguousarray(np.asarray(t).reshape(B * S, D))
    arrays = {"x": rows(x), "ctx": rows(ctx_2048), "w_qkv": L0_attn_w_qkv, "w_out": L0_attn_w_out, "wq": L0_xattn_wq,
              "wk": L0_xattn_wk, "wv": L0_xattn_wv, "wo": L0_xattn_wo, "wg": L0_ffn_wg, "w": L0_ffn_W,
              "bias": L0_ffn_b}
    arrays = {f"in_{n}": np.ascontiguousarray(a) for n, a in arrays.items()}
    nc = bacc.Bacc("TRN2", target_bir_lowering=False, num_devices=1)
    args = [nc.dram_tensor(n, a.shape, mybir.dt.from_np(a.dtype), kind="ExternalInput").ap()
            for n, a in arrays.items()]
    out = nc.dram_tensor("result", [B * S, D], F32, kind="ExternalOutput").ap()
    program(nc, *args, out)
    r = run_bass_kernel_spmd(nc, [arrays], core_ids=[0])
    return r.results[0]["result"].reshape(B, S, D)
```

```python
from contextlib import ExitStack

import concourse.bass as bass
from concourse import mybir

F32 = mybir.dt.float32
F32R = mybir.dt.float32r
BF16 = mybir.dt.bfloat16
I32 = mybir.dt.int32
U32 = mybir.dt.uint32
ALU = mybir.AluOpType
ACT = mybir.ActivationFunctionType
AX = mybir.AxisListType

P = 128
B, S, D = 8, 256, 512
DC = D // P
TB = S // P
NT = B * TB
H, HD = 16, 32
HG = P // HD
G = H // HG
E = 8
STAGED = 3
EPS = 1e-5
NEG = -1e10
BIG = 3e38


def free_ap(ap, offset, dims):
    return bass.AP(tensor=ap.tensor, offset=ap.offset + offset, ap=[list(ap.ap[0])] + dims)


def wait(engine, semaphore, value):
    if not isinstance(value, int) or value > 0:
        engine.wait_ge(semaphore, value)


def batch_rows(tensor, b):
    rows = tensor[b * S:(b + 1) * S, :] if isinstance(b, int) else tensor[bass.ds(b * S, S), :]
    return rows.rearrange("(t p) n -> p t n", p=P)


def three_pass(pe_matmul, out, lhs, rhs, first=True, last=True):
    (lh, ll), (rh, rl) = lhs, rhs
    steps = [(a, b) for a, b in zip(lh, rh)] + [(a, b) for a, b in zip(lh, rl)] + [(a, b) for a, b in zip(ll, rh)]
    for i, (a, b) in enumerate(steps):
        ins = pe_matmul(out, a, b, start=first and i == 0, stop=last and i == len(steps) - 1)
    return ins



def self_attention(nc, ident, x, w_qkv, w_out, x1, xin, xr, x1_out, x1_last_out, x1_first_in, stage, stage_in, next_weights):
    scale = float(HD) ** -0.5
    GH = G // 2
    HEAD_IN = 16 * 3
    NPROB, NPT = 4, 4
    STRIP = 352
    V_AT = {0: 0, 3: 128, 1: 192, 2: 288}
    with ExitStack() as cx:
        sb = lambda n, s, d=F32: cx.enter_context(nc.sbuf_tensor(n, s, d))
        ps = lambda n, s: cx.enter_context(nc.psum_tensor(n, s, F32))
        sem = lambda n: cx.enter_context(nc.semaphore(n))
        w_hi, w_lo = sb("wqkv_hi", [P, DC, 3 * D], F32R), sb("wqkv_lo", [P, DC, 3 * D], F32R)
        wo_hi, wo_lo = sb("wout_hi", [P, DC, D], F32R), sb("wout_lo", [P, DC, D], F32R)
        stats, mv = sb("a_stats", [P, TB, 6]), sb("a_mv", [P, TB, 2])
        veps, rstd, expo = sb("a_veps", [P, TB]), sb("a_rstd", [P, TB]), sb("a_expo", [P, TB])
        xn = sb("a_xn", [P, TB, D])
        xt_hi, xt_lo = sb("a_xt_hi", [P, DC, S], F32R), sb("a_xt_lo", [P, DC, S], F32R)
        qk = sb("qk", [P, 2, 4, GH, S], F32R)
        v_hi, v_lo = sb("v_hi", [P, TB, G * STRIP], F32R), sb("v_lo", [P, TB, G * STRIP], F32R)
        mask = sb("mask", [P, 2 * P])
        nmax = sb("nmax", [P, H, TB])
        prob = sb("prob", [P, NPROB, 3 * P])
        rsum, rinv8 = sb("rsum", [P, G, TB, HG]), sb("rinv8", [P, G, TB, HG])
        rinv = sb("rinv", [P, TB, HG, HD])
        r_sb = o_sb = rinv[:].rearrange("p q j d -> p (q j d)")
        pt_hi, pt_lo = sb("pt_hi", [P, NPT, 4 * P], F32R), sb("pt_lo", [P, NPT, 4 * P], F32R)
        ot_hi, ot_lo = sb("ot_hi", [P, G, S], F32R), sb("ot_lo", [P, G, S], F32R)
        with ExitStack() as early:
            raw = early.enter_context(nc.sbuf_tensor("a_raw", [P, 4, DC, D], F32))
        stack = sb("stack", [3 * HD, 2, HG, 2, GH, S], F32R)
        job_ps = [ps(f"a_job{i}", [P, D]) for i in range(2)]
        s_ps = [ps(f"a_s{i}", [P, TB, S]) for i in range(2)]
        t_ps = [ps(f"a_t{i}", [P, 4 * P]) for i in range(2)]
        o_ps = [ps(f"a_o{i}", [P, 2, S]) for i in range(2)]

        x0_in, x_in, xr_in = sem("a_x0_in"), sem("a_x_in"), sem("a_xr_in")
        w_in = [sem(f"a_w_in{i}") for i in range(4)]
        consts, tick, tick_sp = sem("a_consts"), sem("a_tick"), sem("a_tick_sp")
        w_split_hi, w_split, wo_split = sem("w_split_hi"), sem("w_split"), sem("wo_split")
        ln_dve, ln_rstd, xn_ready = sem("a_ln_dve"), sem("a_ln_rstd"), sem("a_xn_ready")
        job_done, job_hi, job_ev = sem("a_job_done"), sem("a_job_hi"), sem("a_job_ev")
        stacked = [[sem(f"stacked_{half}_{j}") for j in range(HG)] for half in range(2)]
        s_done, mx_done, ex_done = sem("s_done"), sem("mx_done"), sem("ex_done")
        rinv8_done, rinv_done, t_done = sem("rinv8_done"), sem("rinv_done"), sem("t_done")
        pt_hi_done, pt_done = sem("pt_hi_done"), sem("pt_done")
        av_done, r_done, rs_done = sem("av_done"), sem("r_done"), sem("rs_done")
        on_done, ot_hi_done, ot_done = sem("on_done"), sem("ot_hi_done"), sem("ot_done")

        SLOTS = {0: ["q3"], 2: ["k3"], 4: ["w0"], 5: ["w1", "X0"], 6: ["X1"], 7: ["y0"], 8: ["y1"], 9: ["q0"], 10: ["k0"],
                 11: ["q1", "k1"], 12: ["u0"], 13: ["u1"], 14: ["q2"], 15: ["k2"]}
        OWN, LATE = ("q3", "k3", "w0", "w1"), ("y0", "y1")
        ORDER = [j for s in sorted(SLOTS) for j in SLOTS[s]]
        PROLOGUE = ["X0", "X1", "q0", "k0", "q1", "k1", "q2", "k2", "u0", "u1"]
        assert sorted(PROLOGUE) == sorted(j for j in ORDER if j not in OWN + LATE)
        JOBS, HI_JOBS = len(ORDER), len(ORDER) - len(LATE)
        assert JOBS % 2 == 0
        T_LAG, LO_LAG, RINV_LAG, AV_LAG, R_LAG, ON_LAG, OT_LAG = 2, 3, 3, 4, 5, 6, 7
        LO_JOB_LAG = 1
        EPILOGUE_SLOTS = 10
        SPLIT_AT = {"X0": 0, "q0": 1, "q2": 2}

        def w_part(w, i):
            return w[:, :, i * D:(i + 1) * D]

        def has(j, n):
            if not isinstance(n, int):
                return True
            return n >= 1 if j in LATE else n < B if j in OWN else n < B - 1

        def number(j, n):
            return [i for i in ORDER if has(i, n)].index(j)

        def job_at(j, n):
            if not isinstance(n, int):
                return len(PROLOGUE) - len(LATE) + n * JOBS + number(j, n)
            if n < 0:
                return PROLOGUE.index(j)
            return len(PROLOGUE) + sum(has(i, m) for m in range(n) for i in ORDER) + number(j, n)

        def hi_at(j, n):
            if isinstance(n, int) and n < 0:
                return PROLOGUE.index(j)
            order = [i for i in ORDER if has(i, n) and i not in LATE]
            return len(PROLOGUE) + n * HI_JOBS + order.index(j)

        def bank(j, n):
            return job_ps[(job_at(j, n) if isinstance(n, int) else len(PROLOGUE) - len(LATE) + number(j, n)) % 2]

        def jobs_of(slot, n):
            return [j for j in SLOTS.get(slot, []) if has(j, n)]

        def head_at(slot, lag, n):
            t = slot - lag
            if isinstance(n, int) and (n < 1 if t < 0 else n >= B):
                return None
            return t % H if t < H else None

        def group_at(slot, lag, n):
            a = head_at(slot, lag, n)
            return a // HG if a is not None and a % HG == HG - 1 else None

        def groups_before(slot, lag, n):
            return n * G + (slot - lag) // HG

        def pe_job(j, n, tensor=nc.tensor):
            b, i = bank(j, n), int(j[1])
            toks = slice(i * P, (i + 1) * P)
            chunks = range(DC)
            if j[0] == "X":
                for c in chunks:
                    m = tensor.transpose(b[:, c * P:(c + 1) * P], xn[:, i, c * P:(c + 1) * P], ident[:])
            elif j[0] in "uw":
                o = 2 * D + (0 if j[0] == "u" else D // 2)
                cols = slice(o, o + D // 2)
                m = three_pass(tensor.matmul, b[:, 0:D // 2],
                               ([xt_hi[:, c, toks] for c in chunks], [xt_lo[:, c, toks] for c in chunks]),
                               ([w_hi[:, c, cols] for c in chunks], [w_lo[:, c, cols] for c in chunks]))
            elif j[0] == "y":
                m = three_pass(tensor.matmul, b[:, :],
                               ([ot_hi[:, c, toks] for c in chunks], [ot_lo[:, c, toks] for c in chunks]),
                               ([wo_hi[:, c, :] for c in chunks], [wo_lo[:, c, :] for c in chunks]))
            else:
                o = (0 if j[0] == "q" else D) + i * P
                m = three_pass(tensor.matmul, b[:, 0:S],
                               ([w_hi[:, c, o:o + P] for c in chunks], [w_lo[:, c, o:o + P] for c in chunks]),
                               ([xt_hi[:, c, :] for c in chunks], [xt_lo[:, c, :] for c in chunks]))
            m.then_inc(job_done, 1)

        def parts_of(j, n):
            b, i = bank(j, n), int(j[1])
            if j[0] == "X":
                cols = slice(i * P, (i + 1) * P)
                return [(xt_hi[:, :, cols], xt_lo[:, :, cols], b[:, :].rearrange("p (c n) -> p c n", c=DC))]
            if j[0] in "uw":
                first = 0 if j[0] == "u" else GH * STRIP
                out = []
                for a, z in ((0, 3), (1, 2)):
                    dst = [[STRIP, GH], [V_AT[z] - V_AT[a], 2], [1, HD]]
                    out.append((free_ap(v_hi[:, i, :], first + V_AT[a], dst), free_ap(v_lo[:, i, :], first + V_AT[a], dst),
                                free_ap(b[:, :], a * HD, [[P, GH], [(z - a) * HD, 2], [1, HD]])))
                return out
            w = 0 if j[0] == "q" else 2
            at = lambda part: qk[:, i // GH, w + part, i % GH, :]
            return [(at(0), at(1), b[:, 0:S])]

        block = cx.enter_context(nc.Block())

        @block.sync
        def _(sp):
            sp.dma_start(xin[:], batch_rows(x, 0)).then_inc(x0_in, 16)
            for i, w in enumerate([w_qkv[:, j * D:(j + 1) * D] for j in range(3)] + [w_out]):
                sp.dma_start(raw[:, i, :, :], w.rearrange("(c p) n -> p c n", p=P)).then_inc(w_in[i], 16)
            for i, w in enumerate(next_weights):
                sp.dma_start(stage[i][:], w.rearrange("(c p) n -> p c n", p=P)).then_inc(stage_in[i], 16)

            def stack_half(half):
                for j in range(HG):
                    for r, parts in enumerate((slice(0, 3, 2), slice(1, 3), slice(0, 4, 3))):
                        dst = stack[HD * r:HD * (r + 1), half, j, :, :, :].bitcast(F32)
                        src = qk[HD * j:HD * (j + 1), half, parts, :, :].bitcast(F32)
                        sp.dma_start(dst.rearrange("p w g s -> p w (g s)"),
                                     src.rearrange("p w g s -> p w (g s)")).then_inc(stacked[half][j], 16)

            def batch(n):
                wait(sp, job_ev, job_at("k3", n) + 1)
                sp.sem_inc(tick_sp, 1)
                if isinstance(n, int) and n == 0:
                    sp.wait_ge(w_split, 3)
                    sp.wait_ge(wo_split, 2)
                wait(sp, s_done, n * H)
                stack_half(1)
                if has("k1", n):
                    wait(sp, job_ev, job_at("k1", n) + 1)
                    sp.sem_inc(tick_sp, 1)
                    wait(sp, s_done, n * H + H // 2)
                    stack_half(0)

            wait(sp, job_ev, job_at("k1", -1) + 1)
            sp.wait_ge(w_split, 2)
            stack_half(0)
            batch(0)
            with sp.Fori(1, B - 1) as n:
                batch(n)
            batch(B - 1)
            sp.wait_ge(job_ev, job_at("y1", B) + 1)
            sp.dma_start(batch_rows(x1, B - 1), xr[:]).then_inc(x1_last_out, 16)

        @block.gpsimd
        def _(pool):
            nc.gpsimd.memset(ident[:], 0.0).then_inc(consts, 1)
            nc.gpsimd.memset(mask[:], 0.0).then_inc(consts, 1)
            nc.gpsimd.memset(expo[:], -0.5).then_inc(consts, 1)
            pool.wait_ge(consts, 3)
            nc.gpsimd.affine_select(out=ident[:], in_=ident[:], compare_op=ALU.not_equal, fill=1.0, base=0,
                                    pattern=[[-1, P]], channel_multiplier=1).then_inc(consts, 1)
            nc.gpsimd.affine_select(out=mask[:, P:], in_=mask[:, P:], compare_op=ALU.is_ge, fill=NEG, base=0,
                                    pattern=[[-1, P]], channel_multiplier=1).then_inc(consts, 1)

            def rstd_and_next(k, after):
                pool.wait_ge(ln_dve, k * 5 + 5)
                nc.gpsimd.tensor_tensor(rstd[:], veps[:], expo[:], ALU.pow).then_inc(ln_rstd, 1)
                if after:
                    pool.wait_ge(xn_ready, k * TB + TB)
                    pool.dma_start(xin[:], batch_rows(x, k + 1)).then_inc(x_in, 16)

            def store(k):
                pool.wait_ge(job_ev, job_at("y1", k + 1) + 1)
                pool.dma_start(batch_rows(x1, k), xr[:]).then_inc(x1_out, 16)
                pool.wait_ge(x1_out, k * 16 + 16)
                pool.dma_start(xr[:], batch_rows(x, k + 1)).then_inc(xr_in, 16)

            rstd_and_next(0, True)
            pool.dma_start(xr[:], batch_rows(x, 0)).then_inc(xr_in, 16)
            for t in (pt_hi, pt_lo):
                nc.gpsimd.memset(t[:, :, 0:P].bitcast(F32), 0.0).then_inc(consts, 1)
            for t in (v_hi, v_lo):
                nc.gpsimd.memset(t[:].bitcast(F32), 0.0).then_inc(consts, 1)
            pool.wait_ge(w_in[3], 16)
            nc.gpsimd.tensor_copy(wo_hi[:], raw[:, 3, :, :]).then_inc(wo_split, 1)
            pool.wait_ge(wo_split, 1)
            nc.gpsimd.tensor_tensor(wo_lo[:], raw[:, 3, :, :], wo_hi[:].bitcast(F32), ALU.subtract).then_inc(wo_split, 1)
            rstd_and_next(1, True)
            with pool.Fori(1, B - 2) as n:
                rstd_and_next(n + 1, True)
                store(n - 1)
            rstd_and_next(B - 1, False)
            pool.wait_ge(xn_ready, B * TB)
            pool.wait_ge(x1_out, 16)
            pool.dma_start(xin[:], batch_rows(x1, 0)).then_inc(x1_first_in, 16)
            store(B - 3)
            store(B - 2)

        CONSTS = 9

        @block.scalar
        def _(act):
            def evac(j, n):
                act.wait_ge(job_done, job_at(j, n) + 1)
                if j in ("q0", "q2"):
                    for s in stacked["q0 q2".split().index(j)]:
                        wait(act, s, (n + 1) * HEAD_IN)
                if j == "u0":
                    wait(act, av_done, n * H + H // 2 if not isinstance(n, int) or n >= 0 else 0)
                if j == "w0":
                    wait(act, av_done, n * H)
                pieces = parts_of(j, n)
                for i, (hi, _, src) in enumerate(pieces):
                    e = nc.scalar.copy(hi, src)
                e.then_inc(job_hi, 1)

            for j in PROLOGUE:
                if j in SPLIT_AT:
                    i = SPLIT_AT[j]
                    act.wait_ge(w_in[i], 16)
                    nc.scalar.copy(w_part(w_hi, i), raw[:, i, :, :]).then_inc(w_split_hi, 1)
                if j == "u0":
                    act.wait_ge(consts, CONSTS)
                evac(j, -1)

            def slot(n, h):
                e = head_at(h, 0, n)
                if e is not None:
                    g, j = divmod(e, HG)
                    act.wait_ge(mx_done, n * H + h + 1)
                    for q, cols in ((0, slice(0, P)), (1, slice(P, 3 * P))):
                        a = nc.scalar.activation(prob[:, e % NPROB, cols], prob[:, e % NPROB, cols], ACT.Exp, scale=-1.0,
                                                 bias=nmax[:, e, q:q + 1], accum_out=rsum[:, g, q, j:j + 1])
                    a.then_inc(ex_done, 1)
                for j in jobs_of(h, n):
                    if j not in LATE:
                        evac(j, n)
                t = head_at(h, T_LAG, n)
                if t is not None:
                    act.wait_ge(t_done, n * H + h - T_LAG + 1)
                    wait(act, av_done, n * H + h - T_LAG + 1 - NPT)
                    nc.scalar.copy(pt_hi[:, t % NPT, P:], t_ps[t % 2][:, P:]).then_inc(pt_hi_done, 1)
                g = group_at(h, R_LAG, n)
                if g is not None:
                    act.wait_ge(r_done, groups_before(h, R_LAG, n) + 1)
                    nc.scalar.copy(r_sb, o_ps[g % 2][:, 1, :]).then_inc(rs_done, 1)
                g = group_at(h, ON_LAG, n)
                if g is not None:
                    if g == 0 and not (isinstance(n, int) and n < 1):
                        act.wait_ge(job_done, job_at("y1", n) + 1)
                    act.wait_ge(on_done, groups_before(h, ON_LAG, n) + 1)
                    nc.scalar.copy(ot_hi[:, g, :], o_sb).then_inc(ot_hi_done, 1)

            for h in range(H):
                slot(0, h)
            with act.Fori(1, B - 1) as n:
                for h in range(H):
                    slot(n, h)
            for h in range(H):
                slot(B - 1, h)
            for h in range(EPILOGUE_SLOTS):
                slot(B, h)

        @block.tensor
        def _(pe):
            def job(j, n):
                if j == "X0":
                    pe.wait_ge(xn_ready, (n + 2) * TB)
                if j == "q0":
                    pe.wait_ge(job_ev, job_at("X1", n) + 1)
                if j == "y0":
                    pe.wait_ge(ot_done, n * G)
                wait(pe, job_ev, job_at(j, n) - 1)
                pe_job(j, n)

            pe.wait_ge(consts, 4)
            for j in PROLOGUE:
                if j in ("q0", "k0", "u0"):
                    pe.wait_ge(w_split, "qku".index(j[0]) + 1)
                job(j, -1)

            def slot(n, h):
                s = head_at(h, 0, n)
                if s is not None:
                    g, j = divmod(s, HG)
                    if s % (H // 2) < HG:
                        pe.wait_ge(stacked[g // GH][j], (n + 1) * HEAD_IN)
                    wait(pe, mx_done, n * H + h - 1)
                    for q in range(TB):
                        m = nc.tensor.matmul(s_ps[s % 2][:, q, :], stack[:, g // GH, j, 0, g % GH, q * P:(q + 1) * P],
                                             stack[:, g // GH, j, 1, g % GH, :], start=True, stop=True)
                    m.then_inc(s_done, 1)
                for j in jobs_of(h, n):
                    job(j, n)
                t = head_at(h, T_LAG, n)
                if t is not None:
                    pe.wait_ge(ex_done, n * H + h - T_LAG + 1)
                    wait(pe, pt_done, n * H + h - T_LAG - 1)
                    for o, cols in ((P, slice(2 * P, 3 * P)), (2 * P, slice(0, P)), (3 * P, slice(P, 2 * P))):
                        m = nc.tensor.transpose(t_ps[t % 2][:, o:o + P], prob[:, t % NPROB, cols], ident[:])
                    m.then_inc(t_done, 1)
                a = head_at(h, AV_LAG, n)
                if a is not None:
                    g, j = divmod(a, HG)
                    of = n if h >= AV_LAG else n - 1
                    if a == 0:
                        pe.wait_ge(job_ev, job_at("u1", of - 1) + 1)
                    if a == H // 2:
                        pe.wait_ge(job_ev, job_at("w1", of) + 1)
                    if j == 0:
                        wait(pe, on_done, groups_before(h, AV_LAG, n) - 1)
                    pe.wait_ge(pt_done, n * H + h - AV_LAG + 1)
                    at = g * STRIP + V_AT[j] - HD * j
                    keys = range(TB)
                    ranges = [slice(2 * P, 4 * P), slice(0, 2 * P)]
                    m = three_pass(nc.tensor.matmul, o_ps[g % 2][:, 0, :],
                                   ([v_hi[:, k, at:at + P] for k in keys], [v_lo[:, k, at:at + P] for k in keys]),
                                   ([pt_hi[:, a % NPT, r] for r in ranges], [pt_lo[:, a % NPT, r] for r in ranges]),
                                   j == 0, j == HG - 1)
                    m.then_inc(av_done, 1)
                    if j == HG - 1:
                        pe.wait_ge(rinv_done, groups_before(h, AV_LAG, n) + 1)
                        for q in range(TB):
                            m = nc.tensor.matmul(o_ps[g % 2][:, 1, q * P:(q + 1) * P],
                                                 rinv[:, q, :, :].rearrange("p j d -> p (j d)"), ident[:],
                                                 start=True, stop=True)
                        m.then_inc(r_done, 1)

            for h in range(H):
                slot(0, h)
            pe.wait_ge(wo_split, 2)
            with pe.Fori(1, B - 1) as n:
                for h in range(H):
                    slot(n, h)
            for h in range(H):
                slot(B - 1, h)
            for h in range(EPILOGUE_SLOTS):
                slot(B, h)

        @block.vector
        def _(dve):
            def norm_stats(k):
                if isinstance(k, int) and k == 0:
                    dve.wait_ge(x0_in, 16)
                else:
                    dve.wait_ge(x_in, k * 16)
                dve.sem_inc(tick, 1)
                for t in range(TB):
                    nc.vector.bn_stats(stats[:, t, :], xin[:, t, :]).then_inc(ln_dve, 1)
                for t in range(TB):
                    dve.wait_ge(ln_dve, k * 5 + 1 + t)
                    dve.sem_inc(tick, 1)
                    nc.vector.bn_aggr(mv[:, t, :], stats[:, t, :]).then_inc(ln_dve, 1)
                dve.wait_ge(ln_dve, k * 5 + 4)
                nc.vector.tensor_scalar(veps[:], mv[:, :, 1], EPS, None, ALU.add).then_inc(ln_dve, 1)

            def norm_apply(k):
                dve.wait_ge(ln_rstd, k + 1)
                for t in range(TB):
                    nc.vector.tensor_scalar(xn[:, t, :], xin[:, t, :], mv[:, t, 0:1], rstd[:, t:t + 1],
                                            ALU.subtract, ALU.mult).then_inc(xn_ready, 1)

            def evac(j, n):
                dve.wait_ge(job_hi, hi_at(j, n) + 1)
                pieces = parts_of(j, n)
                for hi, lo, src in pieces:
                    m = nc.vector.tensor_tensor(lo, src, hi.bitcast(F32), ALU.subtract)
                m.then_inc(job_ev, 1)

            norm_stats(0)
            norm_apply(0)
            for j in PROLOGUE:
                if j in SPLIT_AT:
                    i = SPLIT_AT[j]
                    dve.wait_ge(w_split_hi, i + 1)
                    nc.vector.tensor_tensor(w_part(w_lo, i), raw[:, i, :, :], w_part(w_hi, i).bitcast(F32),
                                            ALU.subtract).then_inc(w_split, 1)
                if j == "u0":
                    dve.wait_ge(consts, CONSTS)
                evac(j, -1)

            def slot(n, h):
                before = h - LO_JOB_LAG
                for j in jobs_of(before, n) if before >= 0 else jobs_of(H + before, n - 1 if isinstance(n, int) else n):
                    of = n if before >= 0 else n - 1
                    if isinstance(of, int) and of < 0:
                        continue
                    if j in LATE:
                        dve.wait_ge(job_done, job_at(j, of) + 1)
                        dve.wait_ge(xr_in, 16 * of)
                        xt = xr[:, int(j[1]), :]
                        nc.vector.tensor_tensor(xt, bank(j, of)[:, :], xt, ALU.add).then_inc(job_ev, 1)
                    else:
                        evac(j, of)
                s = head_at(h, 0, n)
                if s is not None:
                    dve.wait_ge(s_done, n * H + h + 1)
                    wait(dve, t_done, n * H + h - NPROB + 1)
                    dve.sem_inc(tick, 1)
                    for q, cols in ((0, slice(0, P)), (1, slice(P, 3 * P))):
                        m = nc.vector.tensor_tensor_reduce(
                            out=prob[:, s % NPROB, cols], in0=s_ps[s % 2][:, q, 0:P * (q + 1)],
                            in1=mask[:, P * (1 - q):], scale=-scale, scalar=BIG, op0=ALU.add, op1=ALU.min,
                            accum_out=nmax[:, s, q:q + 1])
                    m.then_inc(mx_done, 1)
                t = head_at(h, LO_LAG, n)
                if t is not None:
                    dve.wait_ge(pt_hi_done, n * H + h - LO_LAG + 1)
                    nc.vector.tensor_tensor(pt_lo[:, t % NPT, P:], t_ps[t % 2][:, P:],
                                            pt_hi[:, t % NPT, P:].bitcast(F32), ALU.subtract).then_inc(pt_done, 1)
                g = group_at(h, ON_LAG, n)
                if g is not None:
                    dve.wait_ge(rs_done, groups_before(h, ON_LAG, n) + 1)
                    nc.vector.tensor_tensor(o_sb, o_ps[g % 2][:, 0, :], r_sb, ALU.mult).then_inc(on_done, 1)
                g = group_at(h, OT_LAG, n)
                if g is not None:
                    dve.wait_ge(ot_hi_done, groups_before(h, OT_LAG, n) + 1)
                    nc.vector.tensor_tensor(ot_lo[:, g, :], o_sb, ot_hi[:, g, :].bitcast(F32),
                                            ALU.subtract).then_inc(ot_done, 1)
                g = group_at(h, RINV_LAG, n)
                if g is not None:
                    before = groups_before(h, RINV_LAG, n)
                    dve.wait_ge(ex_done, before * HG + HG)
                    nc.vector.reciprocal(rinv8[:, g, :, :], rsum[:, g, :, :]).then_inc(rinv8_done, 1)
                    dve.wait_ge(rinv8_done, before + 1)
                    wait(dve, ot_done, before)
                    nc.vector.tensor_copy(rinv[:], free_ap(rinv8[:, g, :, :], 0, [[HG, TB], [1, HG], [0, HD]]))\
                        .then_inc(rinv_done, 1)
                if head_at(h, 0, n) is not None and (not isinstance(n, int) or n < B - 1):
                    if h == 0:
                        norm_stats(n + 1)
                    if h == 2:
                        norm_apply(n + 1)

            for h in range(H):
                slot(0, h)
            with dve.Fori(1, B - 1) as n:
                for h in range(H):
                    slot(n, h)
            for h in range(H):
                slot(B - 1, h)
            for h in range(EPILOGUE_SLOTS):
                slot(B, h)


def cross_attention(nc, ident, logits, x1, x1_out, x1_last_out, x1_first_in, ctx, wv, wo, wg, x2n, x2n_out, xin, xr, x2_sb, xn3_sb, stage, stage_in, w, expert_in):
    scale = float(D) ** -0.5
    RING = 7
    KEYS = 2 * S
    KC = KEYS // P
    with ExitStack() as cx:
        sb = lambda n, s, d=F32: cx.enter_context(nc.sbuf_tensor("b_" + n, s, d))
        sem = lambda n: cx.enter_context(nc.semaphore("b_" + n))
        raw = stage + [sb("raw_o", [P, DC, D])]
        wt_hi = {n: sb(f"w{n}t_hi", [P, DC, D], F32R) for n in "qkvo"}
        wt_lo = {n: sb(f"w{n}t_lo", [P, DC, D], F32R) for n in "qkvo"}
        wg_sb = sb("wg", [P, DC, E])
        cin, xn = sb("cin", [P, TB, D]), sb("xn", [P, TB, D])
        stats, mv, veps, rstd = sb("stats", [P, 2, TB, 6]), sb("mv", [P, 2, TB, 2]), sb("veps", [P, 2, TB]), sb("rstd", [P, 2, TB])
        expo = sb("expo", [P, TB])
        xt_hi, xt_lo = sb("xt_hi", [P, DC, S], F32R), sb("xt_lo", [P, DC, S], F32R)
        qt_hi, qt_lo = sb("qt_hi", [P, DC, S], F32R), sb("qt_lo", [P, DC, S], F32R)
        kt_hi, kt_lo = sb("kt_hi", [P, DC, KEYS], F32R), sb("kt_lo", [P, DC, KEYS], F32R)
        v_hi, v_lo = sb("v_hi", [P, KC, D], F32R), sb("v_lo", [P, KC, D], F32R)
        smax, nmax, rsum, rinv = sb("smax", [P, TB]), sb("nmax", [P, TB]), sb("rsum", [P, TB]), sb("rinv", [P, TB])
        prob = sb("prob", [P, TB, KEYS])
        pt_hi, pt_lo = sb("pt_hi", [P, KC, S], F32R), sb("pt_lo", [P, KC, S], F32R)
        ot_hi, ot_lo = sb("ot_hi", [P, DC, S], F32R), sb("ot_lo", [P, DC, S], F32R)
        xt3 = sb("xt3", [P, DC, S])
        ring = [cx.enter_context(nc.psum_tensor(f"b_bank{i}", [P, D], F32)) for i in range(RING)]

        w_in = stage_in + [sem("wo_in")]
        wg_in, x_in, xr_in, c_in = (sem(n) for n in ("wg_in", "x_in", "xr_in", "c_in"))
        x2_out, xn3_out = x2n_out
        consts, tick = sem("consts"), sem("tick")
        ln_dve, ln_rstd, xn_ready = sem("ln_dve"), sem("ln_rstd"), sem("xn_ready")
        ln3_dve, ln3_rstd, xn3_ready = sem("ln3_dve"), sem("ln3_rstd"), sem("xn3_ready")
        job_done, job_hi, job_ev = sem("job_done"), sem("job_hi"), sem("job_ev")
        c_hi, c_split = sem("c_hi"), sem("c_split")
        max_done, mx_done, ex_done, rinv_done = sem("max_done"), sem("mx_done"), sem("ex_done"), sem("rinv_done")

        ORDER = ("X0 X1 s0 s1 C0 C1 q0 q1 p0 p1 q2 q3 o0 o1 o2 o3 k0 y0 y1 k1 k2 k3 v0 Y0 Y1 v1 l0 l1").split()
        FRONT = "XCqkv"
        LAST = [j for j in ORDER if j[0] not in FRONT]
        PROLOGUE = ("wq0 wq1 wq2 wq3 wk0 wk1 X0 X1 wk2 wk3 q0 q1 C0 C1 q2 q3 wv0 wv1 k0 k1 wv2 wv3 k2 k3 wo0 v0 wo1 v1 "
                    "wo2 wo3").split()
        ev_jobs = lambda js: [j for j in js if j[0] != "s"]
        hi_jobs = lambda js: [j for j in js if j[0] not in "syYl"]

        def order(n):
            return ORDER if not isinstance(n, int) or n < B - 1 else LAST

        def count(j, n, kind):
            if isinstance(n, int) and n < 0:
                return kind(PROLOGUE).index(j)
            return len(kind(PROLOGUE)) + n * len(kind(ORDER)) + kind(order(n)).index(j)

        done_at = lambda j, n: count(j, n, list) + 1
        ev_at = lambda j, n: count(j, n, ev_jobs) + 1
        hi_at = lambda j, n: count(j, n, hi_jobs) + 1

        def bank(j, n):
            if isinstance(n, int) and n < 0:
                return ring[PROLOGUE.index(j) % RING]
            return ring[(len(PROLOGUE) + order(n).index(j)) % RING]
        assert len(ORDER) % RING == 0

        def parts_of(j, n):
            b, i = bank(j, n), int(j[-1])
            toks = slice(i * P, (i + 1) * P)
            chunked = b[:, :].rearrange("p (c n) -> p c n", c=DC)
            return {"w": lambda: (wt_hi[j[1]][:, i, :], wt_lo[j[1]][:, i, :], b[:, :]),
                    "X": lambda: (xt_hi[:, :, toks], xt_lo[:, :, toks], chunked),
                    "C": lambda: (kt_hi[:, :, toks], kt_lo[:, :, toks], chunked),
                    "q": lambda: (qt_hi[:, i, :], qt_lo[:, i, :], b[:, 0:S]),
                    "k": lambda: (kt_hi[:, i, S:], kt_lo[:, i, S:], b[:, 0:S]),
                    "v": lambda: (v_hi[:, TB + i, :], v_lo[:, TB + i, :], b[:, :]),
                    "p": lambda: (pt_hi[:, 2 * i:2 * i + 2, :], pt_lo[:, 2 * i:2 * i + 2, :],
                                  b[:, :].rearrange("p (c n) -> p c n", c=2)),
                    "o": lambda: (ot_hi[:, i, :], ot_lo[:, i, :], b[:, 0:S])}[j[0]]()

        block = cx.enter_context(nc.Block())

        @block.sync
        def _(sp):
            chunks = lambda t: t.rearrange("(c p) n -> p c n", p=P)
            sp.dma_start(cin[:], batch_rows(ctx, 0)).then_inc(c_in, 16)
            sp.dma_start(raw[2][:], chunks(wv)).then_inc(w_in[2], 16)
            sp.dma_start(raw[3][:], chunks(wo)).then_inc(w_in[3], 16)
            sp.wait_ge(x1_out, 16 * (B - 1))
            sp.wait_ge(x1_last_out, 16)
            sp.dma_start(xr[:], batch_rows(x1, 0)).then_inc(xr_in, 16)
            sp.dma_start(wg_sb[:], chunks(wg)).then_inc(wg_in, 16)
            sp.wait_ge(xn_ready, TB)
            sp.dma_start(xin[:], batch_rows(x1, 1)).then_inc(x_in, 16)
            sp.wait_ge(c_split, 1)
            sp.wait_ge(job_done, done_at("C1", -1))
            sp.dma_start(cin[:], batch_rows(ctx, 1)).then_inc(c_in, 16)

            for i, n in enumerate("qkv"):
                sp.wait_ge(job_done, done_at(f"w{n}3", -1))
                sp.dma_start(stage[i][:], w[i].rearrange("(c p) h -> p c h", p=P)).then_inc(expert_in[i], 16)

            def batch(n, more, load):
                if load:
                    sp.wait_ge(xn_ready, (n + 2) * TB)
                    sp.dma_start(xin[:], batch_rows(x1, n + 2)).then_inc(x_in, 16)
                    sp.wait_ge(c_split, n + 2)
                    sp.wait_ge(job_done, done_at("C1", n))
                    sp.dma_start(cin[:], batch_rows(ctx, n + 2)).then_inc(c_in, 16)
                sp.wait_ge(job_ev, ev_at("y1", n))
                sp.dma_start(batch_rows(x2n[:, 0:D], n), x2_sb[:]).then_inc(x2_out, 16)
                if more:
                    sp.dma_start(xr[:], batch_rows(x1, n + 1)).then_inc(xr_in, 16)
                sp.wait_ge(xn3_ready, (n + 1) * TB)
                sp.dma_start(batch_rows(x2n[:, D:], n), xn3_sb[:]).then_inc(xn3_out, 16)

            batch(0, True, True)
            with sp.Fori(1, B - 2) as n:
                batch(n, True, True)
            batch(B - 2, True, False)
            batch(B - 1, False, False)

        @block.gpsimd
        def _(pool):
            nc.gpsimd.memset(expo[:], -0.5).then_inc(consts, 1)
            pool.wait_ge(consts, 1)

            def rstd_ln2(k):
                pool.wait_ge(ln_dve, k * 5 + 5)
                nc.gpsimd.tensor_tensor(rstd[:, 0, :], veps[:, 0, :], expo[:], ALU.pow).then_inc(ln_rstd, 1)

            def rstd_ln3(k):
                pool.wait_ge(ln3_dve, k * 5 + 5)
                nc.gpsimd.tensor_tensor(rstd[:, 1, :], veps[:, 1, :], expo[:], ALU.pow).then_inc(ln3_rstd, 1)

            rstd_ln2(0)
            rstd_ln2(1)
            with pool.Fori(0, B - 2) as n:
                rstd_ln3(n)
                rstd_ln2(n + 2)
            rstd_ln3(B - 2)
            rstd_ln3(B - 1)

        @block.scalar
        def _(act):
            def hi_part(j, n):
                act.wait_ge(job_done, done_at(j, n))
                hi, _, src = parts_of(j, n)
                nc.scalar.copy(hi, src).then_inc(job_hi, 1)

            def ctx_hi(k):
                act.wait_ge(c_in, 16 * (k + 1))
                nc.scalar.copy(v_hi[:, 0:TB, :], cin[:]).then_inc(c_hi, 1)

            for j in PROLOGUE:
                hi_part(j, -1)
                if j == "C1":
                    ctx_hi(0)

            def batch(n):
                for j in order(n):
                    if j[0] == "s":
                        q = int(j[1])
                        act.wait_ge(mx_done, n * TB + q + 1)
                        nc.scalar.activation(prob[:, q, :], bank(j, n)[:, :], ACT.Exp, scale=scale,
                                             bias=nmax[:, q:q + 1], accum_out=rsum[:, q:q + 1]).then_inc(ex_done, 1)
                    if j in hi_jobs(order(n)):
                        hi_part(j, n)
                    if j == "o3" and order(n) is ORDER:
                        ctx_hi(n + 1)

            batch(0)
            with act.Fori(1, B - 1) as n:
                batch(n)
            batch(B - 1)

        @block.tensor
        def _(pe):
            def wait_bank(j, n):
                if isinstance(n, int) and n < 0:
                    before, of = PROLOGUE.index(j) - RING, -1
                    if before < 0:
                        return
                    last = PROLOGUE[before]
                else:
                    before = order(n).index(j) - RING
                    if before >= 0:
                        last, of = order(n)[before], n
                    elif isinstance(n, int) and n == 0:
                        last, of = PROLOGUE[before], -1
                    else:
                        last, of = ORDER[before], n - 1
                if last[0] == "s":
                    pe.wait_ge(ex_done, of * TB + int(last[1]) + 1)
                else:
                    pe.wait_ge(job_ev, ev_at(last, of))

            def job(j, n):
                wait_bank(j, n)
                b, i = bank(j, n), int(j[-1])
                toks = slice(i * P, (i + 1) * P)
                rows = slice(i * P, (i + 1) * P)
                chunks = range(DC)
                if j[0] == "w":
                    if i == 0:
                        pe.wait_ge(w_in["qkvo".index(j[1])], 16)
                    for c in chunks:
                        m = nc.tensor.transpose(b[:, c * P:(c + 1) * P], raw["qkvo".index(j[1])][:, c, rows], ident[:])
                elif j[0] in "XCY":
                    if j == "X0":
                        pe.wait_ge(xn_ready, (n + 2) * TB)
                    if j == "C0":
                        pe.wait_ge(c_in, 16 * (n + 2))
                    if j[0] == "Y":
                        pe.wait_ge(xn3_ready, n * TB + i + 1)
                    src = {"X": xn, "C": cin, "Y": xn3_sb}[j[0]]
                    for c in chunks:
                        m = nc.tensor.transpose(b[:, c * P:(c + 1) * P], src[:, i, c * P:(c + 1) * P], ident[:])
                elif j[0] in "qk":
                    if j == "q0":
                        pe.wait_ge(job_ev, ev_at("X1", n))
                    if isinstance(n, int) and n < 0 and i == 0:
                        pe.wait_ge(job_ev, ev_at(f"w{j[0]}3", n))
                    m = three_pass(nc.tensor.matmul, b[:, 0:S],
                                   ([wt_hi[j[0]][:, c, rows] for c in chunks], [wt_lo[j[0]][:, c, rows] for c in chunks]),
                                   ([xt_hi[:, c, :] for c in chunks], [xt_lo[:, c, :] for c in chunks]))
                elif j[0] == "v":
                    if isinstance(n, int) and n < 0 and i == 0:
                        pe.wait_ge(job_ev, ev_at("wv3", n))
                    m = three_pass(nc.tensor.matmul, b[:, :],
                                   ([xt_hi[:, c, toks] for c in chunks], [xt_lo[:, c, toks] for c in chunks]),
                                   ([wt_hi["v"][:, c, :] for c in chunks], [wt_lo["v"][:, c, :] for c in chunks]))
                elif j[0] == "s":
                    if i == 0:
                        pe.wait_ge(job_ev, ev_at("k3", n - 1))
                    m = three_pass(nc.tensor.matmul, b[:, :],
                                   ([qt_hi[:, c, toks] for c in chunks], [qt_lo[:, c, toks] for c in chunks]),
                                   ([kt_hi[:, c, :] for c in chunks], [kt_lo[:, c, :] for c in chunks]))
                elif j[0] == "p":
                    pe.wait_ge(ex_done, (n + 1) * TB)
                    for k in range(2):
                        for q in range(TB):
                            m = nc.tensor.transpose(b[:, (k * TB + q) * P:(k * TB + q + 1) * P],
                                                    prob[:, q, (2 * i + k) * P:(2 * i + k + 1) * P], ident[:])
                elif j[0] == "o":
                    if i == 0:
                        pe.wait_ge(job_ev, ev_at("p1", n))
                        pe.wait_ge(c_split, n + 1)
                    keys = range(KC)
                    m = three_pass(nc.tensor.matmul, b[:, 0:S],
                                   ([v_hi[:, k, rows] for k in keys], [v_lo[:, k, rows] for k in keys]),
                                   ([pt_hi[:, k, :] for k in keys], [pt_lo[:, k, :] for k in keys]))
                elif j[0] == "y":
                    if i == 0:
                        pe.wait_ge(job_ev, ev_at("o3", n))
                    m = three_pass(nc.tensor.matmul, b[:, :],
                                   ([ot_hi[:, c, toks] for c in chunks], [ot_lo[:, c, toks] for c in chunks]),
                                   ([wt_hi["o"][:, c, :] for c in chunks], [wt_lo["o"][:, c, :] for c in chunks]))
                else:
                    if i == 0:
                        pe.wait_ge(job_ev, ev_at("Y1", n))
                    for c in chunks:
                        m = nc.tensor.matmul(b[:, 0:E], xt3[:, c, toks], wg_sb[:, c, :], start=c == 0, stop=c == DC - 1)
                m.then_inc(job_done, 1)

            for j in PROLOGUE:
                job(j, -1)
            pe.wait_ge(wg_in, 16)

            def batch(n):
                for j in order(n):
                    job(j, n)

            batch(0)
            with pe.Fori(1, B - 1) as n:
                batch(n)
            batch(B - 1)

        @block.vector
        def _(dve):
            def norm_stats(which, k, src, done):
                for t in range(TB):
                    nc.vector.bn_stats(stats[:, which, t, :], src[:, t, :]).then_inc(done, 1)
                for t in range(TB):
                    dve.wait_ge(done, k * 5 + 1 + t)
                    dve.sem_inc(tick, 1)
                    nc.vector.bn_aggr(mv[:, which, t, :], stats[:, which, t, :]).then_inc(done, 1)
                dve.wait_ge(done, k * 5 + 4)
                nc.vector.tensor_scalar(veps[:, which, :], mv[:, which, :, 1], EPS, None, ALU.add).then_inc(done, 1)

            def norm_apply(which, dst, src, ready):
                for t in range(TB):
                    nc.vector.tensor_scalar(dst[:, t, :], src[:, t, :], mv[:, which, t, 0:1], rstd[:, which, t:t + 1],
                                            ALU.subtract, ALU.mult).then_inc(ready, 1)

            def ln2_stats(k):
                if isinstance(k, int) and k == 0:
                    dve.wait_ge(x1_first_in, 16)
                else:
                    dve.wait_ge(x_in, k * 16)
                dve.sem_inc(tick, 1)
                norm_stats(0, k, xin, ln_dve)

            def ln2_apply(k):
                dve.wait_ge(ln_rstd, k + 1)
                norm_apply(0, xn, xin, xn_ready)

            def lo_part(j, n):
                dve.wait_ge(job_hi, hi_at(j, n))
                hi, lo, src = parts_of(j, n)
                nc.vector.tensor_tensor(lo, src, hi.bitcast(F32), ALU.subtract).then_inc(job_ev, 1)

            def ctx_lo(k):
                dve.wait_ge(c_hi, k + 1)
                nc.vector.tensor_tensor(v_lo[:, 0:TB, :], cin[:], v_hi[:, 0:TB, :].bitcast(F32),
                                        ALU.subtract).then_inc(c_split, 1)

            for j in PROLOGUE:
                lo_part(j, -1)
                if j == "wq0":
                    ln2_stats(0)
                if j == "wq2":
                    ln2_apply(0)
                if j == "C1":
                    ctx_lo(0)
                if j == "k1":
                    ln2_stats(1)
                if j == "k3":
                    ln2_apply(1)

            def batch(n):
                for j in order(n):
                    if j[0] == "s":
                        q = int(j[1])
                        dve.wait_ge(job_done, done_at(j, n))
                        dve.sem_inc(tick, 1)
                        nc.vector.tensor_reduce(smax[:, q:q + 1], bank(j, n)[:, :], AX.X, ALU.max).then_inc(max_done, 1)
                        dve.wait_ge(max_done, n * TB + q + 1)
                        nc.vector.tensor_scalar(nmax[:, q:q + 1], smax[:, q:q + 1], -scale, None, ALU.mult)\
                            .then_inc(mx_done, 1)
                    elif j[0] == "y":
                        i = int(j[1])
                        if i == 0:
                            dve.wait_ge(xr_in, 16 * (n + 1))
                            wait(dve, x2_out, 16 * n)
                            dve.wait_ge(rinv_done, n + 1)
                        dve.wait_ge(job_done, done_at(j, n))
                        nc.vector.scalar_tensor_tensor(x2_sb[:, i, :], bank(j, n)[:, :], rinv[:, i:i + 1], xr[:, i, :],
                                                       ALU.mult, ALU.add).then_inc(job_ev, 1)
                    elif j[0] == "Y":
                        dve.wait_ge(job_done, done_at(j, n))
                        nc.vector.tensor_copy(xt3[:, :, int(j[1]) * P:(int(j[1]) + 1) * P],
                                              bank(j, n)[:, :].rearrange("p (c n) -> p c n", c=DC)).then_inc(job_ev, 1)
                    elif j[0] == "l":
                        dve.wait_ge(job_done, done_at(j, n))
                        nc.vector.tensor_copy(logits[:, bass.ds(n * TB + int(j[1]), 1), :],
                                              bank(j, n)[:, 0:E].unsqueeze(1)).then_inc(job_ev, 1)
                    else:
                        lo_part(j, n)
                    if j == "o3" and order(n) is ORDER:
                        ctx_lo(n + 1)
                    if j == "p1":
                        nc.vector.reciprocal(rinv[:], rsum[:]).then_inc(rinv_done, 1)
                    if j == "y1":
                        dve.wait_ge(job_ev, ev_at("y1", n))
                        dve.sem_inc(tick, 1)
                        norm_stats(1, n, x2_sb, ln3_dve)
                    if j == ("k1" if order(n) is ORDER else "y1"):
                        wait(dve, xn3_out, 16 * n)
                        dve.wait_ge(ln3_rstd, n + 1)
                        norm_apply(1, xn3_sb, x2_sb, xn3_ready)
                    if j in ("k3", "v1") and (not isinstance(n, int) or n < B - 2):
                        (ln2_stats if j == "k3" else ln2_apply)(n + 2)

            batch(0)
            with dve.Fori(1, B - 2) as n:
                batch(n)
            batch(B - 2)
            batch(B - 1)


def mixture_of_experts(nc, ident, logits, x2n, x2n_out, w, bias, table, out, stage, expert_in):
    N = B * S
    BLOCKS = NT + E - 1
    AHEAD = 4
    BEHIND = 5
    RX = 6
    FIRST = 5
    YB = 3
    RING = 7
    W_JOBS = E * DC
    assert (BLOCKS - FIRST) % RX == 0 and RX % YB == 0 and FIRST > YB and RX > BEHIND
    assert STAGED * DC * D == RX * 2 * D and RX % STAGED == 0
    TABLE_PARTS = [(0, 4), (4, 12), (12, BLOCKS)]
    with ExitStack() as cx:
        sb = lambda n, s, d=F32: cx.enter_context(nc.sbuf_tensor("c_" + n, s, d))
        sem = lambda n: cx.enter_context(nc.semaphore("c_" + n))
        wt_hi, wt_lo = sb("wt_hi", [P, DC, E * D], F32R), sb("wt_lo", [P, DC, E * D], F32R)
        bias_sb = sb("bias", [P, E * D])
        xt_hi, xt_lo = sb("xt_hi", [P, 2, D], F32R), sb("xt_lo", [P, 2, D], F32R)
        y_sb = sb("y_sb", [P, YB, D])
        lmax, diff, eq = sb("lmax", [P, NT]), sb("diff", [P, NT, E]), sb("eq", [P, NT, E])
        ex, gsum = sb("ex", [P, NT, E]), sb("gsum", [P, NT])
        rank_i, rank = sb("rank_i", [P, E], I32), sb("rank", [P, E])
        best, onehot = sb("best", [P, NT]), sb("onehot", [P, NT, E], BF16)
        before, ones = sb("before", [P, P], BF16), sb("ones", [P, P], BF16)
        full_i, full = sb("full_i", [P, NT], I32), sb("full", [P, NT])
        upto = sb("upto", [P, E, E])
        block_i, block_no = sb("block_i", [P, BLOCKS], I32), sb("block_no", [P, BLOCKS])
        number = sb("number", [P, E])
        over, blocks = sb("over", [P, E, NT]), sb("blocks", [P, E])
        cum, end, start = sb("cum", [P, E, E]), sb("end", [P, E]), sb("start", [P, E])
        past, owner, owner_i = sb("past", [P, BLOCKS, E]), sb("owner", [P, BLOCKS]), sb("owner_i", [P, BLOCKS], I32)
        place, slot, slot_i = sb("place", [P, NT, E]), sb("slot", [P, NT]), sb("slot_i", [P, NT], U32)
        entry = sb("entry", [P, NT, 2], I32)
        unused = sb("unused", [P, BLOCKS, 2], I32)
        tab = sb("tab", [P, BLOCKS + AHEAD, 2], I32)
        gather_no, scatter_no = sb("gather_no", [P, RX, 1], U32), sb("scatter_no", [P, RX, 1], U32)
        route_ps = cx.enter_context(nc.psum_tensor("c_route", [P, 2, NT * E], F32))
        ring = [cx.enter_context(nc.psum_tensor(f"c_bank{i}", [P, D], F32)) for i in range(RING)]
        t_ps, y_ps = ring[0:2], ring[2:4]

        bias_in, init_in, entries_in = sem("bias_in"), sem("init_in"), sem("entries_in")
        w_in = expert_in
        rows_in, out_done = [sem(f"rows_in{i}") for i in range(RX)], [sem(f"out_done{i}") for i in range(RX)]
        tab_in = [sem(f"tab_in{i}") for i in range(len(TABLE_PARTS))]
        consts, route, diff_done, ex_done = sem("consts"), sem("route"), sem("diff_done"), sem("ex_done")
        onehot_done, ranks_done, entry_done, slot_done = sem("onehot_done"), sem("ranks_done"), sem("entry_done"), sem("slot_done")
        owner_done, tick_pool = sem("owner_done"), sem("tick_pool")
        w_done, w_hi_done, w_split = sem("w_done"), sem("w_hi_done"), sem("w_split")
        gather_no_done, scatter_no_done = sem("gather_no_done"), sem("scatter_no_done")
        t_done, xt_hi_done, xt_done = sem("t_done"), sem("xt_hi_done"), sem("xt_done")
        y_done, bias_done, fin_done = sem("y_done"), sem("bias_done"), sem("fin_done")
        block = cx.enter_context(nc.Block())
        CONSTS_INIT, CONSTS = 8, 13

        def rows(k, columns):
            place, part = divmod(k % RX, RX // STAGED)
            return stage[place][:].rearrange("p c n -> p (c n)")[:, part * 2 * D + columns.start:part * 2 * D + columns.stop]

        def blocks_loop(engine, step):
            for k in range(FIRST):
                step(0, k)
            with engine.Fori(0, (BLOCKS - FIRST) // RX) as i:
                for k in range(FIRST, FIRST + RX):
                    step(i, k)

        def number_of(i, k):
            return i * RX + k

        def turn(i, k):
            return i + k // RX

        def column(t, i, k, c):
            return t[:, k, c:c + 1] if isinstance(i, int) else t[:, bass.ds(i * RX + k, 1), c]

        @block.sync
        def _(sp):
            for e in range(E):
                if e >= STAGED:
                    sp.wait_ge(w_done, (e - STAGED + 1) * DC)
                    sp.dma_start(stage[e % STAGED][:], w[e].rearrange("(c p) h -> p c h", p=P)).then_inc(w_in[e % STAGED], 16)
                if e == 0:
                    sp.wait_ge(consts, CONSTS_INIT)
                    sp.dma_start(table.rearrange("(j p) c -> p j c", p=P), unused[:]).then_inc(init_in, 16)
                if e == 1:
                    sp.dma_start(bias_sb[:], bass.AP(tensor=bias.tensor, offset=bias.offset, ap=[[0, P], [1, E * D]]))\
                        .then_inc(bias_in, 16)
            sp.wait_ge(entries_in, 16 * NT)
            rows_of = table.rearrange("(j p) c -> p j c", p=P)
            for (a, b), s in zip(TABLE_PARTS, tab_in):
                sp.dma_start(tab[:, a:b, :], rows_of[:, a:b, :]).then_inc(s, 16)

        @block.gpsimd
        def _(pool):
            nc.gpsimd.memset(unused[:], 0).then_inc(consts, 1)
            pool.wait_ge(consts, 1)
            nc.gpsimd.iota(unused[:, :, 0], pattern=[[P, BLOCKS]], base=N, channel_multiplier=1).then_inc(consts, 1)
            nc.gpsimd.iota(rank_i[:], pattern=[[-1, E]], base=E, channel_multiplier=0).then_inc(consts, 1)
            nc.gpsimd.memset(before[:], 1.0).then_inc(consts, 1)
            nc.gpsimd.memset(ones[:], 1.0).then_inc(consts, 1)
            nc.gpsimd.memset(upto[:], 1.0).then_inc(consts, 1)
            nc.gpsimd.memset(tab[:, BLOCKS:, :], 0).then_inc(consts, 1)
            pool.wait_ge(consts, 7)
            nc.gpsimd.tensor_copy(rank[:], rank_i[:]).then_inc(consts, 1)
            nc.gpsimd.affine_select(out=before[:], in_=before[:], compare_op=ALU.is_gt, fill=0.0, base=0,
                                    pattern=[[1, P]], channel_multiplier=-1).then_inc(consts, 1)
            nc.gpsimd.affine_select(out=upto[:], in_=upto[:], compare_op=ALU.is_ge, fill=0.0, base=0,
                                    pattern=[[1, E], [-1, E]], channel_multiplier=0).then_inc(consts, 1)
            nc.gpsimd.iota(full_i[:], pattern=[[P, NT]], base=0, channel_multiplier=0).then_inc(consts, 1)
            nc.gpsimd.iota(block_i[:], pattern=[[1, BLOCKS]], base=0, channel_multiplier=0).then_inc(consts, 1)
            nc.gpsimd.iota(entry[:, :, 0], pattern=[[P, NT]], base=0, channel_multiplier=1).then_inc(consts, 1)
            pool.wait_ge(entry_done, 1)
            pool.wait_ge(consts, CONSTS)
            pool.wait_ge(slot_done, 1)
            pool.wait_ge(init_in, 16)
            for t in range(NT):
                pool.indirect_dma_start(table, bass.IndirectOffsetOnAxis(ap=slot_i[:, t:t + 1], axis=0),
                                        entry[:, t, :], None).then_inc(entries_in, 16)

            for s in x2n_out:
                pool.wait_ge(s, 16 * B)
            pool.wait_ge(w_done, W_JOBS)

            def gather(i, k):
                m = number_of(i, k)
                pool.wait_ge(gather_no_done, m + 1)
                pool.sem_inc(tick_pool, 1)
                pool.indirect_dma_start(rows(k, slice(0, 2 * D)), None, x2n,
                                        bass.IndirectOffsetOnAxis(ap=gather_no[:, k % RX, :], axis=0),
                                        bounds_check=N - 1, oob_is_err=False).then_inc(rows_in[k % RX], 16)

            def scatter(i, k):
                m = number_of(i, k)
                pool.wait_ge(fin_done, m + 1)
                pool.wait_ge(scatter_no_done, m + 1)
                pool.sem_inc(tick_pool, 1)
                pool.indirect_dma_start(out, bass.IndirectOffsetOnAxis(ap=scatter_no[:, k % RX, :], axis=0),
                                        y_sb[:, k % YB, :], None, bounds_check=N - 1, oob_is_err=False)\
                    .then_inc(out_done[k % RX], 16)

            def step(i, k):
                gather(i, k)
                if k >= BEHIND:
                    scatter(i, k - BEHIND)

            blocks_loop(pool, step)
            for m in range(BLOCKS - BEHIND, BLOCKS):
                scatter(0, m)
            for k in range(BLOCKS - RX, BLOCKS):
                pool.wait_ge(out_done[k % RX], 16 * (turn(0, k) + 1))

        @block.scalar
        def _(act):
            act.wait_ge(diff_done, 1)
            nc.scalar.activation(ex[:], diff[:], ACT.Exp).then_inc(ex_done, 1)
            for e in range(E):
                for c in range(DC):
                    i = e * DC + c
                    act.wait_ge(w_done, i + 1)
                    nc.scalar.copy(wt_hi[:, c, e * D:(e + 1) * D], ring[i % RING][:, :]).then_inc(w_hi_done, 1)

            def gather_numbers(i, k):
                m = number_of(i, k)
                nc.scalar.copy(gather_no[:, k % RX, :], column(tab, i, k, 0)).then_inc(gather_no_done, 1)

            def scatter_numbers(i, k):
                nc.scalar.copy(scatter_no[:, k % RX, :], column(tab, i, k, 0)).then_inc(scatter_no_done, 1)

            for s in tab_in:
                act.wait_ge(s, 16)
            act.wait_ge(consts, CONSTS)
            for m in range(AHEAD):
                gather_numbers(0, m)

            def step(i, k):
                m = number_of(i, k)
                act.wait_ge(t_done, m + 1)
                nc.scalar.copy(xt_hi[:, k % 2, :], t_ps[k % 2][:, :]).then_inc(xt_hi_done, 1)
                gather_numbers(i, k + AHEAD)
                if k >= 1:
                    scatter_numbers(i, k - 1)

            blocks_loop(act, step)
            scatter_numbers(0, BLOCKS - 1)

        @block.tensor
        def _(pe):
            def w_job(i):
                e, c = divmod(i, DC)
                if c == 0:
                    pe.wait_ge(w_in[e % STAGED], 16 * (e // STAGED + 1))
                if i >= RING:
                    pe.wait_ge(w_split, i - RING + 1)
                for o in range(DC):
                    m = nc.tensor.transpose(ring[i % RING][:, o * P:(o + 1) * P],
                                            stage[e % STAGED][:, o, c * P:(c + 1) * P], ident[:])
                m.then_inc(w_done, 1)

            for i in range(DC):
                w_job(i)
            pe.wait_ge(consts, CONSTS)
            pe.wait_ge(onehot_done, 1)
            flat = onehot[:].rearrange("p t e -> p (t e)")
            nc.tensor.matmul(route_ps[:, 0, :], before[:], flat, start=True, stop=False)
            for t in range(NT - 1):
                nc.tensor.matmul(route_ps[:, 0, (t + 1) * E:], ones[:],
                                 free_ap(onehot[:], t * E, [[0, NT - 1 - t], [1, E]]), start=False, stop=t == NT - 2)
            nc.tensor.matmul(route_ps[:, 1, :], ones[:], flat, start=True, stop=True).then_inc(ranks_done, 1)
            for i in range(DC, W_JOBS):
                w_job(i)
            pe.wait_ge(owner_done, 1)
            pe.wait_ge(w_split, W_JOBS)

            def transposes(i, k):
                m = number_of(i, k)
                pe.wait_ge(rows_in[k % RX], (turn(i, k) + 1) * 16)
                if k >= 2:
                    pe.wait_ge(xt_done, m - 1)
                for c in range(DC):
                    t = nc.tensor.transpose(t_ps[k % 2][:, c * P:(c + 1) * P],
                                            rows(k, slice(D + c * P, D + (c + 1) * P)), ident[:])
                t.then_inc(t_done, 1)

            def product(i, k):
                m = number_of(i, k)
                e = pe.value_load(owner_i[0:1, bass.ds(m, 1)] if not isinstance(m, int) else owner_i[0:1, m:m + 1],
                                  min_val=0, max_val=E - 1)
                pe.wait_ge(xt_done, m + 1)
                if k >= 2:
                    pe.wait_ge(bias_done, m - 1)
                y = three_pass(nc.tensor.matmul, y_ps[k % 2][:, :],
                               ([xt_hi[:, k % 2, c * P:(c + 1) * P] for c in range(DC)],
                                [xt_lo[:, k % 2, c * P:(c + 1) * P] for c in range(DC)]),
                               ([wt_hi[:, c, bass.ds(e * D, D)] for c in range(DC)],
                                [wt_lo[:, c, bass.ds(e * D, D)] for c in range(DC)]))
                y.then_inc(y_done, 1)

            def step(i, k):
                transposes(i, k)
                if k >= 1:
                    product(i, k - 1)

            blocks_loop(pe, step)
            product(0, BLOCKS - 1)

        @block.vector
        def _(dve):
            over_e = lambda t: free_ap(t, 0, [[1, NT], [0, E]])
            over_t = lambda t: free_ap(t, 0, [[0, NT], [1, E]])
            steps = [0]

            def then(instruction):
                steps[0] += 1
                instruction.then_inc(route, 1)
                dve.wait_ge(route, steps[0])

            then(nc.vector.tensor_reduce(lmax[:], logits[:], AX.X, ALU.max))
            nc.vector.tensor_tensor(diff[:], logits[:], over_e(lmax[:]), ALU.subtract).then_inc(diff_done, 1)
            then(nc.vector.tensor_tensor(eq[:], logits[:], over_e(lmax[:]), ALU.is_equal))
            dve.wait_ge(consts, CONSTS)
            then(nc.vector.tensor_tensor(eq[:], eq[:], over_t(rank[:]), ALU.mult))
            then(nc.vector.tensor_reduce(best[:], eq[:], AX.X, ALU.max))
            nc.vector.tensor_tensor(onehot[:], eq[:], over_e(best[:]), ALU.is_equal).then_inc(onehot_done, 1)
            dve.wait_ge(ex_done, 1)
            then(nc.vector.tensor_reduce(gsum[:], ex[:], AX.X, ALU.add))
            nc.vector.reciprocal(entry[:, :, 1].bitcast(F32), gsum[:]).then_inc(entry_done, 1)
            nc.vector.tensor_copy(full[:], full_i[:]).then_inc(route, 1)
            then(nc.vector.tensor_copy(block_no[:], block_i[:]))
            steps[0] += 1
            dve.wait_ge(ranks_done, 1)
            then(nc.vector.tensor_reduce(number[:], free_ap(route_ps[:, 1, :], 0, [[1, E], [E, NT]]), AX.X, ALU.add))
            then(nc.vector.tensor_tensor(over[:], free_ap(number[:], 0, [[1, E], [0, NT]]),
                                         free_ap(full[:], 0, [[0, E], [1, NT]]), ALU.is_gt))
            then(nc.vector.tensor_reduce(blocks[:], over[:], AX.X, ALU.add))
            then(nc.vector.tensor_tensor(cum[:], upto[:], free_ap(blocks[:], 0, [[0, E], [1, E]]), ALU.mult))
            then(nc.vector.tensor_reduce(end[:], cum[:], AX.X, ALU.add))
            then(nc.vector.tensor_tensor(start[:], end[:], blocks[:], ALU.subtract))
            then(nc.vector.tensor_scalar(start[:], start[:], float(P), None, ALU.mult))
            then(nc.vector.tensor_tensor(place[:], route_ps[:, 0, :].rearrange("p (t e) -> p t e", e=E),
                                         over_t(start[:]), ALU.add))
            then(nc.vector.tensor_tensor(place[:], place[:], onehot[:], ALU.mult))
            then(nc.vector.tensor_reduce(slot[:], place[:], AX.X, ALU.add))
            nc.vector.tensor_copy(slot_i[:], slot[:]).then_inc(slot_done, 1)
            then(nc.vector.tensor_tensor(past[:], free_ap(end[:], 0, [[0, BLOCKS], [1, E]]),
                                         free_ap(block_no[:], 0, [[1, BLOCKS], [0, E]]), ALU.is_le))
            then(nc.vector.tensor_reduce(owner[:], past[:], AX.X, ALU.add))
            nc.vector.tensor_scalar(owner_i[:], owner[:], float(E - 1), None, ALU.min).then_inc(owner_done, 1)

            for i in range(W_JOBS):
                e, c = divmod(i, DC)
                dve.wait_ge(w_hi_done, i + 1)
                nc.vector.tensor_tensor(wt_lo[:, c, e * D:(e + 1) * D], ring[i % RING][:, :],
                                        wt_hi[:, c, e * D:(e + 1) * D].bitcast(F32), ALU.subtract).then_inc(w_split, 1)
            dve.wait_ge(bias_in, 16)
            dve.wait_ge(owner_done, 1)

            def finish(i, k):
                m = number_of(i, k)
                e = dve.value_load(owner_i[0:1, bass.ds(m, 1)] if not isinstance(m, int) else owner_i[0:1, m:m + 1],
                                   min_val=0, max_val=E - 1)
                if k >= YB:
                    dve.wait_ge(out_done[(k - YB) % RX], (turn(i, k - YB) + 1) * 16)
                dve.wait_ge(y_done, m + 1)
                nc.vector.tensor_tensor(y_sb[:, k % YB, :], y_ps[k % 2][:, :], bias_sb[:, bass.ds(e * D, D)], ALU.add)\
                    .then_inc(bias_done, 1)
                dve.wait_ge(bias_done, m + 1)
                gate = column(tab, i, k, 1).bitcast(F32)
                nc.vector.scalar_tensor_tensor(y_sb[:, k % YB, :], y_sb[:, k % YB, :], gate, rows(k, slice(0, D)),
                                               ALU.mult, ALU.add).then_inc(fin_done, 1)

            def step(i, k):
                m = number_of(i, k)
                dve.wait_ge(xt_hi_done, m + 1)
                nc.vector.tensor_tensor(xt_lo[:, k % 2, :], t_ps[k % 2][:, :], xt_hi[:, k % 2, :].bitcast(F32),
                                        ALU.subtract).then_inc(xt_done, 1)
                if k >= 1:
                    finish(i, k - 1)

            blocks_loop(dve, step)
            finish(0, BLOCKS - 1)


def program(nc, x, ctx, w_qkv, w_out, wq, wk, wv, wo, wg, w, bias, out):
    with ExitStack() as cx:
        ident = cx.enter_context(nc.sbuf_tensor("ident", [P, P], F32))
        logits = cx.enter_context(nc.sbuf_tensor("logits", [P, NT, E], F32))
        x1 = nc.dram_tensor("x1", [B * S, D], F32).ap()
        x2n = nc.dram_tensor("x2n", [B * S, 2 * D], F32).ap()
        table = nc.dram_tensor("slots", [P * (NT + E - 1), 2], I32).ap()
        stage_tensor = lambda i: cx.enter_context(nc.sbuf_tensor(f"stage{i}", [P, DC, D], F32))
        stage = [stage_tensor(0), stage_tensor(1)]
        sem = lambda n: cx.enter_context(nc.semaphore(n))
        x1_out, x1_last_out, x2n_out = sem("x1_out"), sem("x1_last_out"), (sem("x2_out"), sem("xn3_out"))
        rows_tensor = lambda n: cx.enter_context(nc.sbuf_tensor(n, [P, TB, D], F32))
        xin, xr = rows_tensor("xin"), rows_tensor("xr")
        x1_first_in = sem("x1_first_in")
        stage_in = [cx.enter_context(nc.semaphore(f"stage_in{i}")) for i in range(STAGED)]
        expert_in = [cx.enter_context(nc.semaphore(f"expert_in{i}")) for i in range(STAGED)]
        self_attention(nc, ident, x, w_qkv, w_out, x1, xin, xr, x1_out, x1_last_out, x1_first_in,
                       stage, stage_in, (wq, wk))
        stage += [stage_tensor(2)]
        x2_sb, xn3_sb = rows_tensor("x2_sb"), rows_tensor("xn3_sb")
        cross_attention(nc, ident, logits, x1, x1_out, x1_last_out, x1_first_in, ctx, wv, wo, wg, x2n, x2n_out, xin, xr, x2_sb,
                        xn3_sb, stage, stage_in, w, expert_in)
        mixture_of_experts(nc, ident, logits, x2n, x2n_out, w, bias, table, out, stage, expert_in)


def kernel(x, ctx_2048, mask_BxSx4224_bf0, L0_attn_w_qkv, L0_attn_w_out, L0_xattn_wq, L0_xattn_wk, L0_xattn_wv,
           L0_xattn_wo, L0_ffn_wg, L0_ffn_W, L0_ffn_b):
    import concourse.bacc as bacc
    import numpy as np
    from concourse.bass_utils import run_bass_kernel_spmd

    rows = lambda t: np.ascontiguousarray(np.asarray(t).reshape(B * S, D))
    arrays = {"x": rows(x), "ctx": rows(ctx_2048), "w_qkv": L0_attn_w_qkv, "w_out": L0_attn_w_out, "wq": L0_xattn_wq,
              "wk": L0_xattn_wk, "wv": L0_xattn_wv, "wo": L0_xattn_wo, "wg": L0_ffn_wg, "w": L0_ffn_W,
              "bias": L0_ffn_b}
    arrays = {f"in_{n}": np.ascontiguousarray(a) for n, a in arrays.items()}
    nc = bacc.Bacc("TRN2", target_bir_lowering=False, num_devices=1)
    args = [nc.dram_tensor(n, a.shape, mybir.dt.from_np(a.dtype), kind="ExternalInput").ap()
            for n, a in arrays.items()]
    out = nc.dram_tensor("result", [B * S, D], F32, kind="ExternalOutput").ap()
    program(nc, *args, out)
    r = run_bass_kernel_spmd(nc, [arrays], core_ids=[0])
    return r.results[0]["result"].reshape(B, S, D)
```

```python
from contextlib import ExitStack

import concourse.bass as bass
from concourse import mybir

F32 = mybir.dt.float32
F32R = mybir.dt.float32r
BF16 = mybir.dt.bfloat16
I32 = mybir.dt.int32
U32 = mybir.dt.uint32
ALU = mybir.AluOpType
ACT = mybir.ActivationFunctionType
AX = mybir.AxisListType

P = 128
B, S, D = 8, 256, 512
DC = D // P
TB = S // P
NT = B * TB
H, HD = 16, 32
HG = P // HD
G = H // HG
E = 8
STAGED = 3
EPS = 1e-5
NEG = -1e10
BIG = 3e38


def free_ap(ap, offset, dims):
    return bass.AP(tensor=ap.tensor, offset=ap.offset + offset, ap=[list(ap.ap[0])] + dims)


def wait(engine, semaphore, value):
    if not isinstance(value, int) or value > 0:
        engine.wait_ge(semaphore, value)


def batch_rows(tensor, b):
    rows = tensor[b * S:(b + 1) * S, :] if isinstance(b, int) else tensor[bass.ds(b * S, S), :]
    return rows.rearrange("(t p) n -> p t n", p=P)


def three_pass(pe_matmul, out, lhs, rhs, first=True, last=True):
    (lh, ll), (rh, rl) = lhs, rhs
    steps = [(a, b) for a, b in zip(lh, rh)] + [(a, b) for a, b in zip(lh, rl)] + [(a, b) for a, b in zip(ll, rh)]
    for i, (a, b) in enumerate(steps):
        ins = pe_matmul(out, a, b, start=first and i == 0, stop=last and i == len(steps) - 1)
    return ins



def self_attention(nc, ident, x, w_qkv, w_out, x1, xin, xr, x1_out, x1_last_out, x1_first_in,
                   stage, stage_in, next_weights):
    scale = float(HD) ** -0.5
    GH = G // 2
    HEAD_IN = 16 * 3
    NPROB, NPT = 4, 4
    STRIP = 352
    V_AT = {0: 0, 3: 128, 1: 192, 2: 288}
    with ExitStack() as cx:
        sb = lambda n, s, d=F32: cx.enter_context(nc.sbuf_tensor(n, s, d))
        ps = lambda n, s: cx.enter_context(nc.psum_tensor(n, s, F32))
        sem = lambda n: cx.enter_context(nc.semaphore(n))
        w_hi, w_lo = sb("wqkv_hi", [P, DC, 3 * D], F32R), sb("wqkv_lo", [P, DC, 3 * D], F32R)
        wo_hi, wo_lo = sb("wout_hi", [P, DC, D], F32R), sb("wout_lo", [P, DC, D], F32R)
        stats, mv = sb("a_stats", [P, TB, 6]), sb("a_mv", [P, TB, 2])
        veps, rstd, expo = sb("a_veps", [P, TB]), sb("a_rstd", [P, TB]), sb("a_expo", [P, TB])
        xn = sb("a_xn", [P, TB, D])
        xt_hi, xt_lo = sb("a_xt_hi", [P, DC, S], F32R), sb("a_xt_lo", [P, DC, S], F32R)
        qk = sb("qk", [P, 2, 4, GH, S], F32R)
        v_hi, v_lo = sb("v_hi", [P, TB, G * STRIP], F32R), sb("v_lo", [P, TB, G * STRIP], F32R)
        mask = sb("mask", [P, 2 * P])
        nmax = sb("nmax", [P, H, TB])
        prob = sb("prob", [P, NPROB, 3 * P])
        rsum, rinv8 = sb("rsum", [P, G, TB, HG]), sb("rinv8", [P, G, TB, HG])
        rinv = sb("rinv", [P, TB, HG, HD])
        r_sb = o_sb = rinv[:].rearrange("p q j d -> p (q j d)")
        pt_hi, pt_lo = sb("pt_hi", [P, NPT, 4 * P], F32R), sb("pt_lo", [P, NPT, 4 * P], F32R)
        ot_hi, ot_lo = sb("ot_hi", [P, G, S], F32R), sb("ot_lo", [P, G, S], F32R)
        with ExitStack() as early:
            raw = early.enter_context(nc.sbuf_tensor("a_raw", [P, 4, DC, D], F32))
        stack = sb("stack", [3 * HD, 2, HG, 2, GH, S], F32R)
        job_ps = [ps(f"a_job{i}", [P, D]) for i in range(2)]
        s_ps = [ps(f"a_s{i}", [P, TB, S]) for i in range(2)]
        t_ps = [ps(f"a_t{i}", [P, 4 * P]) for i in range(2)]
        o_ps = [ps(f"a_o{i}", [P, 2, S]) for i in range(2)]

        x0_in, x_in, xr_in = sem("a_x0_in"), sem("a_x_in"), sem("a_xr_in")
        w_in = [sem(f"a_w_in{i}") for i in range(4)]
        consts, tick, tick_sp = sem("a_consts"), sem("a_tick"), sem("a_tick_sp")
        w_split_hi, w_split, wo_split = sem("w_split_hi"), sem("w_split"), sem("wo_split")
        ln_dve, ln_rstd, xn_ready = sem("a_ln_dve"), sem("a_ln_rstd"), sem("a_xn_ready")
        job_done, job_hi, job_ev = sem("a_job_done"), sem("a_job_hi"), sem("a_job_ev")
        stacked = [[sem(f"stacked_{half}_{j}") for j in range(HG)] for half in range(2)]
        s_done, mx_done, ex_done = sem("s_done"), sem("mx_done"), sem("ex_done")
        rinv8_done, rinv_done, t_done = sem("rinv8_done"), sem("rinv_done"), sem("t_done")
        pt_hi_done, pt_done = sem("pt_hi_done"), sem("pt_done")
        av_done, r_done, rs_done = sem("av_done"), sem("r_done"), sem("rs_done")
        on_done, ot_hi_done, ot_done = sem("on_done"), sem("ot_hi_done"), sem("ot_done")

        SLOTS = {0: ["q3"], 2: ["k3"], 4: ["w0"], 5: ["w1", "X0"], 6: ["X1"], 7: ["y0"], 8: ["y1"], 9: ["q0"], 10: ["k0"],
                 11: ["q1", "k1"], 12: ["u0"], 13: ["u1"], 14: ["q2"], 15: ["k2"]}
        OWN, LATE = ("q3", "k3", "w0", "w1"), ("y0", "y1")
        ORDER = [j for s in sorted(SLOTS) for j in SLOTS[s]]
        PROLOGUE = ["X0", "X1", "q0", "k0", "q1", "k1", "q2", "k2", "u0", "u1"]
        assert sorted(PROLOGUE) == sorted(j for j in ORDER if j not in OWN + LATE)
        JOBS, HI_JOBS = len(ORDER), len(ORDER) - len(LATE)
        assert JOBS % 2 == 0
        T_LAG, LO_LAG, RINV_LAG, AV_LAG, R_LAG, ON_LAG, OT_LAG = 2, 3, 3, 4, 5, 6, 7
        LO_JOB_LAG = 1
        EPILOGUE_SLOTS = 10
        SPLIT_AT = {"X0": 0, "q0": 1, "q2": 2}

        def w_part(w, i):
            return w[:, :, i * D:(i + 1) * D]

        def has(j, n):
            if not isinstance(n, int):
                return True
            return n >= 1 if j in LATE else n < B if j in OWN else n < B - 1

        def number(j, n):
            return [i for i in ORDER if has(i, n)].index(j)

        def job_at(j, n):
            if not isinstance(n, int):
                return len(PROLOGUE) - len(LATE) + n * JOBS + number(j, n)
            if n < 0:
                return PROLOGUE.index(j)
            return len(PROLOGUE) + sum(has(i, m) for m in range(n) for i in ORDER) + number(j, n)

        def hi_at(j, n):
            if isinstance(n, int) and n < 0:
                return PROLOGUE.index(j)
            order = [i for i in ORDER if has(i, n) and i not in LATE]
            return len(PROLOGUE) + n * HI_JOBS + order.index(j)

        def bank(j, n):
            return job_ps[(job_at(j, n) if isinstance(n, int) else len(PROLOGUE) - len(LATE) + number(j, n)) % 2]

        def jobs_of(slot, n):
            return [j for j in SLOTS.get(slot, []) if has(j, n)]

        def head_at(slot, lag, n):
            t = slot - lag
            if isinstance(n, int) and (n < 1 if t < 0 else n >= B):
                return None
            return t % H if t < H else None

        def group_at(slot, lag, n):
            a = head_at(slot, lag, n)
            return a // HG if a is not None and a % HG == HG - 1 else None

        def groups_before(slot, lag, n):
            return n * G + (slot - lag) // HG

        def pe_job(j, n, tensor=nc.tensor):
            b, i = bank(j, n), int(j[1])
            toks = slice(i * P, (i + 1) * P)
            chunks = range(DC)
            if j[0] == "X":
                for c in chunks:
                    m = tensor.transpose(b[:, c * P:(c + 1) * P], xn[:, i, c * P:(c + 1) * P], ident[:])
            elif j[0] in "uw":
                o = 2 * D + (0 if j[0] == "u" else D // 2)
                cols = slice(o, o + D // 2)
                m = three_pass(tensor.matmul, b[:, 0:D // 2],
                               ([xt_hi[:, c, toks] for c in chunks], [xt_lo[:, c, toks] for c in chunks]),
                               ([w_hi[:, c, cols] for c in chunks], [w_lo[:, c, cols] for c in chunks]))
            elif j[0] == "y":
                m = three_pass(tensor.matmul, b[:, :],
                               ([ot_hi[:, c, toks] for c in chunks], [ot_lo[:, c, toks] for c in chunks]),
                               ([wo_hi[:, c, :] for c in chunks], [wo_lo[:, c, :] for c in chunks]))
            else:
                o = (0 if j[0] == "q" else D) + i * P
                m = three_pass(tensor.matmul, b[:, 0:S],
                               ([w_hi[:, c, o:o + P] for c in chunks], [w_lo[:, c, o:o + P] for c in chunks]),
                               ([xt_hi[:, c, :] for c in chunks], [xt_lo[:, c, :] for c in chunks]))
            m.then_inc(job_done, 1)

        def parts_of(j, n):
            b, i = bank(j, n), int(j[1])
            if j[0] == "X":
                cols = slice(i * P, (i + 1) * P)
                return [(xt_hi[:, :, cols], xt_lo[:, :, cols], b[:, :].rearrange("p (c n) -> p c n", c=DC))]
            if j[0] in "uw":
                first = 0 if j[0] == "u" else GH * STRIP
                out = []
                for a, z in ((0, 3), (1, 2)):
                    dst = [[STRIP, GH], [V_AT[z] - V_AT[a], 2], [1, HD]]
                    out.append((free_ap(v_hi[:, i, :], first + V_AT[a], dst), free_ap(v_lo[:, i, :], first + V_AT[a], dst),
                                free_ap(b[:, :], a * HD, [[P, GH], [(z - a) * HD, 2], [1, HD]])))
                return out
            w = 0 if j[0] == "q" else 2
            at = lambda part: qk[:, i // GH, w + part, i % GH, :]
            return [(at(0), at(1), b[:, 0:S])]

        block = cx.enter_context(nc.Block())

        @block.sync
        def _(sp):
            sp.dma_start(xin[:], batch_rows(x, 0)).then_inc(x0_in, 16)
            for i, w in enumerate([w_qkv[:, j * D:(j + 1) * D] for j in range(3)] + [w_out]):
                sp.dma_start(raw[:, i, :, :], w.rearrange("(c p) n -> p c n", p=P)).then_inc(w_in[i], 16)
            for i, w in enumerate(next_weights):
                sp.dma_start(stage[i][:], w.rearrange("(c p) n -> p c n", p=P)).then_inc(stage_in[i], 16)

            def stack_half(half):
                for j in range(HG):
                    for r, parts in enumerate((slice(0, 3, 2), slice(1, 3), slice(0, 4, 3))):
                        dst = stack[HD * r:HD * (r + 1), half, j, :, :, :].bitcast(F32)
                        src = qk[HD * j:HD * (j + 1), half, parts, :, :].bitcast(F32)
                        sp.dma_start(dst.rearrange("p w g s -> p w (g s)"),
                                     src.rearrange("p w g s -> p w (g s)")).then_inc(stacked[half][j], 16)

            def batch(n):
                wait(sp, job_ev, job_at("k3", n) + 1)
                sp.sem_inc(tick_sp, 1)
                if isinstance(n, int) and n == 0:
                    sp.wait_ge(w_split, 3)
                    sp.wait_ge(wo_split, 2)
                wait(sp, s_done, n * H)
                stack_half(1)
                if has("k1", n):
                    wait(sp, job_ev, job_at("k1", n) + 1)
                    sp.sem_inc(tick_sp, 1)
                    wait(sp, s_done, n * H + H // 2)
                    stack_half(0)

            wait(sp, job_ev, job_at("k1", -1) + 1)
            sp.wait_ge(w_split, 2)
            stack_half(0)
            batch(0)
            with sp.Fori(1, B - 1) as n:
                batch(n)
            batch(B - 1)
            sp.wait_ge(job_ev, job_at("y1", B) + 1)
            sp.dma_start(batch_rows(x1, B - 1), xr[:]).then_inc(x1_last_out, 16)

        @block.gpsimd
        def _(pool):
            nc.gpsimd.memset(ident[:], 0.0).then_inc(consts, 1)
            nc.gpsimd.memset(mask[:], 0.0).then_inc(consts, 1)
            nc.gpsimd.memset(expo[:], -0.5).then_inc(consts, 1)
            pool.wait_ge(consts, 3)
            nc.gpsimd.affine_select(out=ident[:], in_=ident[:], compare_op=ALU.not_equal, fill=1.0, base=0,
                                    pattern=[[-1, P]], channel_multiplier=1).then_inc(consts, 1)
            nc.gpsimd.affine_select(out=mask[:, P:], in_=mask[:, P:], compare_op=ALU.is_ge, fill=NEG, base=0,
                                    pattern=[[-1, P]], channel_multiplier=1).then_inc(consts, 1)

            def rstd_and_next(k, after):
                pool.wait_ge(ln_dve, k * 5 + 5)
                nc.gpsimd.tensor_tensor(rstd[:], veps[:], expo[:], ALU.pow).then_inc(ln_rstd, 1)
                if after:
                    pool.wait_ge(xn_ready, k * TB + TB)
                    pool.dma_start(xin[:], batch_rows(x, k + 1)).then_inc(x_in, 16)

            def store(k):
                pool.wait_ge(job_ev, job_at("y1", k + 1) + 1)
                pool.dma_start(batch_rows(x1, k), xr[:]).then_inc(x1_out, 16)
                pool.wait_ge(x1_out, k * 16 + 16)
                pool.dma_start(xr[:], batch_rows(x, k + 1)).then_inc(xr_in, 16)

            rstd_and_next(0, True)
            pool.dma_start(xr[:], batch_rows(x, 0)).then_inc(xr_in, 16)
            for t in (pt_hi, pt_lo):
                nc.gpsimd.memset(t[:, :, 0:P].bitcast(F32), 0.0).then_inc(consts, 1)
            for t in (v_hi, v_lo):
                nc.gpsimd.memset(t[:].bitcast(F32), 0.0).then_inc(consts, 1)
            pool.wait_ge(w_in[3], 16)
            nc.gpsimd.tensor_copy(wo_hi[:], raw[:, 3, :, :]).then_inc(wo_split, 1)
            pool.wait_ge(wo_split, 1)
            nc.gpsimd.tensor_tensor(wo_lo[:], raw[:, 3, :, :], wo_hi[:].bitcast(F32), ALU.subtract).then_inc(wo_split, 1)
            rstd_and_next(1, True)
            with pool.Fori(1, B - 2) as n:
                rstd_and_next(n + 1, True)
                store(n - 1)
            rstd_and_next(B - 1, False)
            pool.wait_ge(xn_ready, B * TB)
            pool.wait_ge(x1_out, 16)
            pool.dma_start(xin[:], batch_rows(x1, 0)).then_inc(x1_first_in, 16)
            store(B - 3)
            store(B - 2)

        CONSTS = 9

        @block.scalar
        def _(act):
            def evac(j, n):
                act.wait_ge(job_done, job_at(j, n) + 1)
                if j in ("q0", "q2"):
                    for s in stacked["q0 q2".split().index(j)]:
                        wait(act, s, (n + 1) * HEAD_IN)
                if j == "u0":
                    wait(act, av_done, n * H + H // 2 if not isinstance(n, int) or n >= 0 else 0)
                if j == "w0":
                    wait(act, av_done, n * H)
                pieces = parts_of(j, n)
                for i, (hi, _, src) in enumerate(pieces):
                    e = nc.scalar.copy(hi, src)
                e.then_inc(job_hi, 1)

            for j in PROLOGUE:
                if j in SPLIT_AT:
                    i = SPLIT_AT[j]
                    act.wait_ge(w_in[i], 16)
                    nc.scalar.copy(w_part(w_hi, i), raw[:, i, :, :]).then_inc(w_split_hi, 1)
                if j == "u0":
                    act.wait_ge(consts, CONSTS)
                evac(j, -1)

            def slot(n, h):
                e = head_at(h, 0, n)
                if e is not None:
                    g, j = divmod(e, HG)
                    act.wait_ge(mx_done, n * H + h + 1)
                    for q, cols in ((0, slice(0, P)), (1, slice(P, 3 * P))):
                        a = nc.scalar.activation(prob[:, e % NPROB, cols], prob[:, e % NPROB, cols], ACT.Exp, scale=-1.0,
                                                 bias=nmax[:, e, q:q + 1], accum_out=rsum[:, g, q, j:j + 1])
                    a.then_inc(ex_done, 1)
                for j in jobs_of(h, n):
                    if j not in LATE:
                        evac(j, n)
                t = head_at(h, T_LAG, n)
                if t is not None:
                    act.wait_ge(t_done, n * H + h - T_LAG + 1)
                    wait(act, av_done, n * H + h - T_LAG + 1 - NPT)
                    nc.scalar.copy(pt_hi[:, t % NPT, P:], t_ps[t % 2][:, P:]).then_inc(pt_hi_done, 1)
                g = group_at(h, R_LAG, n)
                if g is not None:
                    act.wait_ge(r_done, groups_before(h, R_LAG, n) + 1)
                    nc.scalar.copy(r_sb, o_ps[g % 2][:, 1, :]).then_inc(rs_done, 1)
                g = group_at(h, ON_LAG, n)
                if g is not None:
                    if g == 0 and not (isinstance(n, int) and n < 1):
                        act.wait_ge(job_done, job_at("y1", n) + 1)
                    act.wait_ge(on_done, groups_before(h, ON_LAG, n) + 1)
                    nc.scalar.copy(ot_hi[:, g, :], o_sb).then_inc(ot_hi_done, 1)

            for h in range(H):
                slot(0, h)
            with act.Fori(1, B - 1) as n:
                for h in range(H):
                    slot(n, h)
            for h in range(H):
                slot(B - 1, h)
            for h in range(EPILOGUE_SLOTS):
                slot(B, h)

        @block.tensor
        def _(pe):
            def job(j, n):
                if j == "X0":
                    pe.wait_ge(xn_ready, (n + 2) * TB)
                if j == "q0":
                    pe.wait_ge(job_ev, job_at("X1", n) + 1)
                if j == "y0":
                    pe.wait_ge(ot_done, n * G)
                wait(pe, job_ev, job_at(j, n) - 1)
                pe_job(j, n)

            pe.wait_ge(consts, 4)
            for j in PROLOGUE:
                if j in ("q0", "k0", "u0"):
                    pe.wait_ge(w_split, "qku".index(j[0]) + 1)
                job(j, -1)

            def slot(n, h):
                s = head_at(h, 0, n)
                if s is not None:
                    g, j = divmod(s, HG)
                    if s % (H // 2) < HG:
                        pe.wait_ge(stacked[g // GH][j], (n + 1) * HEAD_IN)
                    wait(pe, mx_done, n * H + h - 1)
                    for q in range(TB):
                        m = nc.tensor.matmul(s_ps[s % 2][:, q, :], stack[:, g // GH, j, 0, g % GH, q * P:(q + 1) * P],
                                             stack[:, g // GH, j, 1, g % GH, :], start=True, stop=True)
                    m.then_inc(s_done, 1)
                for j in jobs_of(h, n):
                    job(j, n)
                t = head_at(h, T_LAG, n)
                if t is not None:
                    pe.wait_ge(ex_done, n * H + h - T_LAG + 1)
                    wait(pe, pt_done, n * H + h - T_LAG - 1)
                    for o, cols in ((P, slice(2 * P, 3 * P)), (2 * P, slice(0, P)), (3 * P, slice(P, 2 * P))):
                        m = nc.tensor.transpose(t_ps[t % 2][:, o:o + P], prob[:, t % NPROB, cols], ident[:])
                    m.then_inc(t_done, 1)
                a = head_at(h, AV_LAG, n)
                if a is not None:
                    g, j = divmod(a, HG)
                    of = n if h >= AV_LAG else n - 1
                    if a == 0:
                        pe.wait_ge(job_ev, job_at("u1", of - 1) + 1)
                    if a == H // 2:
                        pe.wait_ge(job_ev, job_at("w1", of) + 1)
                    if j == 0:
                        wait(pe, on_done, groups_before(h, AV_LAG, n) - 1)
                    pe.wait_ge(pt_done, n * H + h - AV_LAG + 1)
                    at = g * STRIP + V_AT[j] - HD * j
                    keys = range(TB)
                    ranges = [slice(2 * P, 4 * P), slice(0, 2 * P)]
                    m = three_pass(nc.tensor.matmul, o_ps[g % 2][:, 0, :],
                                   ([v_hi[:, k, at:at + P] for k in keys], [v_lo[:, k, at:at + P] for k in keys]),
                                   ([pt_hi[:, a % NPT, r] for r in ranges], [pt_lo[:, a % NPT, r] for r in ranges]),
                                   j == 0, j == HG - 1)
                    m.then_inc(av_done, 1)
                    if j == HG - 1:
                        pe.wait_ge(rinv_done, groups_before(h, AV_LAG, n) + 1)
                        for q in range(TB):
                            m = nc.tensor.matmul(o_ps[g % 2][:, 1, q * P:(q + 1) * P],
                                                 rinv[:, q, :, :].rearrange("p j d -> p (j d)"), ident[:],
                                                 start=True, stop=True)
                        m.then_inc(r_done, 1)

            for h in range(H):
                slot(0, h)
            pe.wait_ge(wo_split, 2)
            with pe.Fori(1, B - 1) as n:
                for h in range(H):
                    slot(n, h)
            for h in range(H):
                slot(B - 1, h)
            for h in range(EPILOGUE_SLOTS):
                slot(B, h)

        @block.vector
        def _(dve):
            def norm_stats(k):
                if isinstance(k, int) and k == 0:
                    dve.wait_ge(x0_in, 16)
                else:
                    dve.wait_ge(x_in, k * 16)
                dve.sem_inc(tick, 1)
                for t in range(TB):
                    nc.vector.bn_stats(stats[:, t, :], xin[:, t, :]).then_inc(ln_dve, 1)
                for t in range(TB):
                    dve.wait_ge(ln_dve, k * 5 + 1 + t)
                    dve.sem_inc(tick, 1)
                    nc.vector.bn_aggr(mv[:, t, :], stats[:, t, :]).then_inc(ln_dve, 1)
                dve.wait_ge(ln_dve, k * 5 + 4)
                nc.vector.tensor_scalar(veps[:], mv[:, :, 1], EPS, None, ALU.add).then_inc(ln_dve, 1)

            def norm_apply(k):
                dve.wait_ge(ln_rstd, k + 1)
                for t in range(TB):
                    nc.vector.tensor_scalar(xn[:, t, :], xin[:, t, :], mv[:, t, 0:1], rstd[:, t:t + 1],
                                            ALU.subtract, ALU.mult).then_inc(xn_ready, 1)

            def evac(j, n):
                dve.wait_ge(job_hi, hi_at(j, n) + 1)
                pieces = parts_of(j, n)
                for hi, lo, src in pieces:
                    m = nc.vector.tensor_tensor(lo, src, hi.bitcast(F32), ALU.subtract)
                m.then_inc(job_ev, 1)

            norm_stats(0)
            norm_apply(0)
            for j in PROLOGUE:
                if j in SPLIT_AT:
                    i = SPLIT_AT[j]
                    dve.wait_ge(w_split_hi, i + 1)
                    nc.vector.tensor_tensor(w_part(w_lo, i), raw[:, i, :, :], w_part(w_hi, i).bitcast(F32),
                                            ALU.subtract).then_inc(w_split, 1)
                if j == "u0":
                    dve.wait_ge(consts, CONSTS)
                evac(j, -1)

            def slot(n, h):
                before = h - LO_JOB_LAG
                for j in jobs_of(before, n) if before >= 0 else jobs_of(H + before, n - 1 if isinstance(n, int) else n):
                    of = n if before >= 0 else n - 1
                    if isinstance(of, int) and of < 0:
                        continue
                    if j in LATE:
                        dve.wait_ge(job_done, job_at(j, of) + 1)
                        dve.wait_ge(xr_in, 16 * of)
                        xt = xr[:, int(j[1]), :]
                        nc.vector.tensor_tensor(xt, bank(j, of)[:, :], xt, ALU.add).then_inc(job_ev, 1)
                    else:
                        evac(j, of)
                s = head_at(h, 0, n)
                if s is not None:
                    dve.wait_ge(s_done, n * H + h + 1)
                    wait(dve, t_done, n * H + h - NPROB + 1)
                    dve.sem_inc(tick, 1)
                    for q, cols in ((0, slice(0, P)), (1, slice(P, 3 * P))):
                        m = nc.vector.tensor_tensor_reduce(
                            out=prob[:, s % NPROB, cols], in0=s_ps[s % 2][:, q, 0:P * (q + 1)],
                            in1=mask[:, P * (1 - q):], scale=-scale, scalar=BIG, op0=ALU.add, op1=ALU.min,
                            accum_out=nmax[:, s, q:q + 1])
                    m.then_inc(mx_done, 1)
                t = head_at(h, LO_LAG, n)
                if t is not None:
                    dve.wait_ge(pt_hi_done, n * H + h - LO_LAG + 1)
                    nc.vector.tensor_tensor(pt_lo[:, t % NPT, P:], t_ps[t % 2][:, P:],
                                            pt_hi[:, t % NPT, P:].bitcast(F32), ALU.subtract).then_inc(pt_done, 1)
                g = group_at(h, ON_LAG, n)
                if g is not None:
                    dve.wait_ge(rs_done, groups_before(h, ON_LAG, n) + 1)
                    nc.vector.tensor_tensor(o_sb, o_ps[g % 2][:, 0, :], r_sb, ALU.mult).then_inc(on_done, 1)
                g = group_at(h, OT_LAG, n)
                if g is not None:
                    dve.wait_ge(ot_hi_done, groups_before(h, OT_LAG, n) + 1)
                    nc.vector.tensor_tensor(ot_lo[:, g, :], o_sb, ot_hi[:, g, :].bitcast(F32),
                                            ALU.subtract).then_inc(ot_done, 1)
                g = group_at(h, RINV_LAG, n)
                if g is not None:
                    before = groups_before(h, RINV_LAG, n)
                    dve.wait_ge(ex_done, before * HG + HG)
                    nc.vector.reciprocal(rinv8[:, g, :, :], rsum[:, g, :, :]).then_inc(rinv8_done, 1)
                    dve.wait_ge(rinv8_done, before + 1)
                    wait(dve, ot_done, before)
                    nc.vector.tensor_copy(rinv[:], free_ap(rinv8[:, g, :, :], 0, [[HG, TB], [1, HG], [0, HD]]))\
                        .then_inc(rinv_done, 1)
                if head_at(h, 0, n) is not None and (not isinstance(n, int) or n < B - 1):
                    if h == 0:
                        norm_stats(n + 1)
                    if h == 2:
                        norm_apply(n + 1)

            for h in range(H):
                slot(0, h)
            with dve.Fori(1, B - 1) as n:
                for h in range(H):
                    slot(n, h)
            for h in range(H):
                slot(B - 1, h)
            for h in range(EPILOGUE_SLOTS):
                slot(B, h)


class Routing:
    SLOTS_OF = B * S
    ROWS = E * SLOTS_OF + (E + 3) * P
    STEPS = 9

    def __init__(self, nc, cx):
        sb = lambda n, s, d=F32: cx.enter_context(nc.sbuf_tensor("r_" + n, s, d))
        sem = lambda n: cx.enter_context(nc.semaphore("r_" + n))
        self.table = nc.dram_tensor("slots", [self.ROWS, 2], I32).ap()
        self.logits = sb("logits", [P, TB, E])
        self.lmax, self.diff, self.eq = sb("lmax", [P, TB]), sb("diff", [P, TB, E]), sb("eq", [P, TB, E])
        self.ex, self.gsum = sb("ex", [P, TB, E]), sb("gsum", [P, TB])
        self.rank_i, self.rank = sb("rank_i", [P, E], I32), sb("rank", [P, E])
        self.best, self.onehot = sb("best", [P, TB]), sb("onehot", [P, TB, E], BF16)
        self.before, self.ones = sb("before", [P, P], BF16), sb("ones", [P, P], BF16)
        self.next_i, self.next = sb("next_i", [P, E], I32), sb("next", [P, E])
        self.place, self.slot, self.slot_i = sb("place", [P, TB, E]), sb("slot", [P, TB]), sb("slot_i", [P, TB], U32)
        self.entry = sb("entry", [P, TB, 2], I32)
        self.token = sb("token", [P, TB])
        self.ranks_ps = cx.enter_context(nc.psum_tensor("r_ranks", [P, TB + 1, E], F32))
        self.consts, self.token_done, self.entries_in = sem("consts"), sem("token_done"), sem("entries_in")
        self.step, self.diff_done, self.ex_done = sem("step"), sem("diff_done"), sem("ex_done")
        self.onehot_done, self.gate_done = sem("onehot_done"), sem("gate_done")
        self.ranks_done, self.slot_done = sem("ranks_done"), sem("slot_done")

    CONSTS = 8

    def constants(self, nc, pool):
        nc.gpsimd.memset(self.before[:], 1.0).then_inc(self.consts, 1)
        nc.gpsimd.memset(self.ones[:], 1.0).then_inc(self.consts, 1)
        nc.gpsimd.iota(self.rank_i[:], pattern=[[-1, E]], base=E, channel_multiplier=0).then_inc(self.consts, 1)
        nc.gpsimd.iota(self.next_i[:], pattern=[[self.SLOTS_OF, E]], base=0, channel_multiplier=0).then_inc(self.consts, 1)
        nc.gpsimd.iota(self.entry[:, :, 0], pattern=[[P, TB]], base=0, channel_multiplier=1).then_inc(self.token_done, 1)
        pool.wait_ge(self.consts, 4)
        pool.wait_ge(self.token_done, 1)
        nc.gpsimd.tensor_copy(self.rank[:], self.rank_i[:]).then_inc(self.consts, 1)
        nc.gpsimd.tensor_copy(self.next[:], self.next_i[:]).then_inc(self.consts, 1)
        nc.gpsimd.tensor_copy(self.token[:], self.entry[:, :, 0]).then_inc(self.consts, 1)
        nc.gpsimd.affine_select(out=self.before[:], in_=self.before[:], compare_op=ALU.is_gt, fill=0.0, base=0,
                                pattern=[[1, P]], channel_multiplier=-1).then_inc(self.consts, 1)

    def choose(self, nc, dve, n):
        done = n * self.STEPS
        over_e = lambda t: free_ap(t, 0, [[1, TB], [0, E]])
        nc.vector.tensor_reduce(self.lmax[:], self.logits[:], AX.X, ALU.max).then_inc(self.step, 1)
        dve.wait_ge(self.step, done + 1)
        nc.vector.tensor_tensor(self.diff[:], self.logits[:], over_e(self.lmax[:]), ALU.subtract).then_inc(self.diff_done, 1)
        nc.vector.tensor_tensor(self.eq[:], self.logits[:], over_e(self.lmax[:]), ALU.is_equal).then_inc(self.step, 1)
        dve.wait_ge(self.step, done + 2)
        nc.vector.tensor_tensor(self.eq[:], self.eq[:], free_ap(self.rank[:], 0, [[0, TB], [1, E]]), ALU.mult)\
            .then_inc(self.step, 1)
        dve.wait_ge(self.step, done + 3)
        nc.vector.tensor_reduce(self.best[:], self.eq[:], AX.X, ALU.max).then_inc(self.step, 1)
        dve.wait_ge(self.step, done + 4)
        nc.vector.tensor_tensor(self.onehot[:], self.eq[:], over_e(self.best[:]), ALU.is_equal).then_inc(self.onehot_done, 1)
        dve.wait_ge(self.ex_done, n + 1)
        nc.vector.tensor_reduce(self.gsum[:], self.ex[:], AX.X, ALU.add).then_inc(self.step, 1)
        dve.wait_ge(self.step, done + 5)
        dve.wait_ge(self.token_done, n + 1)
        nc.vector.reciprocal(self.entry[:, :, 1].bitcast(F32), self.gsum[:]).then_inc(self.gate_done, 1)

    def exponentials(self, nc, act, n):
        act.wait_ge(self.diff_done, n + 1)
        nc.scalar.activation(self.ex[:], self.diff[:], ACT.Exp).then_inc(self.ex_done, 1)

    def count(self, nc, pe, n):
        pe.wait_ge(self.onehot_done, n + 1)
        out, oh = self.ranks_ps, self.onehot
        nc.tensor.matmul(out[:, 0, :], self.before[:], oh[:, 0, :], start=True, stop=True)
        for t in range(TB):
            nc.tensor.matmul(out[:, t + 1, :], self.ones[:], oh[:, 0, :], start=True, stop=False)
            m = nc.tensor.matmul(out[:, t + 1, :], (self.before if t + 1 < TB else self.ones)[:], oh[:, 1, :],
                                 start=False, stop=True)
        m.then_inc(self.ranks_done, 1)
    assert TB == 2

    def place_tokens(self, nc, dve, n):
        done = n * self.STEPS
        dve.wait_ge(self.ranks_done, n + 1)
        nc.vector.tensor_tensor(self.place[:], self.ranks_ps[:, 0:TB, :], free_ap(self.next[:], 0, [[0, TB], [1, E]]),
                                ALU.add).then_inc(self.step, 1)
        dve.wait_ge(self.step, done + 6)
        nc.vector.tensor_tensor(self.place[:], self.place[:], self.onehot[:], ALU.mult).then_inc(self.step, 1)
        nc.vector.tensor_tensor(self.next[:], self.next[:], self.ranks_ps[:, TB, :], ALU.add).then_inc(self.step, 1)
        dve.wait_ge(self.step, done + 8)
        nc.vector.tensor_reduce(self.slot[:], self.place[:], AX.X, ALU.add).then_inc(self.step, 1)
        dve.wait_ge(self.step, done + 9)
        nc.vector.tensor_copy(self.slot_i[:], self.slot[:]).then_inc(self.slot_done, 1)

    def store_entries(self, nc, pool, tick, n, more):
        pool.wait_ge(self.gate_done, n + 1)
        pool.wait_ge(self.slot_done, n + 1)
        pool.sem_inc(tick, 1)
        for t in range(TB):
            pool.indirect_dma_start(self.table, bass.IndirectOffsetOnAxis(ap=self.slot_i[:, t:t + 1], axis=0),
                                    self.entry[:, t, :], None).then_inc(self.entries_in, 16)
        if more:
            pool.wait_ge(self.entries_in, (n + 1) * 16 * TB)
            pool.sem_inc(tick, 1)
            nc.gpsimd.tensor_scalar(self.token[:], self.token[:], float(S), None, ALU.add).then_inc(self.consts, 1)
            pool.wait_ge(self.consts, n + self.CONSTS + 1)
            pool.sem_inc(tick, 1)
            nc.gpsimd.tensor_copy(self.entry[:, :, 0], self.token[:]).then_inc(self.token_done, 1)


def cross_attention(nc, ident, routing, x1, x1_out, x1_last_out, x1_first_in, ctx, wv, wo, wg,
                    x2n, x2n_out, xin, xr, x2_sb, xn3_sb, bias, bias_sb, bias_in, stage, stage_in, w, expert_in):
    scale = float(D) ** -0.5
    RING = 7
    KEYS = 2 * S
    KC = KEYS // P
    with ExitStack() as cx:
        sb = lambda n, s, d=F32: cx.enter_context(nc.sbuf_tensor("b_" + n, s, d))
        sem = lambda n: cx.enter_context(nc.semaphore("b_" + n))
        raw = stage + [bias_sb[:, 0:DC * D].rearrange("p (c n) -> p c n", c=DC)]
        wt_hi = {n: sb(f"w{n}t_hi", [P, DC, D], F32R) for n in "qkvo"}
        wt_lo = {n: sb(f"w{n}t_lo", [P, DC, D], F32R) for n in "qkvo"}
        wg_sb = sb("wg", [P, DC, E])
        cin, xn = sb("cin", [P, TB, D]), sb("xn", [P, TB, D])
        stats, mv = sb("stats", [P, 2, TB, 6]), sb("mv", [P, 2, TB, 2])
        veps, rstd = sb("veps", [P, 2, TB]), sb("rstd", [P, 2, TB])
        expo = sb("expo", [P, TB])
        xt_hi, xt_lo = sb("xt_hi", [P, DC, S], F32R), sb("xt_lo", [P, DC, S], F32R)
        qt_hi, qt_lo = sb("qt_hi", [P, DC, S], F32R), sb("qt_lo", [P, DC, S], F32R)
        kt_hi, kt_lo = sb("kt_hi", [P, DC, KEYS], F32R), sb("kt_lo", [P, DC, KEYS], F32R)
        v_hi, v_lo = sb("v_hi", [P, KC, D], F32R), sb("v_lo", [P, KC, D], F32R)
        smax, nmax, rsum, rinv = sb("smax", [P, TB]), sb("nmax", [P, TB]), sb("rsum", [P, TB]), sb("rinv", [P, TB])
        prob = sb("prob", [P, TB, KEYS])
        pt_hi, pt_lo = sb("pt_hi", [P, KC, S], F32R), sb("pt_lo", [P, KC, S], F32R)
        ot_hi, ot_lo = sb("ot_hi", [P, DC, S], F32R), sb("ot_lo", [P, DC, S], F32R)
        xt3 = sb("xt3", [P, DC, S])
        unused = sb("unused", [P, Routing.ROWS // P, 2], I32)
        assert Routing.ROWS % P == 0
        ring = [cx.enter_context(nc.psum_tensor(f"b_bank{i}", [P, D], F32)) for i in range(RING)]

        w_in = stage_in + [sem("wo_in")]
        wg_in, x_in, xr_in, c_in = (sem(n) for n in ("wg_in", "x_in", "xr_in", "c_in"))
        x2_out, xn3_out = x2n_out
        consts, unused_done, init_in = sem("consts"), sem("unused_done"), sem("init_in")
        tick, tick_pool = sem("tick"), sem("tick_pool")
        ln_dve, ln_rstd, xn_ready = sem("ln_dve"), sem("ln_rstd"), sem("xn_ready")
        ln3_dve, ln3_rstd, xn3_ready = sem("ln3_dve"), sem("ln3_rstd"), sem("xn3_ready")
        job_done, job_hi, job_ev = sem("job_done"), sem("job_hi"), sem("job_ev")
        c_hi, c_split = sem("c_hi"), sem("c_split")
        max_done, mx_done, ex_done, rinv_done = sem("max_done"), sem("mx_done"), sem("ex_done"), sem("rinv_done")

        ORDER = ("X0 X1 s0 s1 C0 C1 q0 q1 p0 p1 q2 q3 o0 o1 o2 o3 k0 y0 y1 k1 k2 k3 v0 Y0 Y1 v1 l0 l1").split()
        FRONT = "XCqkv"
        LAST = [j for j in ORDER if j[0] not in FRONT]
        PROLOGUE = ("wq0 wq1 wq2 wq3 wk0 wk1 X0 X1 wk2 wk3 q0 q1 C0 C1 q2 q3 wv0 wv1 k0 k1 wv2 wv3 k2 k3 wo0 v0 wo1 v1 "
                    "wo2 wo3").split()
        ev_jobs = lambda js: [j for j in js if j[0] != "s"]
        hi_jobs = lambda js: [j for j in js if j[0] not in "syYl"]

        def order(n):
            return ORDER if not isinstance(n, int) or n < B - 1 else LAST

        def count(j, n, kind):
            if isinstance(n, int) and n < 0:
                return kind(PROLOGUE).index(j)
            return len(kind(PROLOGUE)) + n * len(kind(ORDER)) + kind(order(n)).index(j)

        done_at = lambda j, n: count(j, n, list) + 1
        ev_at = lambda j, n: count(j, n, ev_jobs) + 1
        hi_at = lambda j, n: count(j, n, hi_jobs) + 1

        def has_routing(n):
            return not isinstance(n, int) or n > 0

        def route_after(n):
            return "q3" if order(n) is ORDER else "p1"

        def bank(j, n):
            if isinstance(n, int) and n < 0:
                return ring[PROLOGUE.index(j) % RING]
            return ring[(len(PROLOGUE) + order(n).index(j)) % RING]
        assert len(ORDER) % RING == 0

        def parts_of(j, n):
            b, i = bank(j, n), int(j[-1])
            toks = slice(i * P, (i + 1) * P)
            chunked = b[:, :].rearrange("p (c n) -> p c n", c=DC)
            return {"w": lambda: (wt_hi[j[1]][:, i, :], wt_lo[j[1]][:, i, :], b[:, :]),
                    "X": lambda: (xt_hi[:, :, toks], xt_lo[:, :, toks], chunked),
                    "C": lambda: (kt_hi[:, :, toks], kt_lo[:, :, toks], chunked),
                    "q": lambda: (qt_hi[:, i, :], qt_lo[:, i, :], b[:, 0:S]),
                    "k": lambda: (kt_hi[:, i, S:], kt_lo[:, i, S:], b[:, 0:S]),
                    "v": lambda: (v_hi[:, TB + i, :], v_lo[:, TB + i, :], b[:, :]),
                    "p": lambda: (pt_hi[:, 2 * i:2 * i + 2, :], pt_lo[:, 2 * i:2 * i + 2, :],
                                  b[:, :].rearrange("p (c n) -> p c n", c=2)),
                    "o": lambda: (ot_hi[:, i, :], ot_lo[:, i, :], b[:, 0:S])}[j[0]]()

        block = cx.enter_context(nc.Block())

        @block.sync
        def _(sp):
            chunks = lambda t: t.rearrange("(c p) n -> p c n", p=P)
            sp.dma_start(cin[:], batch_rows(ctx, 0)).then_inc(c_in, 16)
            sp.wait_ge(unused_done, 2)
            sp.dma_start(routing.table.rearrange("(p k) c -> p k c", p=P), unused[:]).then_inc(init_in, 16)
            sp.dma_start(raw[2][:], chunks(wv)).then_inc(w_in[2], 16)
            sp.dma_start(raw[3], chunks(wo)).then_inc(w_in[3], 16)
            sp.wait_ge(x1_out, 16 * (B - 1))
            sp.wait_ge(x1_last_out, 16)
            sp.dma_start(xr[:], batch_rows(x1, 0)).then_inc(xr_in, 16)
            sp.dma_start(wg_sb[:], chunks(wg)).then_inc(wg_in, 16)
            sp.wait_ge(xn_ready, TB)
            sp.dma_start(xin[:], batch_rows(x1, 1)).then_inc(x_in, 16)
            sp.wait_ge(c_split, 1)
            sp.wait_ge(job_done, done_at("C1", -1))
            sp.dma_start(cin[:], batch_rows(ctx, 1)).then_inc(c_in, 16)

            for i, n in enumerate("qkv"):
                sp.wait_ge(job_done, done_at(f"w{n}3", -1))
                sp.dma_start(stage[i][:], w[i].rearrange("(c p) h -> p c h", p=P)).then_inc(expert_in[i], 16)

            sp.wait_ge(job_done, done_at("wo3", -1))
            sp.dma_start(bias_sb[:], bass.AP(tensor=bias.tensor, offset=bias.offset, ap=[[0, P], [1, E * D]]))\
                .then_inc(bias_in, 16)

            def batch(n, more, load):
                if load:
                    sp.wait_ge(xn_ready, (n + 2) * TB)
                    sp.dma_start(xin[:], batch_rows(x1, n + 2)).then_inc(x_in, 16)
                    sp.wait_ge(c_split, n + 2)
                    sp.wait_ge(job_done, done_at("C1", n))
                    sp.dma_start(cin[:], batch_rows(ctx, n + 2)).then_inc(c_in, 16)
                sp.wait_ge(job_ev, ev_at("y1", n))
                sp.dma_start(batch_rows(x2n[:, 0:D], n), x2_sb[:]).then_inc(x2_out, 16)
                if more:
                    sp.dma_start(xr[:], batch_rows(x1, n + 1)).then_inc(xr_in, 16)
                sp.wait_ge(xn3_ready, (n + 1) * TB)
                sp.dma_start(batch_rows(x2n[:, D:], n), xn3_sb[:]).then_inc(xn3_out, 16)

            batch(0, True, True)
            with sp.Fori(1, B - 2) as n:
                batch(n, True, True)
            batch(B - 2, True, False)
            batch(B - 1, False, False)

        @block.gpsimd
        def _(pool):
            nc.gpsimd.memset(expo[:], -0.5).then_inc(consts, 1)
            pool.wait_ge(consts, 1)

            def rstd_ln2(k):
                pool.wait_ge(ln_dve, k * 5 + 5)
                nc.gpsimd.tensor_tensor(rstd[:, 0, :], veps[:, 0, :], expo[:], ALU.pow).then_inc(ln_rstd, 1)

            def rstd_ln3(k):
                pool.wait_ge(ln3_dve, k * 5 + 5)
                nc.gpsimd.tensor_tensor(rstd[:, 1, :], veps[:, 1, :], expo[:], ALU.pow).then_inc(ln3_rstd, 1)

            nc.gpsimd.memset(unused[:], 0).then_inc(unused_done, 1)
            pool.wait_ge(unused_done, 1)
            nc.gpsimd.iota(unused[:, :, 0], pattern=[[1, Routing.ROWS // P]], base=B * S,
                           channel_multiplier=Routing.ROWS // P).then_inc(unused_done, 1)
            rstd_ln2(0)
            routing.constants(nc, pool)
            rstd_ln2(1)
            rstd_ln2(2)
            rstd_ln3(0)
            pool.wait_ge(init_in, 16)
            with pool.Fori(1, B - 2) as n:
                rstd_ln2(n + 2)
                rstd_ln3(n)
                routing.store_entries(nc, pool, tick_pool, n - 1, True)
            rstd_ln3(B - 2)
            routing.store_entries(nc, pool, tick_pool, B - 3, True)
            routing.store_entries(nc, pool, tick_pool, B - 2, True)
            rstd_ln3(B - 1)

        @block.scalar
        def _(act):
            def hi_part(j, n):
                act.wait_ge(job_done, done_at(j, n))
                hi, _, src = parts_of(j, n)
                nc.scalar.copy(hi, src).then_inc(job_hi, 1)

            def ctx_hi(k):
                act.wait_ge(c_in, 16 * (k + 1))
                nc.scalar.copy(v_hi[:, 0:TB, :], cin[:]).then_inc(c_hi, 1)

            for j in PROLOGUE:
                hi_part(j, -1)
                if j == "C1":
                    ctx_hi(0)

            def batch(n):
                for j in order(n):
                    if j[0] == "s":
                        q = int(j[1])
                        act.wait_ge(mx_done, n * TB + q + 1)
                        nc.scalar.activation(prob[:, q, :], bank(j, n)[:, :], ACT.Exp, scale=scale,
                                             bias=nmax[:, q:q + 1], accum_out=rsum[:, q:q + 1]).then_inc(ex_done, 1)
                    if j in hi_jobs(order(n)):
                        hi_part(j, n)
                    if j == route_after(n) and has_routing(n):
                        routing.exponentials(nc, act, n - 1)
                    if j == "o3" and order(n) is ORDER:
                        ctx_hi(n + 1)

            batch(0)
            with act.Fori(1, B - 1) as n:
                batch(n)
            batch(B - 1)

        @block.tensor
        def _(pe):
            def wait_bank(j, n):
                if isinstance(n, int) and n < 0:
                    before, of = PROLOGUE.index(j) - RING, -1
                    if before < 0:
                        return
                    last = PROLOGUE[before]
                else:
                    before = order(n).index(j) - RING
                    if before >= 0:
                        last, of = order(n)[before], n
                    elif isinstance(n, int) and n == 0:
                        last, of = PROLOGUE[before], -1
                    else:
                        last, of = ORDER[before], n - 1
                if last[0] == "s":
                    pe.wait_ge(ex_done, of * TB + int(last[1]) + 1)
                else:
                    pe.wait_ge(job_ev, ev_at(last, of))

            def job(j, n):
                wait_bank(j, n)
                b, i = bank(j, n), int(j[-1])
                toks = slice(i * P, (i + 1) * P)
                rows = slice(i * P, (i + 1) * P)
                chunks = range(DC)
                if j[0] == "w":
                    if i == 0:
                        pe.wait_ge(w_in["qkvo".index(j[1])], 16)
                    for c in chunks:
                        m = nc.tensor.transpose(b[:, c * P:(c + 1) * P], raw["qkvo".index(j[1])][:, c, rows], ident[:])
                elif j[0] in "XCY":
                    if j == "X0":
                        pe.wait_ge(xn_ready, (n + 2) * TB)
                    if j == "C0":
                        pe.wait_ge(c_in, 16 * (n + 2))
                    if j[0] == "Y":
                        pe.wait_ge(xn3_ready, n * TB + i + 1)
                    src = {"X": xn, "C": cin, "Y": xn3_sb}[j[0]]
                    for c in chunks:
                        m = nc.tensor.transpose(b[:, c * P:(c + 1) * P], src[:, i, c * P:(c + 1) * P], ident[:])
                elif j[0] in "qk":
                    if j == "q0":
                        pe.wait_ge(job_ev, ev_at("X1", n))
                    if isinstance(n, int) and n < 0 and i == 0:
                        pe.wait_ge(job_ev, ev_at(f"w{j[0]}3", n))
                    m = three_pass(nc.tensor.matmul, b[:, 0:S],
                                   ([wt_hi[j[0]][:, c, rows] for c in chunks], [wt_lo[j[0]][:, c, rows] for c in chunks]),
                                   ([xt_hi[:, c, :] for c in chunks], [xt_lo[:, c, :] for c in chunks]))
                elif j[0] == "v":
                    if isinstance(n, int) and n < 0 and i == 0:
                        pe.wait_ge(job_ev, ev_at("wv3", n))
                    m = three_pass(nc.tensor.matmul, b[:, :],
                                   ([xt_hi[:, c, toks] for c in chunks], [xt_lo[:, c, toks] for c in chunks]),
                                   ([wt_hi["v"][:, c, :] for c in chunks], [wt_lo["v"][:, c, :] for c in chunks]))
                elif j[0] == "s":
                    if i == 0:
                        pe.wait_ge(job_ev, ev_at("k3", n - 1))
                    m = three_pass(nc.tensor.matmul, b[:, :],
                                   ([qt_hi[:, c, toks] for c in chunks], [qt_lo[:, c, toks] for c in chunks]),
                                   ([kt_hi[:, c, :] for c in chunks], [kt_lo[:, c, :] for c in chunks]))
                elif j[0] == "p":
                    pe.wait_ge(ex_done, (n + 1) * TB)
                    for k in range(2):
                        for q in range(TB):
                            m = nc.tensor.transpose(b[:, (k * TB + q) * P:(k * TB + q + 1) * P],
                                                    prob[:, q, (2 * i + k) * P:(2 * i + k + 1) * P], ident[:])
                elif j[0] == "o":
                    if i == 0:
                        pe.wait_ge(job_ev, ev_at("p1", n))
                        pe.wait_ge(c_split, n + 1)
                    keys = range(KC)
                    m = three_pass(nc.tensor.matmul, b[:, 0:S],
                                   ([v_hi[:, k, rows] for k in keys], [v_lo[:, k, rows] for k in keys]),
                                   ([pt_hi[:, k, :] for k in keys], [pt_lo[:, k, :] for k in keys]))
                elif j[0] == "y":
                    if i == 0:
                        pe.wait_ge(job_ev, ev_at("o3", n))
                    m = three_pass(nc.tensor.matmul, b[:, :],
                                   ([ot_hi[:, c, toks] for c in chunks], [ot_lo[:, c, toks] for c in chunks]),
                                   ([wt_hi["o"][:, c, :] for c in chunks], [wt_lo["o"][:, c, :] for c in chunks]))
                else:
                    if i == 0:
                        pe.wait_ge(job_ev, ev_at("Y1", n))
                    for c in chunks:
                        m = nc.tensor.matmul(b[:, 0:E], xt3[:, c, toks], wg_sb[:, c, :], start=c == 0, stop=c == DC - 1)
                m.then_inc(job_done, 1)

            for j in PROLOGUE:
                job(j, -1)
            pe.wait_ge(wg_in, 16)
            pe.wait_ge(routing.consts, Routing.CONSTS)

            def batch(n):
                for j in order(n):
                    job(j, n)
                    if j == "o1" and has_routing(n):
                        routing.count(nc, pe, n - 1)

            batch(0)
            with pe.Fori(1, B - 1) as n:
                batch(n)
            batch(B - 1)

        @block.vector
        def _(dve):
            def norm_stats(which, k, src, done):
                for t in range(TB):
                    nc.vector.bn_stats(stats[:, which, t, :], src[:, t, :]).then_inc(done, 1)
                for t in range(TB):
                    dve.wait_ge(done, k * 5 + 1 + t)
                    dve.sem_inc(tick, 1)
                    nc.vector.bn_aggr(mv[:, which, t, :], stats[:, which, t, :]).then_inc(done, 1)
                dve.wait_ge(done, k * 5 + 4)
                nc.vector.tensor_scalar(veps[:, which, :], mv[:, which, :, 1], EPS, None, ALU.add).then_inc(done, 1)

            def norm_apply(which, dst, src, ready):
                for t in range(TB):
                    nc.vector.tensor_scalar(dst[:, t, :], src[:, t, :], mv[:, which, t, 0:1], rstd[:, which, t:t + 1],
                                            ALU.subtract, ALU.mult).then_inc(ready, 1)

            def ln2_stats(k):
                if isinstance(k, int) and k == 0:
                    dve.wait_ge(x1_first_in, 16)
                else:
                    dve.wait_ge(x_in, k * 16)
                dve.sem_inc(tick, 1)
                norm_stats(0, k, xin, ln_dve)

            def ln2_apply(k):
                dve.wait_ge(ln_rstd, k + 1)
                norm_apply(0, xn, xin, xn_ready)

            def lo_part(j, n):
                dve.wait_ge(job_hi, hi_at(j, n))
                hi, lo, src = parts_of(j, n)
                nc.vector.tensor_tensor(lo, src, hi.bitcast(F32), ALU.subtract).then_inc(job_ev, 1)

            def ctx_lo(k):
                dve.wait_ge(c_hi, k + 1)
                nc.vector.tensor_tensor(v_lo[:, 0:TB, :], cin[:], v_hi[:, 0:TB, :].bitcast(F32),
                                        ALU.subtract).then_inc(c_split, 1)

            for j in PROLOGUE:
                lo_part(j, -1)
                if j == "wq0":
                    ln2_stats(0)
                if j == "wq2":
                    ln2_apply(0)
                if j == "C1":
                    ctx_lo(0)
                if j == "k1":
                    ln2_stats(1)
                if j == "k3":
                    ln2_apply(1)

            def batch(n):
                for j in order(n):
                    if j[0] == "s":
                        q = int(j[1])
                        dve.wait_ge(job_done, done_at(j, n))
                        dve.sem_inc(tick, 1)
                        nc.vector.tensor_reduce(smax[:, q:q + 1], bank(j, n)[:, :], AX.X, ALU.max).then_inc(max_done, 1)
                        dve.wait_ge(max_done, n * TB + q + 1)
                        nc.vector.tensor_scalar(nmax[:, q:q + 1], smax[:, q:q + 1], -scale, None, ALU.mult)\
                            .then_inc(mx_done, 1)
                    elif j[0] == "y":
                        i = int(j[1])
                        if i == 0:
                            dve.wait_ge(xr_in, 16 * (n + 1))
                            wait(dve, x2_out, 16 * n)
                            dve.wait_ge(rinv_done, n + 1)
                        dve.wait_ge(job_done, done_at(j, n))
                        nc.vector.scalar_tensor_tensor(x2_sb[:, i, :], bank(j, n)[:, :], rinv[:, i:i + 1], xr[:, i, :],
                                                       ALU.mult, ALU.add).then_inc(job_ev, 1)
                    elif j[0] == "Y":
                        dve.wait_ge(job_done, done_at(j, n))
                        nc.vector.tensor_copy(xt3[:, :, int(j[1]) * P:(int(j[1]) + 1) * P],
                                              bank(j, n)[:, :].rearrange("p (c n) -> p c n", c=DC)).then_inc(job_ev, 1)
                    elif j[0] == "l":
                        dve.wait_ge(job_done, done_at(j, n))
                        nc.vector.tensor_copy(routing.logits[:, int(j[1]), :], bank(j, n)[:, 0:E]).then_inc(job_ev, 1)
                    else:
                        lo_part(j, n)
                    if j == route_after(n) and has_routing(n):
                        dve.wait_ge(job_ev, ev_at("l1", n - 1))
                        dve.sem_inc(tick, 1)
                        routing.choose(nc, dve, n - 1)
                    if j == ("k0" if order(n) is ORDER else "o3") and has_routing(n):
                        routing.place_tokens(nc, dve, n - 1)
                    if j == "o3" and order(n) is ORDER:
                        ctx_lo(n + 1)
                    if j == "p1":
                        nc.vector.reciprocal(rinv[:], rsum[:]).then_inc(rinv_done, 1)
                    if j == "y1":
                        dve.wait_ge(job_ev, ev_at("y1", n))
                        dve.sem_inc(tick, 1)
                        norm_stats(1, n, x2_sb, ln3_dve)
                    if j == ("k1" if order(n) is ORDER else "y1"):
                        wait(dve, xn3_out, 16 * n)
                        dve.wait_ge(ln3_rstd, n + 1)
                        norm_apply(1, xn3_sb, x2_sb, xn3_ready)
                    if j in ("p1", "o1") and (not isinstance(n, int) or n < B - 2):
                        (ln2_stats if j == "p1" else ln2_apply)(n + 2)

            dve.wait_ge(routing.consts, Routing.CONSTS)
            batch(0)
            with dve.Fori(1, B - 2) as n:
                batch(n)
            batch(B - 2)
            batch(B - 1)


def mixture_of_experts(nc, ident, routing, x2n, x2n_out, w, bias_sb, bias_in, out, stage, expert_in):
    N = B * S
    BLOCKS = NT + E - 1
    AHEAD = 4
    BEHIND = 5
    RX = 6
    FIRST = 5
    YB = 3
    RING = 7
    EARLY = 8
    W_JOBS = E * DC
    assert (BLOCKS - FIRST) % RX == 0 and RX % YB == 0 and FIRST > YB and RX > BEHIND
    assert STAGED * DC * D == RX * 2 * D and RX % STAGED == 0
    assert E * Routing.SLOTS_OF + (BLOCKS + AHEAD - N // P) * P <= Routing.ROWS
    with ExitStack() as cx:
        sb = lambda n, s, d=F32: cx.enter_context(nc.sbuf_tensor("c_" + n, s, d))
        sem = lambda n: cx.enter_context(nc.semaphore("c_" + n))
        wt_hi, wt_lo = sb("wt_hi", [P, DC, E * D], F32R), sb("wt_lo", [P, DC, E * D], F32R)
        xt_hi, xt_lo = sb("xt_hi", [P, 2, D], F32R), sb("xt_lo", [P, 2, D], F32R)
        y_sb = sb("y_sb", [P, YB, D])
        upto = sb("upto", [P, E, E])
        full_i, full = sb("full_i", [P, NT], I32), sb("full", [P, NT])
        block_i, block_no = sb("block_i", [P, BLOCKS + AHEAD], I32), sb("block_no", [P, BLOCKS + AHEAD])
        first_i, first = sb("first_i", [P, E], I32), sb("first", [P, E])
        number = sb("number", [P, E])
        over, blocks = sb("over", [P, E, NT]), sb("blocks", [P, E])
        cum, end, skip = sb("cum", [P, E, E]), sb("end", [P, E]), sb("skip", [P, E])
        past, owner = sb("past", [P, BLOCKS + AHEAD, E]), sb("owner", [P, BLOCKS + AHEAD])
        owner_i = sb("owner_i", [P, BLOCKS + AHEAD], I32)
        at, at_sum = sb("at", [P, BLOCKS + AHEAD, E]), sb("at_sum", [P, BLOCKS + AHEAD])
        at_i = sb("at_i", [P, BLOCKS + AHEAD], I32)
        tab = sb("tab", [P, BLOCKS + AHEAD, 2], I32)
        gather_no, scatter_no = sb("gather_no", [P, RX, 1], U32), sb("scatter_no", [P, RX, 1], U32)
        ring = [cx.enter_context(nc.psum_tensor(f"c_bank{i}", [P, D], F32)) for i in range(RING)]
        t_ps, y_ps = ring[0:2], ring[2:4]

        w_in = expert_in
        rows_in, out_done = [sem(f"rows_in{i}") for i in range(RX)], [sem(f"out_done{i}") for i in range(RX)]
        tab_in = [sem(f"tab_in{i}") for i in range(RX)]
        consts, route, at_done = sem("consts"), sem("route"), sem("at_done")
        owner_done, tick_pool, tick_act = sem("owner_done"), sem("tick_pool"), sem("tick_act")
        w_done, w_hi_done, w_split = sem("w_done"), sem("w_hi_done"), sem("w_split")
        gather_first_done, gather_no_done = sem("gather_first_done"), sem("gather_no_done")
        scatter_no_done = sem("scatter_no_done")
        t_done, xt_hi_done, xt_done = sem("t_done"), sem("xt_hi_done"), sem("xt_done")
        y_done, bias_done, fin_done = sem("y_done"), sem("bias_done"), sem("fin_done")
        block = cx.enter_context(nc.Block())
        CONSTS = 9

        def rows(k, columns):
            place, part = divmod(k % RX, RX // STAGED)
            first_column = part * 2 * D
            return stage[(E + place) % STAGED][:].rearrange("p c n -> p (c n)")[:, first_column + columns.start:
                                                                               first_column + columns.stop]

        def blocks_loop(engine, step):
            for k in range(FIRST):
                step(0, k)
            with engine.Fori(0, (BLOCKS - FIRST) // RX) as i:
                for k in range(FIRST, FIRST + RX):
                    step(i, k)

        def number_of(i, k):
            return i * RX + k

        def turn(i, k):
            return i + k // RX

        def column(t, i, k, c):
            return t[:, k, c:c + 1] if isinstance(i, int) else t[:, bass.ds(i * RX + k, 1), c]

        @block.sync
        def _(sp):
            def weights(e):
                sp.wait_ge(w_done, (e - STAGED + 1) * DC)
                sp.dma_start(stage[e % STAGED][:], w[e].rearrange("(c p) h -> p c h", p=P)).then_inc(w_in[e % STAGED], 16)

            def entries(i, k):
                m = number_of(i, k)
                if k >= RX:
                    sp.wait_ge(tab_in[k % RX], 16 * turn(i, k))
                row = sp.value_load(at_i[0:1, m:m + 1] if isinstance(m, int) else at_i[0:1, bass.ds(m, 1)],
                                    min_val=0, max_val=Routing.ROWS - P)
                place = tab[:, m, :] if isinstance(m, int) else tab[:, bass.ds(m, 1), :].rearrange("p o c -> p (o c)")
                sp.dma_start(place, routing.table[bass.ds(row, P), :]).then_inc(tab_in[k % RX], 16)

            for e in range(STAGED, E - 1):
                weights(e)
            sp.wait_ge(routing.entries_in, 16 * NT)
            sp.wait_ge(at_done, 1)
            for k in range(AHEAD):
                entries(0, k)
            weights(E - 1)
            alone = RX + (BLOCKS + AHEAD) % RX
            for k in range(AHEAD, alone):
                entries(0, k)
            with sp.Fori(0, (BLOCKS + AHEAD - alone) // RX) as i:
                for k in range(alone, alone + RX):
                    entries(i, k)

        @block.gpsimd
        def _(pool):
            nc.gpsimd.memset(upto[:], 1.0).then_inc(consts, 1)
            nc.gpsimd.iota(full_i[:], pattern=[[P, NT]], base=0, channel_multiplier=0).then_inc(consts, 1)
            nc.gpsimd.iota(block_i[:], pattern=[[1, BLOCKS + AHEAD]], base=0, channel_multiplier=0).then_inc(consts, 1)
            nc.gpsimd.iota(first_i[:], pattern=[[Routing.SLOTS_OF, E]], base=0, channel_multiplier=0).then_inc(consts, 1)
            pool.wait_ge(consts, 4)
            nc.gpsimd.affine_select(out=upto[:], in_=upto[:], compare_op=ALU.is_ge, fill=0.0, base=0,
                                    pattern=[[1, E], [-1, E]], channel_multiplier=0).then_inc(consts, 1)
            nc.gpsimd.tensor_copy(full[:], full_i[:]).then_inc(consts, 1)
            nc.gpsimd.tensor_copy(block_no[:], block_i[:]).then_inc(consts, 1)
            nc.gpsimd.tensor_copy(first[:], first_i[:]).then_inc(consts, 1)
            nc.gpsimd.memset(at[:], 0.0).then_inc(consts, 1)
            routing.store_entries(nc, pool, tick_pool, B - 1, False)
            for s in x2n_out:
                pool.wait_ge(s, 16 * B)

            def gather(i, k):
                m = number_of(i, k)
                if isinstance(i, int) and k < RX and k % (RX // STAGED) == 0:
                    pool.wait_ge(w_done, (E - STAGED + 1 + k // (RX // STAGED)) * DC)
                if isinstance(i, int) and k < AHEAD:
                    pool.wait_ge(tab_in[k], 16)
                    nc.gpsimd.tensor_copy(gather_no[:, k, :], tab[:, k, 0:1]).then_inc(gather_first_done, 1)
                    pool.wait_ge(gather_first_done, k + 1)
                else:
                    pool.wait_ge(gather_no_done, m + 1 - AHEAD)
                pool.sem_inc(tick_pool, 1)
                pool.indirect_dma_start(rows(k, slice(0, 2 * D)), None, x2n,
                                        bass.IndirectOffsetOnAxis(ap=gather_no[:, k % RX, :], axis=0),
                                        bounds_check=N - 1, oob_is_err=False).then_inc(rows_in[k % RX], 16)

            def scatter(i, k):
                m = number_of(i, k)
                pool.wait_ge(fin_done, m + 1)
                pool.wait_ge(scatter_no_done, m + 1)
                pool.sem_inc(tick_pool, 1)
                pool.indirect_dma_start(out, bass.IndirectOffsetOnAxis(ap=scatter_no[:, k % RX, :], axis=0),
                                        y_sb[:, k % YB, :], None, bounds_check=N - 1, oob_is_err=False)\
                    .then_inc(out_done[k % RX], 16)

            def step(i, k):
                gather(i, k)
                if k >= BEHIND:
                    scatter(i, k - BEHIND)

            blocks_loop(pool, step)
            for m in range(BLOCKS - BEHIND, BLOCKS):
                scatter(0, m)
            for k in range(BLOCKS - RX, BLOCKS):
                pool.wait_ge(out_done[k % RX], 16 * (turn(0, k) + 1))

        @block.scalar
        def _(act):
            routing.exponentials(nc, act, B - 1)
            for e in range(E):
                for c in range(DC):
                    i = e * DC + c
                    act.wait_ge(w_done, i + 1)
                    nc.scalar.copy(wt_hi[:, c, e * D:(e + 1) * D], ring[i % RING][:, :]).then_inc(w_hi_done, 1)

            def gather_numbers(i, k):
                act.wait_ge(tab_in[k % RX], (turn(i, k) + 1) * 16)
                act.sem_inc(tick_act, 1)
                nc.scalar.copy(gather_no[:, k % RX, :], column(tab, i, k, 0)).then_inc(gather_no_done, 1)

            def scatter_numbers(i, k):
                nc.scalar.copy(scatter_no[:, k % RX, :], column(tab, i, k, 0)).then_inc(scatter_no_done, 1)


            def step(i, k):
                m = number_of(i, k)
                act.wait_ge(t_done, m + 1)
                nc.scalar.copy(xt_hi[:, k % 2, :], t_ps[k % 2][:, :]).then_inc(xt_hi_done, 1)
                gather_numbers(i, k + AHEAD)
                if k >= 1:
                    scatter_numbers(i, k - 1)

            blocks_loop(act, step)
            scatter_numbers(0, BLOCKS - 1)

        @block.tensor
        def _(pe):
            def w_job(i):
                e, c = divmod(i, DC)
                if c == 0:
                    pe.wait_ge(w_in[e % STAGED], 16 * (e // STAGED + 1))
                if i >= RING:
                    pe.wait_ge(w_split, i - RING + 1)
                for o in range(DC):
                    m = nc.tensor.transpose(ring[i % RING][:, o * P:(o + 1) * P],
                                            stage[e % STAGED][:, o, c * P:(c + 1) * P], ident[:])
                m.then_inc(w_done, 1)

            for i in range(DC):
                w_job(i)
            routing.count(nc, pe, B - 1)
            for i in range(DC, W_JOBS):
                w_job(i)
            pe.wait_ge(owner_done, 1)
            pe.wait_ge(w_split, W_JOBS)

            def transposes(i, k):
                m = number_of(i, k)
                pe.wait_ge(rows_in[k % RX], (turn(i, k) + 1) * 16)
                if k >= 2:
                    pe.wait_ge(xt_done, m - 1)
                for c in range(DC):
                    t = nc.tensor.transpose(t_ps[k % 2][:, c * P:(c + 1) * P],
                                            rows(k, slice(D + c * P, D + (c + 1) * P)), ident[:])
                t.then_inc(t_done, 1)

            def product(i, k):
                m = number_of(i, k)
                e = pe.value_load(owner_i[0:1, bass.ds(m, 1)] if not isinstance(m, int) else owner_i[0:1, m:m + 1],
                                  min_val=0, max_val=E - 1)
                pe.wait_ge(xt_done, m + 1)
                if k >= 2:
                    pe.wait_ge(bias_done, m - 1)
                y = three_pass(nc.tensor.matmul, y_ps[k % 2][:, :],
                               ([xt_hi[:, k % 2, c * P:(c + 1) * P] for c in range(DC)],
                                [xt_lo[:, k % 2, c * P:(c + 1) * P] for c in range(DC)]),
                               ([wt_hi[:, c, bass.ds(e * D, D)] for c in range(DC)],
                                [wt_lo[:, c, bass.ds(e * D, D)] for c in range(DC)]))
                y.then_inc(y_done, 1)

            def step(i, k):
                transposes(i, k)
                if k >= 1:
                    product(i, k - 1)

            blocks_loop(pe, step)
            product(0, BLOCKS - 1)

        @block.vector
        def _(dve):
            steps = [0]

            def then(instruction):
                steps[0] += 1
                instruction.then_inc(route, 1)
                dve.wait_ge(route, steps[0])

            def w_lo_part(i):
                e, c = divmod(i, DC)
                dve.wait_ge(w_hi_done, i + 1)
                nc.vector.tensor_tensor(wt_lo[:, c, e * D:(e + 1) * D], ring[i % RING][:, :],
                                        wt_hi[:, c, e * D:(e + 1) * D].bitcast(F32), ALU.subtract).then_inc(w_split, 1)

            routing.choose(nc, dve, B - 1)
            for i in range(EARLY):
                w_lo_part(i)
            routing.place_tokens(nc, dve, B - 1)
            dve.wait_ge(consts, CONSTS)
            then(nc.vector.tensor_tensor(number[:], routing.next[:], first[:], ALU.subtract))
            then(nc.vector.tensor_tensor(over[:], free_ap(number[:], 0, [[1, E], [0, NT]]),
                                         free_ap(full[:], 0, [[0, E], [1, NT]]), ALU.is_gt))
            then(nc.vector.tensor_reduce(blocks[:], over[:], AX.X, ALU.add))
            nc.vector.tensor_scalar(skip[:], blocks[:], -float(P), float(Routing.SLOTS_OF), ALU.mult, ALU.add)\
                .then_inc(route, 1)
            steps[0] += 1
            then(nc.vector.tensor_tensor(cum[:], upto[:], free_ap(blocks[:], 0, [[0, E], [1, E]]), ALU.mult))
            then(nc.vector.tensor_reduce(end[:], cum[:], AX.X, ALU.add))
            then(nc.vector.tensor_tensor(past[:], free_ap(end[:], 0, [[0, BLOCKS + AHEAD], [1, E]]),
                                         free_ap(block_no[:], 0, [[1, BLOCKS + AHEAD], [0, E]]), ALU.is_le))
            then(nc.vector.tensor_tensor(at[:, :, 0:E - 1], past[:, :, 0:E - 1],
                                         free_ap(skip[:], 0, [[0, BLOCKS + AHEAD], [1, E - 1]]), ALU.mult))
            then(nc.vector.tensor_reduce(at_sum[:], at[:], AX.X, ALU.add))
            nc.vector.scalar_tensor_tensor(at_i[:], block_no[:], float(P), at_sum[:], ALU.mult, ALU.add).then_inc(at_done, 1)
            then(nc.vector.tensor_reduce(owner[:], past[:], AX.X, ALU.add))
            nc.vector.tensor_scalar(owner_i[:], owner[:], float(E - 1), None, ALU.min).then_inc(owner_done, 1)

            for i in range(EARLY, W_JOBS):
                w_lo_part(i)
            dve.wait_ge(bias_in, 16)

            def finish(i, k):
                m = number_of(i, k)
                e = dve.value_load(owner_i[0:1, bass.ds(m, 1)] if not isinstance(m, int) else owner_i[0:1, m:m + 1],
                                   min_val=0, max_val=E - 1)
                if k >= YB:
                    dve.wait_ge(out_done[(k - YB) % RX], (turn(i, k - YB) + 1) * 16)
                dve.wait_ge(y_done, m + 1)
                nc.vector.tensor_tensor(y_sb[:, k % YB, :], y_ps[k % 2][:, :], bias_sb[:, bass.ds(e * D, D)], ALU.add)\
                    .then_inc(bias_done, 1)
                dve.wait_ge(bias_done, m + 1)
                gate = column(tab, i, k, 1).bitcast(F32)
                nc.vector.scalar_tensor_tensor(y_sb[:, k % YB, :], y_sb[:, k % YB, :], gate, rows(k, slice(0, D)),
                                               ALU.mult, ALU.add).then_inc(fin_done, 1)

            def step(i, k):
                m = number_of(i, k)
                dve.wait_ge(xt_hi_done, m + 1)
                nc.vector.tensor_tensor(xt_lo[:, k % 2, :], t_ps[k % 2][:, :], xt_hi[:, k % 2, :].bitcast(F32),
                                        ALU.subtract).then_inc(xt_done, 1)
                if k >= 1:
                    finish(i, k - 1)

            blocks_loop(dve, step)
            finish(0, BLOCKS - 1)


def program(nc, x, ctx, w_qkv, w_out, wq, wk, wv, wo, wg, w, bias, out):
    with ExitStack() as cx:
        ident = cx.enter_context(nc.sbuf_tensor("ident", [P, P], F32))
        x1 = nc.dram_tensor("x1", [B * S, D], F32).ap()
        x2n = nc.dram_tensor("x2n", [B * S, 2 * D], F32).ap()
        stage_tensor = lambda i: cx.enter_context(nc.sbuf_tensor(f"stage{i}", [P, DC, D], F32))
        stage = [stage_tensor(0), stage_tensor(1)]
        sem = lambda n: cx.enter_context(nc.semaphore(n))
        x1_out, x1_last_out, x2n_out = sem("x1_out"), sem("x1_last_out"), (sem("x2_out"), sem("xn3_out"))
        rows_tensor = lambda n: cx.enter_context(nc.sbuf_tensor(n, [P, TB, D], F32))
        xin, xr = rows_tensor("xin"), rows_tensor("xr")
        x1_first_in = sem("x1_first_in")
        stage_in = [cx.enter_context(nc.semaphore(f"stage_in{i}")) for i in range(STAGED)]
        expert_in = [cx.enter_context(nc.semaphore(f"expert_in{i}")) for i in range(STAGED)]
        self_attention(nc, ident, x, w_qkv, w_out, x1, xin, xr, x1_out, x1_last_out, x1_first_in,
                       stage, stage_in, (wq, wk))
        stage += [stage_tensor(2)]
        routing = Routing(nc, cx)
        bias_sb, bias_in = cx.enter_context(nc.sbuf_tensor("bias_sb", [P, E * D], F32)), sem("bias_in")
        x2_sb, xn3_sb = rows_tensor("x2_sb"), rows_tensor("xn3_sb")
        cross_attention(nc, ident, routing, x1, x1_out, x1_last_out, x1_first_in, ctx, wv, wo, wg,
                        x2n, x2n_out, xin, xr, x2_sb, xn3_sb, bias, bias_sb, bias_in, stage, stage_in, w, expert_in)
        mixture_of_experts(nc, ident, routing, x2n, x2n_out, w, bias_sb, bias_in, out, stage, expert_in)


def kernel(x, ctx_2048, mask_BxSx4224_bf0, L0_attn_w_qkv, L0_attn_w_out, L0_xattn_wq, L0_xattn_wk, L0_xattn_wv,
           L0_xattn_wo, L0_ffn_wg, L0_ffn_W, L0_ffn_b):
    import concourse.bacc as bacc
    import numpy as np
    from concourse.bass_utils import run_bass_kernel_spmd

    rows = lambda t: np.ascontiguousarray(np.asarray(t).reshape(B * S, D))
    arrays = {"x": rows(x), "ctx": rows(ctx_2048), "w_qkv": L0_attn_w_qkv, "w_out": L0_attn_w_out, "wq": L0_xattn_wq,
              "wk": L0_xattn_wk, "wv": L0_xattn_wv, "wo": L0_xattn_wo, "wg": L0_ffn_wg, "w": L0_ffn_W,
              "bias": L0_ffn_b}
    arrays = {f"in_{n}": np.ascontiguousarray(a) for n, a in arrays.items()}
    nc = bacc.Bacc("TRN2", target_bir_lowering=False, num_devices=1)
    args = [nc.dram_tensor(n, a.shape, mybir.dt.from_np(a.dtype), kind="ExternalInput").ap()
            for n, a in arrays.items()]
    out = nc.dram_tensor("result", [B * S, D], F32, kind="ExternalOutput").ap()
    program(nc, *args, out)
    r = run_bass_kernel_spmd(nc, [arrays], core_ids=[0])
    return r.results[0]["result"].reshape(B, S, D)
```
